# Optimizing a Trainium2 kernel written in Bass

```python
import numpy as np
import jax
import jax.numpy as jnp

def _softmax(x, axis=-1):
    return jax.nn.softmax(x, axis=axis)

def _gelu(x):
    return jax.nn.gelu(x, approximate=True)

def _silu(x):
    return jax.nn.silu(x)

def _sigmoid(x):
    return jax.nn.sigmoid(x)

def _layernorm(x, axis=-1, eps=1e-05):
    m = jnp.mean(x, axis=axis, keepdims=True)
    v = jnp.var(x, axis=axis, keepdims=True)
    return (x - m) / jnp.sqrt(v + eps)

def _scatter_add(tgt, idx, src, axis=0):
    return tgt.at[idx].add(src)

def _segment_sum(src, seg, n):
    return jax.ops.segment_sum(src, seg, n)
kernel_name = 'mk_metaformer_d1_conv_nhwc768_r2_ca2980'

def setup_inputs(seed: int=0):
    np.random.seed(seed)
    _w = jnp.asarray

    def _rec_inputs():
        import jax
        import jax.numpy as jnp
        _gk = jax.random.key(seed)
        x = -0.0008768 + 1.001 * jax.random.normal(jax.random.fold_in(_gk, 1), (1, 48, 48, 384), jnp.float32)
        return x
    x = _rec_inputs()

    def _L0_conv_setup():
        import jax, jax.numpy as jnp
        import numpy as np
        NUM_HEADS = 12

        def _rel_gather(rel_pos, size):
            coords = jnp.arange(size)[:, None] - jnp.arange(size)[None, :] + (size - 1)
            return rel_pos[coords]
        key = jax.random.key(seed)
        ks = jax.random.split(key, 7)
        B, H, W, C = (1, 48, 48, 384)
        hd = C // NUM_HEADS
        s = 0.02
        return {'x': jax.random.normal(ks[0], (B, H, W, C), jnp.float32), 'qkv_w': jax.random.normal(ks[1], (C, 3 * C), jnp.float32) * s, 'qkv_b': jax.random.normal(ks[2], (3 * C,), jnp.float32) * s, 'proj_w': jax.random.normal(ks[3], (C, C), jnp.float32) * s, 'proj_b': jax.random.normal(ks[4], (C,), jnp.float32) * s, 'rel_pos_h': jax.random.normal(ks[5], (2 * H - 1, hd), jnp.float32) * s, 'rel_pos_w': jax.random.normal(ks[6], (2 * W - 1, hd), jnp.float32) * s}
    _L0_conv_all = _L0_conv_setup()
    _L0_conv_in = {k: v for k, v in _L0_conv_all.items() if k in ('qkv_w', 'qkv_b', 'proj_w', 'proj_b', 'rel_pos_h', 'rel_pos_w')}
    del _L0_conv_all

    def _L0_ffn_setup():
        import jax, jax.numpy as jnp
        import numpy as np
        B, T, D = (4, 1024, 384)
        E, F, K = (8, 4 * 384, 2)
        key = jax.random.key(seed)
        ks = jax.random.split(key, 5)
        s = 0.02
        return {'x': jax.random.normal(ks[0], (B, T, D), dtype=jnp.float32), 'Wg': jax.random.normal(ks[1], (D, E), dtype=jnp.float32) * s, 'bg': jnp.zeros((E,), dtype=jnp.float32), 'W1': jax.random.normal(ks[2], (E, D, F), dtype=jnp.float32) * s, 'b1': jnp.zeros((E, F), dtype=jnp.float32), 'W2': jax.random.normal(ks[3], (E, F, D), dtype=jnp.float32) * s, 'b2': jnp.zeros((E, D), dtype=jnp.float32)}
    _L0_ffn_all = _L0_ffn_setup()
    _L0_ffn_in = {k: v for k, v in _L0_ffn_all.items() if k in ('Wg', 'bg', 'W1', 'b1', 'W2', 'b2')}
    del _L0_ffn_all
    return {'x': x, 'L0_conv_qkv_w': _L0_conv_in['qkv_w'], 'L0_conv_qkv_b': _L0_conv_in['qkv_b'], 'L0_conv_proj_w': _L0_conv_in['proj_w'], 'L0_conv_proj_b': _L0_conv_in['proj_b'], 'L0_conv_rel_pos_h': _L0_conv_in['rel_pos_h'], 'L0_conv_rel_pos_w': _L0_conv_in['rel_pos_w'], 'L0_ffn_Wg': _L0_ffn_in['Wg'], 'L0_ffn_bg': _L0_ffn_in['bg'], 'L0_ffn_W1': _L0_ffn_in['W1'], 'L0_ffn_b1': _L0_ffn_in['b1'], 'L0_ffn_W2': _L0_ffn_in['W2'], 'L0_ffn_b2': _L0_ffn_in['b2']}

def reference(x, L0_conv_qkv_w, L0_conv_qkv_b, L0_conv_proj_w, L0_conv_proj_b, L0_conv_rel_pos_h, L0_conv_rel_pos_w, L0_ffn_Wg, L0_ffn_bg, L0_ffn_W1, L0_ffn_b1, L0_ffn_W2, L0_ffn_b2):
    import jax
    import jax.numpy as jnp

    def _L0_conv_ref(x, qkv_w, qkv_b, proj_w, proj_b, rel_pos_h, rel_pos_w):
        import jax, jax.numpy as jnp
        import numpy as np
        NUM_HEADS = 12

        def _rel_gather(rel_pos, size):
            coords = jnp.arange(size)[:, None] - jnp.arange(size)[None, :] + (size - 1)
            return rel_pos[coords]
        B, H, W, C = x.shape
        nh = NUM_HEADS
        hd = C // nh
        scale = hd ** (-0.5)
        S = H * W
        qkv = x @ qkv_w + qkv_b
        qkv = qkv.reshape(B, S, 3, nh, hd).transpose(2, 0, 3, 1, 4)
        qkv = qkv.reshape(3, B * nh, S, hd)
        q, k, v = (qkv[0], qkv[1], qkv[2])
        attn = jnp.einsum('bqd,bkd->bqk', q * scale, k)
        Rh = _rel_gather(rel_pos_h, H)
        Rw = _rel_gather(rel_pos_w, W)
        qr = q.reshape(B * nh, H, W, hd)
        rel_h = jnp.einsum('bhwc,hkc->bhwk', qr, Rh)
        rel_w = jnp.einsum('bhwc,wkc->bhwk', qr, Rw)
        bias = (rel_h[..., :, None] + rel_w[..., None, :]).reshape(B * nh, S, S)
        attn = jax.nn.softmax(attn + bias, axis=-1)
        out = jnp.einsum('bqk,bkd->bqd', attn, v)
        out = out.reshape(B, nh, H, W, hd).transpose(0, 2, 3, 1, 4).reshape(B, H, W, C)
        return out @ proj_w + proj_b

    def _L0_ffn_ref(x, Wg, bg, W1, b1, W2, b2):
        import jax, jax.numpy as jnp
        import numpy as np
        B, T, D = (4, 1024, 384)
        E, F, K = (8, 4 * 384, 2)
        b, t, d = x.shape
        x_flat = x.reshape(-1, d)
        n = x_flat.shape[0]
        gates = jax.nn.softmax(x_flat @ Wg + bg, axis=-1)
        topk_g, topk_i = jax.lax.top_k(gates, K)
        combine = jnp.zeros((n, W1.shape[0]), dtype=gates.dtype)
        combine = combine.at[jnp.arange(n)[:, None], topk_i].add(topk_g)
        h = jnp.einsum('nd,edf->enf', x_flat, W1) + b1[:, None, :]
        h = jax.nn.gelu(h, approximate=False)
        y = jnp.einsum('enf,efd->end', h, W2) + b2[:, None, :]
        out = jnp.einsum('ne,end->nd', combine, y)
        return out.reshape(b, t, d)

    def _gn(v, G=32, eps=1e-05):
        B_, H_, W_, C_ = v.shape
        g = v.reshape(B_, H_, W_, G, C_ // G)
        m = jnp.mean(g, axis=(1, 2, 4), keepdims=True)
        s = jnp.var(g, axis=(1, 2, 4), keepdims=True)
        return ((g - m) / jnp.sqrt(s + eps)).reshape(v.shape)

    def _ln_c(v, eps=1e-06):
        m = jnp.mean(v, axis=-1, keepdims=True)
        s = jnp.var(v, axis=-1, keepdims=True)
        return (v - m) / jnp.sqrt(s + eps)

    def _ln_t(v, eps=1e-05):
        m = jnp.mean(v, axis=-1, keepdims=True)
        s = jnp.var(v, axis=-1, keepdims=True)
        return (v - m) / jnp.sqrt(s + eps)

    def _to_tokens(v):
        B_, H_, W_, C_ = v.shape
        return v.reshape(B_, H_ * W_, C_)

    def _from_tokens(t, like):
        return t.reshape(like.shape)
    x = x + _L0_conv_ref(_ln_c(x), L0_conv_qkv_w, L0_conv_qkv_b, L0_conv_proj_w, L0_conv_proj_b, L0_conv_rel_pos_h, L0_conv_rel_pos_w)
    t = _to_tokens(x)
    t = t + _L0_ffn_ref(_ln_t(t), L0_ffn_Wg, L0_ffn_bg, L0_ffn_W1, L0_ffn_b1, L0_ffn_W2, L0_ffn_b2)
    x = _from_tokens(t, x)
    return x

_drawn_inputs = setup_inputs


def setup_inputs(seed=0):
    import zlib

    import numpy as np

    out = dict(_drawn_inputs(seed))
    spreads = {'L0_ffn_bg': (0.0, 2.0), 'L0_ffn_b1': (0.0, 2.0), 'L0_ffn_b2': (0.0, 1.835)}
    factors = {'L0_conv_qkv_w': 8.0,
     'L0_conv_qkv_b': 6.826,
     'L0_conv_proj_w': 6.761,
     'L0_conv_proj_b': 19.401,
     'L0_conv_rel_pos_h': 8.0,
     'L0_conv_rel_pos_w': 8.0,
     'L0_ffn_Wg': 3.56,
     'L0_ffn_W1': 6.917,
     'L0_ffn_W2': 3.501}
    for name, (base, spread) in spreads.items():
        noise = np.random.default_rng([zlib.crc32(name.encode()), seed]).standard_normal(out[name].shape)
        drawn = base * np.exp(spread * noise) if base else spread * noise
        out[name] = jnp.asarray(drawn.astype(out[name].dtype))
    for name, factor in factors.items():
        out[name] = (out[name] * factor).astype(out[name].dtype)
    return out
```

```python
from contextlib import ExitStack

import concourse.bass as bass
from concourse import mybir

F32 = mybir.dt.float32
F32R = mybir.dt.float32r
ACT = mybir.ActivationFunctionType
ALU = mybir.AluOpType
AX = mybir.AxisListType

P = 128
SIDE = 48
S = SIDE * SIDE
C = 384
KC = C // P
HEADS = 12
HD = C // HEADS
TILES = S // P
TB = 384
BLOCKS = S // TB
TPB = TB // P
QK_TILES = 2 * KC
HPT = P // HD
REL = 2 * SIDE - 1
VW = 2 * HD + 1
SCALE = float(HD) ** -0.5
LN1_EPS = 1e-6
LN2_EPS = 1e-5


def phase_qkv(nc, x, qkv_w, qkv_b, qkv_b_t, qk_hi_d, qk_lo_d, v_d):
    GT = 6
    with ExitStack() as ctx:
        def sb(name, shape, dt=F32):
            return ctx.enter_context(nc.sbuf_tensor(name, shape, dt))

        def sem(name):
            return ctx.enter_context(nc.semaphore(name))

        x_sb = sb("x_sb", [P, TILES, C])
        xn = [sb(f"xn{i}", [P, TPB, C]) for i in range(2)]
        stats = sb("stats", [P, TILES, 6])
        mv = sb("mv", [P, TILES, 2])
        veps = sb("veps", [P, TILES])
        root = sb("root", [P, TILES])
        rstd = sb("rstd", [P, TILES])
        nt = sb("nt", [P, TILES])
        w_raw = sb("w_raw", [P, KC, 3 * C])
        w_hi = sb("w_hi", [P, KC, 3 * C], F32R)
        w_lo = sb("w_lo", [P, KC, 3 * C], F32R)
        b_qk = sb("b_qk", [P, QK_TILES])
        b_v = sb("b_v", [P, C])
        ident = sb("ident", [P, P])
        xt_hi = [sb(f"xt_hi{i}", [P, KC, TB], F32R) for i in range(2)]
        xt_lo = [sb(f"xt_lo{i}", [P, KC, TB], F32R) for i in range(2)]
        qk_hi = [sb(f"qk_hi{i}", [P, QK_TILES, TB], F32R) for i in range(2)]
        qk_lo = [sb(f"qk_lo{i}", [P, QK_TILES, TB], F32R) for i in range(2)]
        v_f = sb("v_f", [P, 3, C])
        v_sb = sb("v_sb", [P, HEADS, TILES, VW], F32R)
        ps_t = ctx.enter_context(nc.psum_tensor("ps_t", [P, KC, 512], F32))
        ps_y = ctx.enter_context(nc.psum_tensor("ps_y", [P, 3, 512], F32))

        x_in = [sem(f"x_in{g}") for g in range(TILES // GT)]
        w_in = sem("w_in")
        b_in = sem("b_in")
        ident_ok = sem("ident_ok")
        w_scaled = sem("w_scaled")
        w_hi_ok = sem("w_hi_ok")
        w_lo_ok = sem("w_lo_ok")
        ln_step = sem("ln_step")
        root_ok = sem("root_ok")
        ln_own = sem("ln_own")
        xn_ok = sem("xn_ok")
        turned = sem("turned")
        xt_hi_ok = sem("xt_hi_ok")
        xt_lo_ok = sem("xt_lo_ok")
        y_ok = sem("y_ok")
        hi_ok = sem("hi_ok")
        lo_ok = sem("lo_ok")
        vf_ok = sem("vf_ok")
        st_out = [sem(f"st_out{i}") for i in range(2)]
        v_out = sem("v_out")
        block = ctx.enter_context(nc.Block())

        x_v = x.rearrange("(t p) c -> p t c", p=P)
        qk_hi_v = qk_hi_d.rearrange("(m p) n -> p m n", p=P)
        qk_lo_v = qk_lo_d.rearrange("(m p) n -> p m n", p=P)
        OPB = QK_TILES + TPB

        @block.sync
        def _(sp):
            for g in range(TILES // GT):
                sp.dma_start(x_sb[:, g * GT:(g + 1) * GT, :], x_v[:, g * GT:(g + 1) * GT, :]).then_inc(x_in[g], 16)
                if g == 0:
                    sp.dma_start(w_raw[:], qkv_w.rearrange("(k p) n -> p k n", p=P)).then_inc(w_in, 16)
            sp.dma_start(b_qk[:], qkv_b_t[:, 0:QK_TILES]).then_inc(b_in, 16)
            sp.dma_start(b_v[:], qkv_b[2 * C:3 * C].rearrange("(a n) -> a n", a=1).broadcast_to([P, C])).then_inc(b_in, 16)
            with sp.Fori(0, BLOCKS // 2) as i:
                for par in range(2):
                    blk = 2 * i + par
                    sp.wait_ge(hi_ok, OPB * blk + QK_TILES)
                    sp.wait_ge(lo_ok, OPB * blk + QK_TILES)
                    cols = bass.ds(blk * TB, TB)
                    sp.dma_start(qk_hi_v[:, :, cols], qk_hi[par][:].bitcast(F32)).then_inc(st_out[par], 16)
                    sp.dma_start(qk_lo_v[:, :, cols], qk_lo[par][:].bitcast(F32)).then_inc(st_out[par], 16)
            sp.wait_ge(ident_ok, 3)
            sp.wait_ge(hi_ok, OPB * BLOCKS)
            sp.wait_ge(lo_ok, OPB * BLOCKS)
            for h in range(HEADS):
                sp.dma_start(v_d[h], v_sb[:, h, :, :].bitcast(F32).rearrange("p t w -> p (t w)")).then_inc(v_out, 16)
            for par in range(2):
                sp.wait_ge(st_out[par], 32 + 16 * BLOCKS)
            sp.wait_ge(v_out, 16 * HEADS)

        @block.gpsimd
        def _(pool):
            for par in range(2):
                pool.sem_inc(st_out[par], 32)
            pool.memset(ident[:], 0.0).then_inc(ident_ok, 1)
            pool.wait_ge(ident_ok, 1)
            pool.affine_select(out=ident[:], in_=ident[:], compare_op=ALU.not_equal, fill=1.0, base=0,
                               pattern=[[-1, P]], channel_multiplier=1).then_inc(ident_ok, 1)
            pool.memset(v_sb[:, :, :, 2 * HD:VW].bitcast(F32), 1.0).then_inc(ident_ok, 1)

        @block.scalar
        def _(act):
            act.wait_ge(w_scaled, 2)
            act.copy(w_hi[:], w_raw[:]).then_inc(w_hi_ok, 1)
            for g in range(TILES // GT):
                act.wait_ge(ln_step, g + 1)
                act.activation(root[:, g * GT:(g + 1) * GT], veps[:, g * GT:(g + 1) * GT], ACT.Sqrt).then_inc(root_ok, 1)
            with act.Fori(0, BLOCKS // 2) as i:
                for par in range(2):
                    blk = 2 * i + par
                    act.wait_ge(turned, blk + 1)
                    act.copy(xt_hi[par][:], ps_t[:, :, 0:TB]).then_inc(xt_hi_ok, 1)
                    act.wait_ge(st_out[par], 32 * i + 32)
                    for m in range(QK_TILES):
                        act.wait_ge(y_ok, OPB * blk + m + 1)
                        act.activation(qk_hi[par][:, m, :], ps_y[:, m % 3, 0:TB], ACT.Identity,
                                       bias=b_qk[:, m:m + 1]).then_inc(hi_ok, 1)
                    for t in range(TPB):
                        act.wait_ge(vf_ok, TPB * blk + TPB + t + 1)
                        act.copy(v_sb[:, :, bass.ds(TPB * blk + t, 1), 0:HD],
                                 v_f[:, t, :].rearrange("p (h a d) -> p h a d", a=1, d=HD)).then_inc(hi_ok, 1)

        @block.vector
        def _(dve):
            dve.sem_inc(vf_ok, TPB)
            dve.wait_ge(w_in, 16)
            dve.wait_ge(b_in, 32)
            dve.tensor_scalar(b_qk[:, KC:QK_TILES], b_qk[:, KC:QK_TILES], SCALE, None, ALU.mult).then_inc(w_scaled, 1)
            dve.tensor_scalar(w_raw[:, :, C:2 * C], w_raw[:, :, C:2 * C], SCALE, None, ALU.mult).then_inc(w_scaled, 1)
            own = [0]

            def step(ins):
                own[0] += 1
                ins.then_inc(ln_own, 1)
                dve.wait_ge(ln_own, own[0])

            for g in range(TILES // GT):
                cut = slice(g * GT, (g + 1) * GT)
                dve.wait_ge(x_in[g], 16)
                for t in range(g * GT, (g + 1) * GT):
                    last = dve.bn_stats(stats[:, t, :], x_sb[:, t, :])
                step(last)
                for t in range(g * GT, (g + 1) * GT):
                    last = dve.bn_aggr(mv[:, t, :], stats[:, t, :])
                step(last)
                dve.tensor_scalar(veps[:, cut], mv[:, cut, 1], LN1_EPS, None, ALU.add).then_inc(ln_step, 1)
                dve.wait_ge(root_ok, g + 1)
                step(dve.reciprocal(rstd[:, cut], root[:, cut]))
                step(dve.tensor_tensor(nt[:, cut], rstd[:, cut], rstd[:, cut], ALU.mult))
                step(dve.tensor_tensor(nt[:, cut], nt[:, cut], veps[:, cut], ALU.mult))
                step(dve.tensor_scalar(nt[:, cut], nt[:, cut], -0.5, 1.5, ALU.mult, ALU.add))
                step(dve.tensor_tensor(rstd[:, cut], rstd[:, cut], nt[:, cut], ALU.mult))
                if g == 0:
                    dve.wait_ge(w_hi_ok, 1)
                    dve.tensor_tensor(w_lo[:], w_raw[:], w_hi[:].bitcast(F32), ALU.subtract).then_inc(w_lo_ok, 1)
            with dve.Fori(0, BLOCKS // 2) as i:
                for par in range(2):
                    blk = 2 * i + par
                    for t in range(TPB):
                        tile = bass.ds(TPB * blk + t, 1)
                        last = dve.tensor_scalar(xn[par][:, t, :], x_sb[:, tile, :].rearrange("p a c -> p (a c)"),
                                                 mv[:, tile, 0:1].rearrange("p a c -> p (a c)"), rstd[:, tile],
                                                 ALU.subtract, ALU.mult)
                    last.then_inc(xn_ok, 1)
                    dve.wait_ge(xt_hi_ok, blk + 1)
                    dve.tensor_tensor(xt_lo[par][:], ps_t[:, :, 0:TB], xt_hi[par][:].bitcast(F32),
                                      ALU.subtract).then_inc(xt_lo_ok, 1)
                    for m in range(QK_TILES):
                        dve.wait_ge(hi_ok, OPB * blk + m + 1)
                        dve.scalar_tensor_tensor(qk_lo[par][:, m, :], ps_y[:, m % 3, 0:TB], b_qk[:, m:m + 1],
                                                 qk_hi[par][:, m, :].bitcast(F32), ALU.add, ALU.subtract).then_inc(lo_ok, 1)
                    for t in range(TPB):
                        dve.wait_ge(y_ok, OPB * blk + QK_TILES + t + 1)
                        dve.tensor_tensor(v_f[:, t, :], ps_y[:, t, 0:TB], b_v[:], ALU.add).then_inc(vf_ok, 1)
                    for t in range(TPB):
                        dve.wait_ge(hi_ok, OPB * blk + QK_TILES + t + 1)
                        tile = bass.ds(TPB * blk + t, 1)
                        dve.tensor_tensor(v_sb[:, :, tile, HD:2 * HD],
                                          v_f[:, t, :].rearrange("p (h a d) -> p h a d", a=1, d=HD),
                                          v_sb[:, :, tile, 0:HD].bitcast(F32), ALU.subtract).then_inc(lo_ok, 1)

        @block.tensor
        def _(pe):
            pe.wait_ge(ident_ok, 2)
            pe.wait_ge(w_lo_ok, 1)
            with pe.Fori(0, BLOCKS // 2) as i:
                for par in range(2):
                    blk = 2 * i + par
                    pe.wait_ge(xn_ok, blk + 1)
                    for k in range(KC):
                        for t in range(TPB):
                            last = pe.transpose(ps_t[:, k, t * P:(t + 1) * P],
                                                xn[par][:, t, k * P:(k + 1) * P], ident[:])
                    last.then_inc(turned, 1)
                    pe.wait_ge(xt_lo_ok, blk + 1)
                    hi, lo = xt_hi[par], xt_lo[par]
                    for m in range(QK_TILES):
                        if m < 3:
                            pe.wait_ge(vf_ok, TPB * blk + m + 1)
                        else:
                            pe.wait_ge(lo_ok, OPB * blk + m - 2)
                        cut = slice(m * P, (m + 1) * P)
                        for n, (w, v) in enumerate([(w_hi, hi), (w_hi, lo), (w_lo, hi)]):
                            for k in range(KC):
                                last = pe.matmul(ps_y[:, m % 3, 0:TB], w[:, k, cut], v[:, k, :],
                                                 start=(n + k == 0), stop=(n == 2 and k == KC - 1))
                        last.then_inc(y_ok, 1)
                    for t in range(TPB):
                        pe.wait_ge(lo_ok, OPB * blk + t + 4)
                        cut = slice(t * P, (t + 1) * P)
                        for n, (v, w) in enumerate([(hi, w_hi), (hi, w_lo), (lo, w_hi)]):
                            for k in range(KC):
                                last = pe.matmul(ps_y[:, t, 0:TB], v[:, k, cut], w[:, k, 2 * C:3 * C],
                                                 start=(n + k == 0), stop=(n == 2 and k == KC - 1))
                        last.then_inc(y_ok, 1)


def phase_rel(nc, rel_t, qk_hi_d, qk_lo_d, rel_hi_d, rel_lo_d):
    with ExitStack() as ctx:
        def sb(name, shape, dt=F32):
            return ctx.enter_context(nc.sbuf_tensor(name, shape, dt))

        def sem(name):
            return ctx.enter_context(nc.semaphore(name))

        K3 = 3 * HD
        NQ = HPT * SIDE
        CPB = 2
        BANKS = 8
        FILLS = 2 * SIDE // CPB
        GROUPS = HEADS // HPT
        tab_raw = sb("tab_raw", [K3, 2, REL])
        tab_hi = sb("tab_hi", [K3, 2, REL], F32R)
        tab = sb("tab", [K3, 2, REL], F32R)
        neg_lo = sb("neg_lo", [P, 1])
        q_sb = sb("q_sb", [K3, HPT, S], F32R)
        out_hi = [sb(f"out_hi{a}", [SIDE, HPT, S], F32R) for a in range(2)]
        out_lo = [sb(f"out_lo{a}", [SIDE, HPT, S], F32R) for a in range(2)]
        ps = ctx.enter_context(nc.psum_tensor("ps", [P, BANKS, 512], F32))

        tab_in = sem("tab_in")
        mask_ok = sem("mask_ok")
        tab_hi_ok = sem("tab_hi_ok")
        tab_ok = sem("tab_ok")
        q_in = sem("q_in")
        ps_ok = sem("ps_ok")
        r_hi = sem("r_hi")
        r_lo = sem("r_lo")
        r_out = [sem(f"r_out{a}") for a in range(2)]
        block = ctx.enter_context(nc.Block())

        @block.sync
        def _(sp):
            for r in range(3):
                sp.dma_start(tab_raw[r * HD:(r + 1) * HD, :, :], rel_t.rearrange("a d n -> d a n")).then_inc(tab_in, 16)
            with sp.Fori(0, GROUPS) as g:
                sp.wait_ge(ps_ok, FILLS * g + 1)
                for r, src in enumerate((qk_hi_d, qk_hi_d, qk_lo_d)):
                    sp.dma_start(q_sb[r * HD:(r + 1) * HD, :, :].bitcast(F32),
                                 src[bass.ds(g * P, P), :].rearrange("(h d) n -> d h n", d=HD)).then_inc(q_in, 16)
                for a in range(2):
                    half = FILLS // 2
                    sp.wait_ge(r_hi, FILLS * g + half * (a + 1))
                    sp.wait_ge(r_lo, BANKS + FILLS * g + half * (a + 1))
                    for o, d in ((out_hi, rel_hi_d), (out_lo, rel_lo_d)):
                        sp.dma_start(d[bass.ds(g * HPT, HPT), a * SIDE:(a + 1) * SIDE, :].rearrange("h r n -> r h n"),
                                     o[a][:].bitcast(F32)).then_inc(r_out[a], 16)
            for a in range(2):
                sp.wait_ge(r_out[a], 32 + 32 * GROUPS)

        @block.gpsimd
        def _(pool):
            for a in range(2):
                pool.sem_inc(r_out[a], 32)
            pool.sem_inc(ps_ok, 1)
            pool.memset(neg_lo[:], 0.0).then_inc(mask_ok, 1)
            pool.wait_ge(mask_ok, 1)
            pool.memset(neg_lo[HD:2 * HD, :], -1.0).then_inc(mask_ok, 1)

        @block.tensor
        def _(pe):
            pe.wait_ge(tab_ok, 1)
            with pe.Fori(0, GROUPS) as g:
                pe.wait_ge(q_in, 48 * g + 48)
                for f in range(FILLS):
                    a, bank = f // (FILLS // 2), f % BANKS
                    pe.wait_ge(r_lo, FILLS * g + f + 1)
                    for n in range(CPB):
                        c = (f * CPB + n) % SIDE
                        own = slice(c, S, SIDE) if a == 0 else slice(c * SIDE, (c + 1) * SIDE)
                        last = pe.matmul(ps[0:SIDE, bank, n * NQ:(n + 1) * NQ],
                                         tab[:, a, SIDE - 1 - c:REL - c], q_sb[:, :, own], start=True, stop=True)
                    last.then_inc(ps_ok, 1)

        def places(o, f):
            c = f * CPB % SIDE
            v = o[:].rearrange("r h (y x) -> r h y x", x=SIDE)
            if f < FILLS // 2:
                return v[:, :, :, c:c + CPB].rearrange("r h y c -> r c h y")
            return v[:, :, c:c + CPB, :].rearrange("r h c x -> r c h x")

        def results(bank):
            return ps[0:SIDE, bank, 0:CPB * NQ].rearrange("r (c h y) -> r c h y", c=CPB, h=HPT)

        @block.scalar
        def _(act):
            act.wait_ge(tab_in, 48)
            act.copy(tab_hi[:], tab_raw[:]).then_inc(tab_hi_ok, 1)
            with act.Fori(0, GROUPS) as g:
                for f in range(FILLS):
                    a = f // (FILLS // 2)
                    if f % (FILLS // 2) == 0:
                        act.wait_ge(r_out[a], 32 * g + 32)
                    act.wait_ge(ps_ok, FILLS * g + f + 2)
                    act.copy(places(out_hi[a], f), results(f % BANKS)).then_inc(r_hi, 1)

        @block.vector
        def _(dve):
            dve.sem_inc(r_lo, BANKS)
            dve.wait_ge(mask_ok, 2)
            dve.wait_ge(tab_hi_ok, 1)
            dve.scalar_tensor_tensor(tab[:], tab_hi[:].bitcast(F32), neg_lo[0:K3, :], tab_raw[:], ALU.mult, ALU.add).then_inc(tab_ok, 1)
            with dve.Fori(0, GROUPS) as g:
                for f in range(FILLS):
                    a = f // (FILLS // 2)
                    dve.wait_ge(r_hi, FILLS * g + f + 1)
                    dve.tensor_tensor(places(out_lo[a], f), results(f % BANKS), places(out_hi[a], f).bitcast(F32),
                                      ALU.subtract).then_inc(r_lo, 1)


QB = 2 * TB
QBLOCKS = S // QB
VARIANTS = TILES // 3
VROWS = SIDE // VARIANTS
TOP = 2 * HD + SIDE + VROWS + 1
UNITS = QBLOCKS * TILES
LEAD = 2
SHIFT = 4
RING = 4


def phase_attention(nc, qk_hi_d, qk_lo_d, rel_hi_d, rel_lo_d, v_d, m_d, ot_d):
    with ExitStack() as ctx:
        def sb(name, shape, dt=F32):
            return ctx.enter_context(nc.sbuf_tensor(name, shape, dt))

        def sem(name):
            return ctx.enter_context(nc.semaphore(name))

        query_hi = [sb(f"query_hi{i}", [P, S], F32R) for i in range(2)]
        key_hi = [sb(f"key_hi{i}", [P, S], F32R) for i in range(2)]
        query_rest = [sb(f"query_rest{i}", [TOP, VARIANTS, QB], F32R) for i in range(QBLOCKS)]
        key_rest = [sb(f"key_rest{i}", [TOP, S], F32R) for i in range(2)]
        val = [sb(f"val{i}", [P, TILES, VW], F32R) for i in range(2)]
        p_hi = [sb(f"p_hi{i}", [P, 2, TB], F32R) for i in range(RING)]
        p_lo = [sb(f"p_lo{i}", [P, 2, TB], F32R) for i in range(RING)]
        p_f = [sb(f"p_f{i}", [P, 2, TB]) for i in range(2)]
        hot_hi = sb("hot_hi", [P, S])
        hot_rest = sb("hot_rest", [P, S])
        ident = sb("ident2", [P, P])
        mx = [sb(f"mx{i}", [P, 6, 3]) for i in range(QBLOCKS)]
        neg_m = [sb(f"neg_m{i}", [P, 6]) for i in range(QBLOCKS)]
        neg_mt = [sb(f"neg_mt{i}", [6, P], F32R) for i in range(QBLOCKS)]
        o_t = [sb(f"o_t{i}", [VW, 2, TB]) for i in range(2)]
        ps_s = ctx.enter_context(nc.psum_tensor("ps_s", [P, 4, 512], F32))
        ps_m = ctx.enter_context(nc.psum_tensor("ps_m", [P, 2, 512], F32))
        ps_o = ctx.enter_context(nc.psum_tensor("ps_o", [P, 2, 512], F32))

        hot_ok = sem("hot_ok")
        hot_hi_ok = sem("hot_hi_ok")
        hot_rest_ok = sem("hot_rest_ok")
        hi_in = [sem(f"hi_in{i}") for i in range(2)]
        kv_in = [sem(f"kv_in{i}") for i in range(2)]
        rest_in = [sem(f"rest_in{i}") for i in range(QBLOCKS)]
        m_out = sem("m_out")
        s_ok = sem("s_ok")
        hi_ok = sem("p_hi_ok")
        f_ok = sem("f_ok")
        lo_ok = sem("p_lo_ok")
        pv_ok = sem("pv_ok")
        mm_ok = sem("mm_ok")
        mx_ok = sem("mx_ok")
        neg_ok = sem("neg_ok")
        turned = sem("turned2")
        negt_ok = sem("negt_ok")
        acc_a = sem("acc_a")
        acc_d = sem("acc_d")
        ot_out = [sem(f"ot_out{i}") for i in range(2)]
        block = ctx.enter_context(nc.Block())

        loop_heads = HEADS - 2

        def chunk_at(h, par, k):
            return (par, UNITS - SHIFT + k) if k < SHIFT else (1 - par, k - SHIFT)

        def unit_at(par, k):
            return (par, k + LEAD) if k + LEAD < UNITS else (1 - par, k + LEAD - UNITS)

        turn_at = {TILES + SHIFT + 2: 0, 2 * TILES + SHIFT + 2: 1, SHIFT + 2: 2}

        def turned_at(k, last):
            b = turn_at.get(k)
            return None if b is None or (last and b < 2) else b

        @block.sync
        def _(sp):
            def load_hi(h, par):
                rows = bass.ds(h * HD, HD)
                krows = bass.ds(C + h * HD, HD)
                sp.dma_start(key_hi[par][0:HD, :].bitcast(F32), qk_hi_d[krows, :]).then_inc(hi_in[par], 16)
                sp.dma_start(query_hi[par][0:HD, :].bitcast(F32), qk_hi_d[rows, :]).then_inc(hi_in[par], 16)
                sp.dma_start(query_hi[par][HD:P, :].bitcast(F32), rel_hi_d[bass.ds(h, 1), :, :].rearrange("a r n -> (a r) n")).then_inc(hi_in[par], 16)

            def load_kv(h, par):
                krows = bass.ds(C + h * HD, HD)
                sp.dma_start(key_rest[par][0:HD, :].bitcast(F32), qk_hi_d[krows, :]).then_inc(kv_in[par], 16)
                sp.dma_start(key_rest[par][HD:2 * HD, :].bitcast(F32), qk_lo_d[krows, :]).then_inc(kv_in[par], 16)
                sp.dma_start(val[par][:].bitcast(F32).rearrange("p t w -> p (t w)"), v_d[bass.ds(h, 1), :, :].rearrange("a p n -> (a p) n")).then_inc(kv_in[par], 16)

            def load_rest(h, b):
                rows = bass.ds(h * HD, HD)
                dst = query_rest[b]
                cols = slice(b * QB, (b + 1) * QB)

                def shared(src):
                    return src.rearrange("r (a n) -> r a n", a=1).broadcast_to([src.shape[0], VARIANTS, QB])
                rel = rel_lo_d[bass.ds(h, 1), :, cols].rearrange("a r n -> (a r) n")
                sp.dma_start(dst[0:HD, :, :].bitcast(F32), shared(qk_lo_d[rows, cols])).then_inc(rest_in[b], 16)
                sp.dma_start(dst[HD:2 * HD, :, :].bitcast(F32), shared(qk_hi_d[rows, cols])).then_inc(rest_in[b], 16)
                sp.dma_start(dst[2 * HD:2 * HD + SIDE, :, :].bitcast(F32), shared(rel[0:SIDE, :])).then_inc(rest_in[b], 16)
                sp.dma_start(dst[2 * HD + SIDE:TOP - 1, :, :].bitcast(F32),
                             rel[SIDE:2 * SIDE, :].rearrange("(v r) n -> r v n", r=VROWS)).then_inc(rest_in[b], 16)

            def load_max(h, b):
                row = m_d[bass.ds(h, 1), b * QB:(b + 1) * QB]
                sp.wait_ge(negt_ok, QBLOCKS * h + b + 1)
                sp.dma_start(row.rearrange("a (t p) -> (a t) p", p=P), neg_mt[b][:].bitcast(F32)).then_inc(m_out, 16)
                sp.wait_ge(m_out, 16 * (QBLOCKS * h + b + 1))
                sp.dma_start(query_rest[b][TOP - 1:TOP, :, :].bitcast(F32),
                             row.rearrange("r (a n) -> r a n", a=1).broadcast_to([1, VARIANTS, QB])).then_inc(rest_in[b], 16)

            def store(h, par, b):
                g = (QBLOCKS * par + b) % 2
                sp.wait_ge(acc_a, QBLOCKS * h + b + 2)
                sp.wait_ge(acc_d, QBLOCKS * h + b + 2)
                sp.dma_start(ot_d[bass.ds(h, 1), :, b * QB:(b + 1) * QB].rearrange("a r n -> (a r) n"),
                             o_t[g][:].rearrange("r c n -> r (c n)")).then_inc(ot_out[g], 16)

            def head(h, par, last=False):
                if not last:
                    sp.wait_ge(s_ok, UNITS * h + LEAD)
                    load_hi(h + 1, 1 - par)
                load_max(h, 2)
                if not last:
                    sp.wait_ge(pv_ok, UNITS * h + RING)
                    load_kv(h + 1, 1 - par)
                for b in range(QBLOCKS):
                    if not last:
                        sp.wait_ge(s_ok, UNITS * h + TILES * (b + 1))
                        load_rest(h + 1, b)
                    store(h, par, b)
                    if not last and b < 2:
                        load_max(h + 1, b)

            sp.wait_ge(hot_hi_ok, 2)
            load_hi(0, 0)
            sp.wait_ge(hot_rest_ok, 2)
            load_kv(0, 0)
            for b in range(QBLOCKS):
                load_rest(0, b)
            for b in range(2):
                load_max(0, b)
            with sp.Fori(0, loop_heads // 2) as i:
                for par in range(2):
                    head(2 * i + par, par)
            head(HEADS - 2, 0)
            head(HEADS - 1, 1, last=True)
            for g in range(2):
                sp.wait_ge(ot_out[g], 16 + 16 * QBLOCKS * HEADS // 2)

        @block.gpsimd
        def _(pool):
            for g in range(2):
                pool.sem_inc(ot_out[g], 16)
            n = 0

            def made(ins):
                nonlocal n
                n += 1
                ins.then_inc(hot_ok, 1)
                pool.wait_ge(hot_ok, n)

            def fill_where(m, base, pattern):
                view = m[:].rearrange("p (y x) -> p y x", x=SIDE) if len(pattern) == 2 else m[:].rearrange("p (v y x) -> p v y x", y=VROWS, x=SIDE)
                made(pool.affine_select(out=view, in_=view, compare_op=ALU.not_equal, fill=1.0, base=base,
                                        pattern=pattern, channel_multiplier=1))

            made(pool.memset(hot_hi[:], 0.0))
            fill_where(hot_hi, -HD, [[0, SIDE], [-1, SIDE]])
            fill_where(hot_hi, -(HD + SIDE), [[-1, SIDE], [0, SIDE]])
            made(pool.memset(hot_rest[:], 0.0))
            fill_where(hot_rest, -2 * HD, [[0, SIDE], [-1, SIDE]])
            fill_where(hot_rest, -(2 * HD + SIDE), [[0, VARIANTS], [-1, VROWS], [0, SIDE]])
            fill_where(hot_rest, -(TOP - 1), [[0, SIDE], [0, SIDE]])
            made(pool.memset(ident[:], 0.0))
            made(pool.affine_select(out=ident[:], in_=ident[:], compare_op=ALU.not_equal, fill=1.0, base=0,
                                    pattern=[[-1, P]], channel_multiplier=1))

        @block.tensor
        def _(pe):
            def chunk(tp, s, ps):
                tile = slice(s // 3 * P, (s // 3 + 1) * P)
                for c in range(2):
                    keys = slice(s % 3 * QB + c * TB, s % 3 * QB + (c + 1) * TB)
                    last = pe.matmul(ps[:, c, 0:TB], query_hi[tp][:, tile], key_hi[tp][:, keys], start=True, stop=True)
                last.then_inc(mm_ok, 1)

            def scores(n, par, idx, turn=None):
                b, j = idx // TILES, idx % TILES
                bank = 2 * (idx % 2)
                pe.wait_ge(f_ok, n + 1)
                if turn is not None:
                    pe.transpose(ps_s[0:6, bank, TB:TB + P], neg_m[turn][:], ident[:])
                for c in range(2):
                    pe.matmul(ps_s[:, bank + c, 0:TB], key_hi[par][:, j * P:(j + 1) * P],
                              query_hi[par][:, b * QB + c * TB:b * QB + (c + 1) * TB], start=True, stop=False)
                for c in range(2):
                    last = pe.matmul(ps_s[:, bank + c, 0:TB], key_rest[par][:, j * P:(j + 1) * P],
                                     query_rest[b][:, j // 3, c * TB:(c + 1) * TB], start=False, stop=True)
                last.then_inc(s_ok, 1)

            def pv(n, par, idx):
                j, r = idx % TILES, (2 * par + idx) % RING
                pe.wait_ge(lo_ok, n + 3)
                for part in (p_hi, p_lo):
                    for c in range(2):
                        last = pe.matmul(ps_o[0:VW, c, 0:TB], val[par][:, j, :], part[r][:, c, :],
                                         start=(j == 0 and part is p_hi), stop=(j == TILES - 1 and part is p_lo))
                last.then_inc(pv_ok, 1)

            def head(h, par, last=False):
                for k in range(UNITS):
                    up, idx = unit_at(par, k)
                    if not (last and up != par):
                        turn = turned_at(k, last)
                        if idx == 0:
                            pe.wait_ge(kv_in[up], 48 * ((h + 1) // 2 + 1) if isinstance(h, int) else 48 * (h0 + 1 + par))
                        if idx % TILES == 0:
                            pe.wait_ge(rest_in[idx // TILES], 80 * (h + 1 + (up != par)))
                        if turn is not None:
                            pe.wait_ge(neg_ok, QBLOCKS * (h + (turn < 2)) + turn + 1)
                        scores(UNITS * h + k + LEAD, up, idx, turn)
                    tp, s = chunk_at(h, par, k)
                    if not (last and tp != par):
                        if s == 0:
                            pe.wait_ge(hi_in[tp], 48 * ((h + 1) // 2 + 1) if isinstance(h, int) else 48 * (h0 + 1 + par))
                        pe.wait_ge(mx_ok, UNITS * (h + 1) + k - SHIFT)
                        chunk(tp, s, ps_m)
                    if k % TILES == 0:
                        pe.wait_ge(acc_a, QBLOCKS * h + k // TILES + 1)
                        pe.wait_ge(acc_d, QBLOCKS * h + k // TILES + 1)
                    pv(UNITS * h + k, par, k)

            pe.wait_ge(hi_in[0], 48)
            spare = [ps_m, ps_s[:, 0:2, :], ps_s[:, 2:4, :]]
            for s in range(UNITS - SHIFT):
                if s >= 3:
                    pe.wait_ge(mx_ok, s - 2)
                chunk(0, s, spare[s % 3])
                for b in range(2):
                    if s == TILES * (b + 1) + 3:
                        if b == 0:
                            pe.wait_ge(hot_ok, 9)
                        pe.wait_ge(neg_ok, b + 1)
                        pe.transpose(ps_o[0:6, b, 0:P], neg_m[b][:], ident[:]).then_inc(turned, 1)
            pe.wait_ge(mx_ok, UNITS - SHIFT)
            pe.wait_ge(kv_in[0], 48)
            pe.wait_ge(rest_in[0], 80)
            for idx in range(LEAD):
                scores(idx, 0, idx)
            pe.wait_ge(negt_ok, 2)
            with pe.Fori(0, loop_heads // 2) as h0:
                for par in range(2):
                    head(2 * h0 + par, par)
            head(HEADS - 2, 0)
            head(HEADS - 1, 1, last=True)

        @block.scalar
        def _(act):
            def exps(n, par, idx, turn=None):
                bank, r = 2 * (idx % 2), (2 * par + idx) % RING
                act.wait_ge(s_ok, n + 1)
                act.wait_ge(pv_ok, n + 1)
                act.activation(p_hi[r][:], ps_s[:, bank:bank + 2, 0:TB], ACT.Exp).then_inc(hi_ok, 1)
                if turn is not None:
                    act.copy(neg_mt[turn][:], ps_s[0:6, bank, TB:TB + P]).then_inc(negt_ok, 1)
                act.wait_ge(lo_ok, n + 1)
                act.activation(p_f[idx % 2][:], ps_s[:, bank:bank + 2, 0:TB], ACT.Exp).then_inc(f_ok, 1)

            def head(h, par, last=False):
                for k in range(UNITS):
                    up, idx = unit_at(par, k)
                    if not (last and up != par):
                        exps(UNITS * h + k + LEAD, up, idx, turned_at(k, last))
                    if k % TILES == TILES - 1:
                        b = k // TILES
                        g = (QBLOCKS * par + b) % 2
                        act.wait_ge(pv_ok, UNITS * h + k + 1 + RING)
                        act.wait_ge(ot_out[g], out_count(h, par, b))
                        act.copy(o_t[g][:, 0, :], ps_o[0:VW, 0, 0:TB]).then_inc(acc_a, 1)

            def out_count(h, par, b):
                return 16 * ((QBLOCKS * par + b) // 2) + 16 * QBLOCKS * half(h, par) + 16

            def half(h, par):
                return (h - par) // 2 if isinstance(h, int) else h0

            act.wait_ge(hot_ok, 3)
            for i in range(2):
                act.copy(key_hi[i][:], hot_hi[:]).then_inc(hot_hi_ok, 1)
            act.sem_inc(acc_a, 1)
            act.sem_inc(f_ok, 2)
            for b in range(2):
                act.wait_ge(turned, b + 1)
                act.copy(neg_mt[b][:], ps_o[0:6, b, 0:P]).then_inc(negt_ok, 1)
            for idx in range(LEAD):
                exps(idx, 0, idx)
            with act.Fori(0, loop_heads // 2) as h0:
                for par in range(2):
                    head(2 * h0 + par, par)
            head(HEADS - 2, 0)
            head(HEADS - 1, 1, last=True)

        @block.vector
        def _(dve):
            def reduce(count, s, ps):
                dve.wait_ge(mm_ok, count + 1)
                dve.tensor_reduce(mx[s // TILES][:, s // 3 % 6, s % 3:s % 3 + 1], ps[:, :, 0:TB], AX.XY, ALU.max).then_inc(mx_ok, 1)
                if s % TILES == TILES - 1:
                    dve.wait_ge(mx_ok, count + 1)
                    dve.tensor_reduce(neg_m[s // TILES][:], mx[s // TILES][:], AX.X, ALU.max, negate=True).then_inc(neg_ok, 1)

            def low(n, par, idx):
                r = (2 * par + idx) % RING
                dve.wait_ge(f_ok, n + 3)
                dve.tensor_tensor(p_lo[r][:], p_f[idx % 2][:], p_hi[r][:].bitcast(F32), ALU.subtract).then_inc(lo_ok, 1)

            def head(h, par, last=False):
                for k in range(UNITS):
                    tp, s = chunk_at(h, par, k)
                    if not (last and tp != par):
                        reduce(UNITS * (h + 1) + k - SHIFT, s, ps_m)
                    up, idx = unit_at(par, k)
                    if not (last and up != par):
                        low(UNITS * h + k + LEAD, up, idx)
                    if k % TILES == TILES - 1:
                        b = k // TILES
                        g = (QBLOCKS * par + b) % 2
                        dve.wait_ge(pv_ok, UNITS * h + k + 1 + RING)
                        dve.wait_ge(ot_out[g], out_count(h, par, b))
                        dve.tensor_copy(o_t[g][:, 1, :], ps_o[0:VW, 1, 0:TB]).then_inc(acc_d, 1)

            def out_count(h, par, b):
                return 16 * ((QBLOCKS * par + b) // 2) + 16 * QBLOCKS * half(h, par) + 16

            def half(h, par):
                return (h - par) // 2 if isinstance(h, int) else h0

            dve.sem_inc(acc_d, 1)
            dve.sem_inc(lo_ok, 2)
            dve.sem_inc(pv_ok, RING)
            dve.wait_ge(hot_ok, 7)
            for i in range(2):
                dve.tensor_copy(key_rest[i][:], hot_rest[0:TOP, :]).then_inc(hot_rest_ok, 1)
            for s in range(UNITS - SHIFT):
                reduce(s, s, [ps_m, ps_s[:, 0:2, :], ps_s[:, 2:4, :]][s % 3])
            for idx in range(LEAD):
                low(idx, 0, idx)
            with dve.Fori(0, loop_heads // 2) as h0:
                for par in range(2):
                    head(2 * h0 + par, par)
            head(HEADS - 2, 0)
            head(HEADS - 1, 1, last=True)


EXPERTS = 8
TOP_K = 2
FF = 4 * C
QUARTERS = 4
FQ = FF // QUARTERS
FC = FQ // P


def phase_proj(nc, x, ot_d, proj_w, proj_b, gate_w, gate_b, x1, xt_hi, xt_lo, comb):
    with ExitStack() as ctx:
        def sb(name, shape, dt=F32):
            return ctx.enter_context(nc.sbuf_tensor(name, shape, dt))

        def sem(name):
            return ctx.enter_context(nc.semaphore(name))

        oh = sb("oh", [P, KC, S])
        ol = sb("ol", [P, KC, S])
        rsum = sb("rsum", [HEADS, S])
        spread = sb("spread", [HEADS, KC, P])
        o_f = [sb(f"o_f{i}", [P, KC, TB]) for i in range(2)]
        o_hi = [sb(f"o_hi{i}", [P, KC, TB], F32R) for i in range(2)]
        o_lo = [sb(f"o_lo{i}", [P, KC, TB], F32R) for i in range(2)]
        w_raw = sb("pw_raw", [P, KC, C])
        w_hi = sb("pw_hi", [P, KC, C], F32R)
        w_lo = sb("pw_lo", [P, KC, C], F32R)
        g_raw = sb("g_raw", [P, KC, EXPERTS])
        g_hi = sb("g_hi", [P, KC, EXPERTS], F32R)
        g_lo = sb("g_lo", [P, KC, EXPERTS], F32R)
        g_b = sb("g_b", [EXPERTS, 1])
        p_b = sb("p_b", [P, C])
        ident = sb("ident3", [P, P])
        stats = sb("stats2", [P, TILES, 6])
        mv = sb("mv2", [P, TILES, 2])
        veps = sb("veps2", [P, TILES])
        root = sb("root2", [P, TILES])
        rstd = sb("rstd2", [P, TILES])
        nt = sb("nt2", [P, TILES])
        xn = [sb(f"xnn{i}", [P, TPB, C]) for i in range(2)]
        logit_t = rsum[0:EXPERTS, :]
        gate = sb("gate", [P, TILES, EXPERTS])
        gate_e = sb("gate_e", [P, TILES, EXPERTS])
        beats = sb("beats", [P, EXPERTS, TILES, EXPERTS])
        rank = sb("rank", [P, TILES, EXPERTS])
        top = sb("top", [P, TILES])
        ps_r = ctx.enter_context(nc.psum_tensor("ps_r", [P, KC, 512], F32))
        ps_y = ctx.enter_context(nc.psum_tensor("ps_y2", [P, TPB, 512], F32))
        ps_g = ctx.enter_context(nc.psum_tensor("ps_g", [P, 2, 512], F32))
        ps_t = [ps_r, ps_y]

        o_in = sem("o_in")
        x_in = sem("x_in2")
        w_in = sem("w_in2")
        const_ok = sem("const_ok")
        w_hi_ok = sem("w_hi_ok2")
        w_lo_ok = sem("w_lo_ok2")
        x_ok = sem("x_ok")
        o_sum = sem("o_sum")
        r_ok = sem("r_ok")
        spread_ok = sem("spread_ok")
        of_ok = sem("of_ok")
        ohi_ok = sem("ohi_ok")
        olo_ok = sem("olo_ok")
        y_ok = sem("y_ok2")
        x1_ok = sem("x1_ok")
        own = sem("own2")
        root_in = sem("root_in")
        root_ok = sem("root_ok2")
        xn_ok = sem("xn_ok2")
        t_ok = sem("t_ok")
        thi_ok = sem("thi_ok")
        tlo_ok = sem("tlo_ok")
        l_ok = sem("l_ok")
        lt_ok = sem("lt_ok")
        g_ok = sem("g_ok")
        e_in = sem("e_in")
        e_ok = sem("e_ok")
        block = ctx.enter_context(nc.Block())

        @block.sync
        def _(sp):
            for c in range(KC):
                heads = slice(c * HPT, (c + 1) * HPT)
                for n in range(HPT):
                    h = c * HPT + n
                    rows = slice(n * HD, (n + 1) * HD)
                    sp.dma_start(oh[rows, c, :], ot_d[h, 0:HD, :]).then_inc(o_in, 16)
                    sp.dma_start(ol[rows, c, :], ot_d[h, HD:2 * HD, :]).then_inc(o_in, 16)
            sp.dma_start(rsum[:], ot_d[:, 2 * HD, :]).then_inc(o_in, 16)
            sp.wait_ge(o_in, 16 * (2 * HEADS + 1))

        @block.gpsimd
        def _(pool):
            pool.memset(ident[:], 0.0).then_inc(const_ok, 1)
            pool.memset(spread[:], 1.0).then_inc(const_ok, 1)
            pool.wait_ge(const_ok, 2)
            pool.affine_select(out=ident[:], in_=ident[:], compare_op=ALU.not_equal, fill=1.0, base=0,
                               pattern=[[-1, P]], channel_multiplier=1).then_inc(const_ok, 1)
            flat = spread[:].rearrange("h c r -> h (c r)")
            pool.affine_select(out=flat, in_=flat, compare_op=ALU.is_ge, fill=0.0, base=0,
                               pattern=[[1, KC * P]], channel_multiplier=-HD).then_inc(const_ok, 1)
            pool.wait_ge(const_ok, 4)
            pool.affine_select(out=flat, in_=flat, compare_op=ALU.is_ge, fill=0.0, base=HD - 1,
                               pattern=[[-1, KC * P]], channel_multiplier=HD).then_inc(const_ok, 1)
            pool.wait_ge(o_in, 16 * (2 * HEADS + 1))
            with pool.Fori(0, BLOCKS) as b:
                cols = bass.ds(b * TB, TB)
                pool.tensor_tensor(oh[:, :, cols], oh[:, :, cols], ol[:, :, cols], ALU.add).then_inc(o_sum, 1)

        @block.tensor
        def _(pe):
            def transposed(par):
                for k in range(KC):
                    for t in range(TPB):
                        last = pe.transpose(ps_t[par][:, k, t * P:(t + 1) * P], xn[par][:, t, k * P:(k + 1) * P], ident[:])
                last.then_inc(t_ok, 1)

            pe.wait_ge(const_ok, 5)
            pe.wait_ge(r_ok, 1)
            pe.wait_ge(w_lo_ok, 2)
            with pe.Fori(0, BLOCKS // 2) as i:
                for par in range(2):
                    pe.wait_ge(of_ok, 2 * i + par + 1)
                    for c in range(KC):
                        last = pe.matmul(ps_r[:, c, 0:TB], spread[:, c, :], rsum[:, bass.ds((2 * i + par) * TB, TB)],
                                         start=True, stop=True)
                    last.then_inc(spread_ok, 1)
                for par in range(2):
                    blk = 2 * i + par
                    pe.wait_ge(olo_ok, blk + 1)
                    for t in range(TPB):
                        pe.wait_ge(x1_ok, TPB * blk + t + 1)
                        cut = slice(t * P, (t + 1) * P)
                        for n, (v, w) in enumerate([(o_hi, w_hi), (o_hi, w_lo), (o_lo, w_hi)]):
                            for k in range(KC):
                                last = pe.matmul(ps_y[:, t, 0:C], v[par][:, k, cut], w[:, k, :],
                                                 start=(n + k == 0), stop=(n == 2 and k == KC - 1))
                        last.then_inc(y_ok, 1)
            with pe.Fori(0, BLOCKS // 2) as i:
                for par in range(2):
                    pe.wait_ge(xn_ok, 2 * i + par + 1)
                    transposed(par)
                for par in range(2):
                    blk = 2 * i + par
                    pe.wait_ge(tlo_ok, blk + 1)
                    pe.wait_ge(lt_ok, blk + 1)
                    cols = bass.ds(blk * TB, TB)
                    for n, (w, v) in enumerate([(g_hi, xt_hi), (g_lo, xt_hi), (g_hi, xt_lo)]):
                        for k in range(KC):
                            last = pe.matmul(ps_g[0:EXPERTS, par, 0:TB], w[:, k, :], v[:, k, cols],
                                             start=(n + k == 0), stop=(n == 2 and k == KC - 1))
                    last.then_inc(l_ok, 1)
            pe.wait_ge(lt_ok, BLOCKS + 2)
            for t in range(TILES):
                last = pe.transpose(ps_g[:, 0, t * EXPERTS:(t + 1) * EXPERTS], logit_t[:, t * P:(t + 1) * P],
                                    ident[0:EXPERTS, 0:EXPERTS])
            last.then_inc(g_ok, 1)

        @block.scalar
        def _(act):
            act.dma_start(w_raw[:], proj_w.rearrange("(k p) n -> p k n", p=P)).then_inc(w_in, 16)
            act.dma_start(g_raw[:], gate_w.rearrange("(k p) n -> p k n", p=P)).then_inc(w_in, 16)
            act.dma_start(g_b[:], gate_b.rearrange("(n a) -> n a", a=1)).then_inc(w_in, 16)
            act.dma_start(p_b[:], proj_b.rearrange("(a n) -> a n", a=1).broadcast_to([P, C])).then_inc(w_in, 16)
            act.dma_start(x1[:], x.rearrange("(t p) c -> p t c", p=P)).then_inc(x_in, 16)
            act.wait_ge(w_in, 64)
            act.copy(w_hi[:], w_raw[:]).then_inc(w_hi_ok, 1)
            act.copy(g_hi[:], g_raw[:]).then_inc(w_hi_ok, 1)
            with act.Fori(0, BLOCKS // 2) as i:
                for par in range(2):
                    blk = 2 * i + par
                    act.wait_ge(of_ok, blk + 2)
                    act.copy(o_hi[par][:], o_f[par][:]).then_inc(ohi_ok, 1)
            act.wait_ge(root_in, 1)
            act.activation(root[:], veps[:], ACT.Sqrt).then_inc(root_ok, 1)
            with act.Fori(0, BLOCKS // 2) as i:
                for par in range(2):
                    act.wait_ge(t_ok, 2 * i + par + 1)
                    act.copy(xt_hi[:, :, bass.ds((2 * i + par) * TB, TB)], ps_t[par][:, :, 0:TB]).then_inc(thi_ok, 1)
                for par in range(2):
                    act.wait_ge(l_ok, 2 * i + par + 1)
                    act.activation(logit_t[:, bass.ds((2 * i + par) * TB, TB)], ps_g[0:EXPERTS, par, 0:TB], ACT.Identity,
                                   bias=g_b[:]).then_inc(lt_ok, 1)
            act.wait_ge(e_in, 1)
            act.activation(gate_e[:], gate[:], ACT.Exp).then_inc(e_ok, 1)

        @block.vector
        def _(dve):
            n_own = [0]

            def step(ins):
                n_own[0] += 1
                ins.then_inc(own, 1)
                dve.wait_ge(own, n_own[0])

            dve.sem_inc(x1_ok, TPB)
            dve.sem_inc(of_ok, 1)
            dve.sem_inc(lt_ok, 2)
            dve.wait_ge(w_in, 64)
            dve.wait_ge(x_in, 16)
            bias = p_b[:].rearrange("p (a n) -> p a n", a=1).broadcast_to([P, TILES, C])
            dve.tensor_tensor(x1[:], x1[:], bias, ALU.add).then_inc(x_ok, 1)
            dve.wait_ge(w_hi_ok, 2)
            dve.tensor_tensor(w_lo[:], w_raw[:], w_hi[:].bitcast(F32), ALU.subtract).then_inc(w_lo_ok, 1)
            dve.tensor_tensor(g_lo[:], g_raw[:], g_hi[:].bitcast(F32), ALU.subtract).then_inc(w_lo_ok, 1)
            dve.wait_ge(o_in, 16 * (2 * HEADS + 1))
            dve.reciprocal(rsum[:], rsum[:]).then_inc(r_ok, 1)
            dve.wait_ge(x_ok, 1)

            def normalised(i, par):
                blk = 2 * i + par
                dve.wait_ge(spread_ok, blk + 1)
                dve.wait_ge(o_sum, blk + 1)
                dve.tensor_tensor(o_f[par][:], ps_r[:, :, 0:TB], oh[:, :, bass.ds(blk * TB, TB)], ALU.mult).then_inc(of_ok, 1)

            with dve.Fori(0, BLOCKS // 2) as i:
                for par in range(2):
                    normalised(i, par)
                for par in range(2):
                    dve.wait_ge(ohi_ok, 2 * i + par + 1)
                    dve.tensor_tensor(o_lo[par][:], o_f[par][:], o_hi[par][:].bitcast(F32), ALU.subtract).then_inc(olo_ok, 1)
                for par in range(2):
                    blk = 2 * i + par
                    for t in range(TPB):
                        tile = bass.ds(TPB * blk + t, 1)
                        dve.wait_ge(y_ok, TPB * blk + t + 1)
                        row = x1[:, tile, :].rearrange("p a c -> p (a c)")
                        dve.tensor_tensor(row, ps_y[:, t, 0:C], row, ALU.add).then_inc(x1_ok, 1)
                        dve.wait_ge(x1_ok, TPB * blk + t + 1 + TPB)
                        dve.bn_stats(stats[:, tile, :].rearrange("p a c -> p (a c)"), row).then_inc(own, 1)
            n_own[0] += TILES
            dve.wait_ge(own, n_own[0])
            for t in range(TILES):
                last = dve.bn_aggr(mv[:, t, :], stats[:, t, :])
            step(last)
            dve.tensor_scalar(veps[:], mv[:, :, 1], LN2_EPS, None, ALU.add).then_inc(root_in, 1)
            dve.wait_ge(root_ok, 1)
            step(dve.reciprocal(rstd[:], root[:]))
            step(dve.tensor_tensor(nt[:], rstd[:], rstd[:], ALU.mult))
            step(dve.tensor_tensor(nt[:], nt[:], veps[:], ALU.mult))
            step(dve.tensor_scalar(nt[:], nt[:], -0.5, 1.5, ALU.mult, ALU.add))
            step(dve.tensor_tensor(rstd[:], rstd[:], nt[:], ALU.mult))
            with dve.Fori(0, BLOCKS // 2) as i:
                for par in range(2):
                    blk = 2 * i + par
                    for t in range(TPB):
                        tile = bass.ds(TPB * blk + t, 1)
                        last = dve.tensor_scalar(xn[par][:, t, :], x1[:, tile, :].rearrange("p a c -> p (a c)"),
                                                 mv[:, tile, 0:1].rearrange("p a c -> p (a c)"), rstd[:, tile],
                                                 ALU.subtract, ALU.mult)
                    last.then_inc(xn_ok, 1)
                for par in range(2):
                    blk = 2 * i + par
                    cols = bass.ds(blk * TB, TB)
                    dve.wait_ge(thi_ok, blk + 1)
                    dve.tensor_tensor(xt_lo[:, :, cols], ps_t[par][:, :, 0:TB], xt_hi[:, :, cols].bitcast(F32),
                                      ALU.subtract).then_inc(tlo_ok, 1)
            each = [P, TILES, EXPERTS]

            def over(v):
                return v.rearrange("p (t a) -> p t a", a=1).broadcast_to(each)
            dve.wait_ge(g_ok, 1)
            logits = ps_g[:, 0, 0:TILES * EXPERTS].rearrange("p (t e) -> p t e", e=EXPERTS)
            step(dve.tensor_reduce(top[:], logits, AX.X, ALU.max))
            dve.tensor_tensor(gate[:], logits, over(top[:]), ALU.subtract).then_inc(e_in, 1)
            dve.wait_ge(e_ok, 1)
            step(dve.tensor_reduce(top[:], gate_e[:], AX.X, ALU.add))
            step(dve.reciprocal(top[:], top[:]))
            step(dve.tensor_tensor(gate[:], gate_e[:], over(top[:]), ALU.mult))
            for s in range(EXPERTS):
                for lo_e, hi_e, op in ((0, s + 1, ALU.is_gt), (s + 1, EXPERTS, ALU.is_ge)):
                    if lo_e < hi_e:
                        last = dve.tensor_tensor(beats[:, s, :, lo_e:hi_e],
                                                 gate[:, :, s:s + 1].broadcast_to([P, TILES, hi_e - lo_e]),
                                                 gate[:, :, lo_e:hi_e], op)
            step(last)
            step(dve.tensor_reduce(rank[:].rearrange("p t e -> p (t e)"), beats[:].rearrange("p s t e -> p (t e) s"), AX.X, ALU.add))
            step(dve.scalar_tensor_tensor(comb[:].rearrange("p e t -> p t e"), rank[:], TOP_K - 0.5, gate[:], ALU.is_lt, ALU.mult))


def phase_experts(nc, w1_u, b1_t, w2_u, b2, out, x1, xt_hi, xt_lo, comb):
    with ExitStack() as ctx:
        def sb(name, shape, dt=F32):
            return ctx.enter_context(nc.sbuf_tensor(name, shape, dt))

        def sem(name):
            return ctx.enter_context(nc.semaphore(name))

        WN = KC * FQ
        w1_raw = [sb(f"w1_raw{i}", [P, KC, FQ]) for i in range(2)]
        w2_raw = [sb(f"w2_raw{i}", [P, FC, C]) for i in range(2)]
        w1_hi = [sb(f"w1_hi{i}", [P, KC, FQ], F32R) for i in range(2)]
        w1_lo = [sb(f"w1_lo{i}", [P, KC, FQ], F32R) for i in range(2)]
        w2_hi = [sb(f"w2_hi{i}", [P, FC, C], F32R) for i in range(2)]
        w2_lo = [sb(f"w2_lo{i}", [P, FC, C], F32R) for i in range(2)]
        h_f = sb("h_f", [P, FC, TB])
        h_hi = [sb(f"h_hi{i}", [P, FC, TB], F32R) for i in range(2)]
        h_lo = [sb(f"h_lo{i}", [P, FC, TB], F32R) for i in range(2)]
        b1_sb = sb("b1_sb", [P, EXPERTS * FF // P])
        b2_sb = sb("b2_sb", [P, EXPERTS * C])
        ps_h = ctx.enter_context(nc.psum_tensor("ps_h", [P, FC, 512], F32))
        ps_o = ctx.enter_context(nc.psum_tensor("ps_o3", [P, TPB, 512], F32))

        b_in = sem("b_in3")
        raw_in = [sem(f"raw_in{i}") for i in range(2)]
        split_go = sem("split_go")
        w_hi_ok = sem("w_hi_ok3")
        w_ok = sem("w_ok")
        h_ok = sem("h_ok")
        g_hi = sem("g_hi_ok")
        g_f = sem("g_f_ok")
        g_lo = sem("g_lo_ok")
        y_ok = sem("y_ok3")
        y_free = sem("y_free")
        b2_ok = sem("b2_ok")
        done = sem("done")
        block = ctx.enter_context(nc.Block())

        UNITS_E = EXPERTS * QUARTERS
        CB2 = C // QUARTERS
        OUT_CREDIT = TILES + 1

        @block.sync
        def _(sp):
            sp.dma_start(b1_sb[:], b1_t).then_inc(b_in, 16)
            sp.dma_start(b2_sb[:], b2.rearrange("(a e) n -> a (e n)", a=1).broadcast_to([P, EXPERTS * C])).then_inc(b_in, 16)
            with sp.Fori(0, UNITS_E // 2) as i:
                for par in range(2):
                    u = 2 * i + par
                    sp.wait_ge(w_ok, u + 1)
                    sp.dma_start(w1_raw[par][:].rearrange("p k n -> p (k n)"), w1_u[bass.ds(u, 1), :, :].rearrange("a p n -> (a p) n")).then_inc(raw_in[par], 16)
                    sp.dma_start(w2_raw[par][:].rearrange("p k n -> p (k n)"), w2_u[bass.ds(u, 1), :, :].rearrange("a p n -> (a p) n")).then_inc(raw_in[par], 16)
            sp.wait_ge(y_free, TPB + UNITS_E * TILES)
            sp.wait_ge(b2_ok, UNITS_E * TILES)
            sp.dma_start(out.rearrange("(t p) c -> p t c", p=P), x1[:]).then_inc(done, 16)
            sp.wait_ge(done, 16)

        @block.gpsimd
        def _(pool):
            pool.sem_inc(w_ok, 2)
            with pool.Fori(0, UNITS_E // 2) as i:
                for par in range(2):
                    u = 2 * i + par
                    pool.wait_ge(raw_in[par], 32 * i + 32)
                    pool.wait_ge(y_ok, TILES * u - TILES + OUT_CREDIT)
                    pool.sem_inc(split_go, 1)
                    pool.tensor_copy(w1_hi[par][:], w1_raw[par][:]).then_inc(w_hi_ok, 1)
                    pool.tensor_copy(w2_hi[par][:], w2_raw[par][:]).then_inc(w_hi_ok, 1)
                    pool.wait_ge(w_hi_ok, 4 * i + 2 * par + 2)
                    pool.tensor_tensor(w1_lo[par][:], w1_raw[par][:], w1_hi[par][:].bitcast(F32), ALU.subtract)
                    pool.tensor_tensor(w2_lo[par][:], w2_raw[par][:], w2_hi[par][:].bitcast(F32), ALU.subtract).then_inc(w_ok, 1)

        @block.tensor
        def _(pe):
            with pe.Fori(0, UNITS_E // 2) as i:
                for w in range(2):
                    with pe.Fori(0, BLOCKS // 2) as j:
                        pe.wait_ge(w_ok, 2 * i + w + 3)
                        for par in range(2):
                            blk = 2 * j + par
                            n = (2 * i + w) * BLOCKS + blk
                            cols = bass.ds(blk * TB, TB)
                            for f in range(FC):
                                pe.wait_ge(g_f, FC * n + f + 1)
                                cut = slice(f * P, (f + 1) * P)
                                for m, (wt, v) in enumerate([(w1_hi, xt_hi), (w1_lo, xt_hi), (w1_hi, xt_lo)]):
                                    for k in range(KC):
                                        last = pe.matmul(ps_h[:, f, 0:TB], wt[w][:, k, cut], v[:, k, cols],
                                                         start=(m + k == 0), stop=(m == 2 and k == KC - 1))
                                last.then_inc(h_ok, 1)
                            for f in range(FC):
                                pe.wait_ge(g_lo, FC * n + f + 1 + FC)
                                for t in range(TPB):
                                    if f == 0:
                                        pe.wait_ge(y_free, TPB * n + t + 1)
                                    cut = slice(t * P, (t + 1) * P)
                                    for m, (v, wt) in enumerate([(h_hi, w2_hi), (h_hi, w2_lo), (h_lo, w2_hi)]):
                                        last = pe.matmul(ps_o[:, t, 0:C], v[par][:, f, cut], wt[w][:, f, :],
                                                         start=(m + f == 0), stop=(m == 2 and f == FC - 1))
                                    if f == FC - 1:
                                        last.then_inc(y_ok, 1)

        @block.scalar
        def _(act):
            act.sem_inc(g_f, FC)
            act.wait_ge(b_in, 32)
            with act.Fori(0, UNITS_E) as u:
                with act.Fori(0, BLOCKS // 2) as j:
                    for par in range(2):
                        n = u * BLOCKS + 2 * j + par
                        act.wait_ge(y_ok, TPB * n - TPB + OUT_CREDIT)
                        for f in range(FC):
                            bias = b1_sb[:, bass.ds(FC * u + f, 1)]
                            act.wait_ge(h_ok, FC * n + f + 1)
                            act.activation(h_hi[par][:, f, :], ps_h[:, f, 0:TB], ACT.Gelu, bias=bias).then_inc(g_hi, 1)
                            act.wait_ge(g_lo, FC * n + f + 1)
                            act.activation(h_f[:, f, :], ps_h[:, f, 0:TB], ACT.Gelu, bias=bias).then_inc(g_f, 1)

        @block.vector
        def _(dve):
            dve.sem_inc(g_lo, FC)
            dve.sem_inc(y_ok, OUT_CREDIT)
            dve.sem_inc(y_free, TPB)
            dve.wait_ge(b_in, 32)
            with dve.Fori(0, EXPERTS) as e:
                with dve.Fori(0, QUARTERS) as q:
                    with dve.Fori(0, BLOCKS // 2) as j:
                        for par in range(2):
                            blk = 2 * j + par
                            n = e * (QUARTERS * BLOCKS) + q * BLOCKS + blk
                            for t in range(TPB):
                                part = x1[:, bass.ds(TPB * blk + t, 1), bass.ds(q * CB2, CB2)].rearrange("p a c -> p (a c)")
                                weight = comb[:].rearrange("p e t -> p (e t)")[:, bass.ds(e * TILES + TPB * blk + t, 1)]
                                dve.scalar_tensor_tensor(part, b2_sb[:, bass.ds(e * C + q * CB2, CB2)], weight, part,
                                                         ALU.mult, ALU.add).then_inc(b2_ok, 1)
                            for f in range(FC):
                                dve.wait_ge(g_f, FC * n + f + 1 + FC)
                                dve.tensor_tensor(h_lo[par][:, f, :], h_f[:, f, :], h_hi[par][:, f, :].bitcast(F32),
                                                  ALU.subtract).then_inc(g_lo, 1)
                            dve.wait_ge(b2_ok, TPB * n + TPB)
                            for t in range(TPB):
                                row = x1[:, bass.ds(TPB * blk + t, 1), :].rearrange("p a c -> p (a c)")
                                weight = comb[:].rearrange("p e t -> p (e t)")[:, bass.ds(e * TILES + TPB * blk + t, 1)]
                                dve.wait_ge(y_ok, TPB * n + t + 1 + OUT_CREDIT)
                                dve.scalar_tensor_tensor(row, ps_o[:, t, 0:C], weight, row, ALU.mult, ALU.add).then_inc(y_free, 1)


def program(nc, x, qkv_w, qkv_b, qkv_b_t, proj_w, proj_b, rel_t, gate_w, gate_b, w1_u, b1_t, w2_u, b2, out):
    def dram(name, shape):
        return nc.dram_tensor(name, shape, F32).ap()

    nc.disable_value_cache = True
    qk_hi_d = dram("qk_hi_d", [2 * C, S])
    qk_lo_d = dram("qk_lo_d", [2 * C, S])
    v_d = dram("v_d", [HEADS, P, TILES * VW])
    rel_hi_d = dram("rel_hi_d", [HEADS, 2 * SIDE, S])
    rel_lo_d = dram("rel_lo_d", [HEADS, 2 * SIDE, S])
    m_d = dram("m_d", [HEADS, S])
    ot_d = dram("ot_d", [HEADS, VW, S])
    phase_qkv(nc, x, qkv_w, qkv_b, qkv_b_t, qk_hi_d, qk_lo_d, v_d)
    phase_rel(nc, rel_t, qk_hi_d, qk_lo_d, rel_hi_d, rel_lo_d)
    phase_attention(nc, qk_hi_d, qk_lo_d, rel_hi_d, rel_lo_d, v_d, m_d, ot_d)
    with ExitStack() as ctx:
        x1 = ctx.enter_context(nc.sbuf_tensor("x1", [P, TILES, C], F32))
        xt_hi = ctx.enter_context(nc.sbuf_tensor("xt_hi", [P, KC, S], F32R))
        xt_lo = ctx.enter_context(nc.sbuf_tensor("xt_lo", [P, KC, S], F32R))
        comb = ctx.enter_context(nc.sbuf_tensor("comb", [P, EXPERTS, TILES], F32))
        phase_proj(nc, x, ot_d, proj_w, proj_b, gate_w, gate_b, x1, xt_hi, xt_lo, comb)
        phase_experts(nc, w1_u, b1_t, w2_u, b2, out, x1, xt_hi, xt_lo, comb)


def kernel(**inputs):
    import numpy as np
    import concourse.bacc as bacc
    from concourse.bass_utils import run_bass_kernel_spmd

    a = {k: np.asarray(v) for k, v in inputs.items()}
    laid = {
        "x": a["x"].reshape(S, C),
        "qkv_w": a["L0_conv_qkv_w"],
        "qkv_b": a["L0_conv_qkv_b"],
        "qkv_b_t": a["L0_conv_qkv_b"].reshape(-1, P).T,
        "proj_w": a["L0_conv_proj_w"],
        "proj_b": a["L0_conv_proj_b"],
        "rel_t": np.stack([a["L0_conv_rel_pos_w"][::-1].T, a["L0_conv_rel_pos_h"][::-1].T]),
        "gate_w": a["L0_ffn_Wg"],
        "gate_b": a["L0_ffn_bg"],
        "w1_u": a["L0_ffn_W1"].reshape(EXPERTS, KC, P, QUARTERS, FQ).transpose(0, 3, 2, 1, 4).reshape(-1, P, KC * FQ),
        "b1_t": a["L0_ffn_b1"].reshape(-1, P).T,
        "w2_u": a["L0_ffn_W2"].reshape(EXPERTS * QUARTERS, FC, P, C).transpose(0, 2, 1, 3).reshape(-1, P, FC * C),
        "b2": a["L0_ffn_b2"],
    }
    laid = {k: np.ascontiguousarray(v) for k, v in laid.items()}
    nc = bacc.Bacc("TRN2", target_bir_lowering=False, num_devices=1)
    aps = {k: nc.dram_tensor(k, v.shape, mybir.dt.from_np(v.dtype), kind="ExternalInput").ap() for k, v in laid.items()}
    out = nc.dram_tensor("out", (S, C), F32, kind="ExternalOutput").ap()
    program(nc, **aps, out=out)
    r = run_bass_kernel_spmd(nc, [laid], core_ids=[0])
    return r.results[0]["out"].reshape(a["x"].shape)
```

```python
from contextlib import ExitStack

import concourse.bass as bass
from concourse import mybir

F32 = mybir.dt.float32
F32R = mybir.dt.float32r
ACT = mybir.ActivationFunctionType
ALU = mybir.AluOpType
AX = mybir.AxisListType

P = 128
SIDE = 48
S = SIDE * SIDE
C = 384
KC = C // P
HEADS = 12
HD = C // HEADS
TILES = S // P
TB = 384
BLOCKS = S // TB
TPB = TB // P
QK_TILES = 2 * KC
HPT = P // HD
REL = 2 * SIDE - 1
VW = 2 * HD + 1
SCALE = float(HD) ** -0.5
LN1_EPS = 1e-6
LN2_EPS = 1e-5


def phase_qkv(nc, x, qkv_w, qkv_b, qkv_b_t, qk_hi_d, qk_lo_d, v_d):
    GT = 6
    with ExitStack() as ctx:
        def sb(name, shape, dt=F32):
            return ctx.enter_context(nc.sbuf_tensor(name, shape, dt))

        def sem(name):
            return ctx.enter_context(nc.semaphore(name))

        x_sb = sb("x_sb", [P, TILES, C])
        xn = [sb(f"xn{i}", [P, TPB, C]) for i in range(2)]
        stats = sb("stats", [P, TILES, 6])
        mv = sb("mv", [P, TILES, 2])
        veps = sb("veps", [P, TILES])
        root = sb("root", [P, TILES])
        rstd = sb("rstd", [P, TILES])
        nt = sb("nt", [P, TILES])
        w_raw = sb("w_raw", [P, KC, 3 * C])
        w_hi = sb("w_hi", [P, KC, 3 * C], F32R)
        w_lo = sb("w_lo", [P, KC, 3 * C], F32R)
        b_qk = sb("b_qk", [P, QK_TILES])
        b_v = sb("b_v", [P, C])
        ident = sb("ident", [P, P])
        xt_hi = [sb(f"xt_hi{i}", [P, KC, TB], F32R) for i in range(2)]
        xt_lo = [sb(f"xt_lo{i}", [P, KC, TB], F32R) for i in range(2)]
        qk_hi = [sb(f"qk_hi{i}", [P, QK_TILES, TB], F32R) for i in range(2)]
        qk_lo = [sb(f"qk_lo{i}", [P, QK_TILES, TB], F32R) for i in range(2)]
        v_f = sb("v_f", [P, 3, C])
        v_sb = sb("v_sb", [P, HEADS, TILES, VW], F32R)
        ps_t = ctx.enter_context(nc.psum_tensor("ps_t", [P, KC, 512], F32))
        ps_y = ctx.enter_context(nc.psum_tensor("ps_y", [P, 3, 512], F32))

        x_in = [sem(f"x_in{g}") for g in range(TILES // GT)]
        w_in = sem("w_in")
        b_in = sem("b_in")
        ident_ok = sem("ident_ok")
        w_scaled = sem("w_scaled")
        w_hi_ok = sem("w_hi_ok")
        w_lo_ok = sem("w_lo_ok")
        ln_step = sem("ln_step")
        root_ok = sem("root_ok")
        ln_own = sem("ln_own")
        xn_ok = sem("xn_ok")
        turned = sem("turned")
        xt_hi_ok = sem("xt_hi_ok")
        xt_lo_ok = sem("xt_lo_ok")
        y_ok = sem("y_ok")
        hi_ok = sem("hi_ok")
        lo_ok = sem("lo_ok")
        vf_ok = sem("vf_ok")
        st_out = [sem(f"st_out{i}") for i in range(2)]
        v_out = sem("v_out")
        block = ctx.enter_context(nc.Block())

        x_v = x.rearrange("(t p) c -> p t c", p=P)
        qk_hi_v = qk_hi_d.rearrange("(m p) n -> p m n", p=P)
        qk_lo_v = qk_lo_d.rearrange("(m p) n -> p m n", p=P)
        OPB = QK_TILES + TPB

        @block.sync
        def _(sp):
            for g in range(TILES // GT):
                sp.dma_start(x_sb[:, g * GT:(g + 1) * GT, :], x_v[:, g * GT:(g + 1) * GT, :]).then_inc(x_in[g], 16)
                if g == 0:
                    sp.dma_start(w_raw[:], qkv_w.rearrange("(k p) n -> p k n", p=P)).then_inc(w_in, 16)
            sp.dma_start(b_qk[:], qkv_b_t[:, 0:QK_TILES]).then_inc(b_in, 16)
            sp.dma_start(b_v[:], qkv_b[2 * C:3 * C].rearrange("(a n) -> a n", a=1).broadcast_to([P, C])).then_inc(b_in, 16)
            with sp.Fori(0, BLOCKS // 2) as i:
                for par in range(2):
                    blk = 2 * i + par
                    sp.wait_ge(hi_ok, OPB * blk + QK_TILES)
                    sp.wait_ge(lo_ok, OPB * blk + QK_TILES)
                    cols = bass.ds(blk * TB, TB)
                    sp.dma_start(qk_hi_v[:, :, cols], qk_hi[par][:].bitcast(F32)).then_inc(st_out[par], 16)
                    sp.dma_start(qk_lo_v[:, :, cols], qk_lo[par][:].bitcast(F32)).then_inc(st_out[par], 16)
            sp.wait_ge(ident_ok, 3)
            sp.wait_ge(hi_ok, OPB * BLOCKS)
            sp.wait_ge(lo_ok, OPB * BLOCKS)
            for h in range(HEADS):
                sp.dma_start(v_d[h], v_sb[:, h, :, :].bitcast(F32).rearrange("p t w -> p (t w)")).then_inc(v_out, 16)
            for par in range(2):
                sp.wait_ge(st_out[par], 32 + 16 * BLOCKS)
            sp.wait_ge(v_out, 16 * HEADS)

        @block.gpsimd
        def _(pool):
            for par in range(2):
                pool.sem_inc(st_out[par], 32)
            pool.memset(ident[:], 0.0).then_inc(ident_ok, 1)
            pool.wait_ge(ident_ok, 1)
            pool.affine_select(out=ident[:], in_=ident[:], compare_op=ALU.not_equal, fill=1.0, base=0,
                               pattern=[[-1, P]], channel_multiplier=1).then_inc(ident_ok, 1)
            pool.memset(v_sb[:, :, :, 2 * HD:VW].bitcast(F32), 1.0).then_inc(ident_ok, 1)

        @block.scalar
        def _(act):
            act.wait_ge(w_scaled, 2)
            act.copy(w_hi[:], w_raw[:]).then_inc(w_hi_ok, 1)
            for g in range(TILES // GT):
                act.wait_ge(ln_step, g + 1)
                act.activation(root[:, g * GT:(g + 1) * GT], veps[:, g * GT:(g + 1) * GT], ACT.Sqrt).then_inc(root_ok, 1)
            with act.Fori(0, BLOCKS // 2) as i:
                for par in range(2):
                    blk = 2 * i + par
                    act.wait_ge(turned, blk + 1)
                    act.copy(xt_hi[par][:], ps_t[:, :, 0:TB]).then_inc(xt_hi_ok, 1)
                    act.wait_ge(st_out[par], 32 * i + 32)
                    for m in range(QK_TILES):
                        act.wait_ge(y_ok, OPB * blk + m + 1)
                        act.activation(qk_hi[par][:, m, :], ps_y[:, m % 3, 0:TB], ACT.Identity,
                                       bias=b_qk[:, m:m + 1]).then_inc(hi_ok, 1)
                    for t in range(TPB):
                        act.wait_ge(vf_ok, TPB * blk + TPB + t + 1)
                        act.copy(v_sb[:, :, bass.ds(TPB * blk + t, 1), 0:HD],
                                 v_f[:, t, :].rearrange("p (h a d) -> p h a d", a=1, d=HD)).then_inc(hi_ok, 1)

        @block.vector
        def _(dve):
            dve.sem_inc(vf_ok, TPB)
            dve.wait_ge(w_in, 16)
            dve.wait_ge(b_in, 32)
            dve.tensor_scalar(b_qk[:, KC:QK_TILES], b_qk[:, KC:QK_TILES], SCALE, None, ALU.mult).then_inc(w_scaled, 1)
            dve.tensor_scalar(w_raw[:, :, C:2 * C], w_raw[:, :, C:2 * C], SCALE, None, ALU.mult).then_inc(w_scaled, 1)
            own = [0]

            def step(ins):
                own[0] += 1
                ins.then_inc(ln_own, 1)
                dve.wait_ge(ln_own, own[0])

            for g in range(TILES // GT):
                cut = slice(g * GT, (g + 1) * GT)
                dve.wait_ge(x_in[g], 16)
                for t in range(g * GT, (g + 1) * GT):
                    last = dve.bn_stats(stats[:, t, :], x_sb[:, t, :])
                step(last)
                for t in range(g * GT, (g + 1) * GT):
                    last = dve.bn_aggr(mv[:, t, :], stats[:, t, :])
                step(last)
                dve.tensor_scalar(veps[:, cut], mv[:, cut, 1], LN1_EPS, None, ALU.add).then_inc(ln_step, 1)
                dve.wait_ge(root_ok, g + 1)
                step(dve.reciprocal(rstd[:, cut], root[:, cut]))
                step(dve.tensor_tensor(nt[:, cut], rstd[:, cut], rstd[:, cut], ALU.mult))
                step(dve.tensor_tensor(nt[:, cut], nt[:, cut], veps[:, cut], ALU.mult))
                step(dve.tensor_scalar(nt[:, cut], nt[:, cut], -0.5, 1.5, ALU.mult, ALU.add))
                step(dve.tensor_tensor(rstd[:, cut], rstd[:, cut], nt[:, cut], ALU.mult))
                if g == 0:
                    dve.wait_ge(w_hi_ok, 1)
                    dve.tensor_tensor(w_lo[:], w_raw[:], w_hi[:].bitcast(F32), ALU.subtract).then_inc(w_lo_ok, 1)
            with dve.Fori(0, BLOCKS // 2) as i:
                for par in range(2):
                    blk = 2 * i + par
                    for t in range(TPB):
                        tile = bass.ds(TPB * blk + t, 1)
                        last = dve.tensor_scalar(xn[par][:, t, :], x_sb[:, tile, :].rearrange("p a c -> p (a c)"),
                                                 mv[:, tile, 0:1].rearrange("p a c -> p (a c)"), rstd[:, tile],
                                                 ALU.subtract, ALU.mult)
                    last.then_inc(xn_ok, 1)
                    dve.wait_ge(xt_hi_ok, blk + 1)
                    dve.tensor_tensor(xt_lo[par][:], ps_t[:, :, 0:TB], xt_hi[par][:].bitcast(F32),
                                      ALU.subtract).then_inc(xt_lo_ok, 1)
                    for m in range(QK_TILES):
                        dve.wait_ge(hi_ok, OPB * blk + m + 1)
                        dve.scalar_tensor_tensor(qk_lo[par][:, m, :], ps_y[:, m % 3, 0:TB], b_qk[:, m:m + 1],
                                                 qk_hi[par][:, m, :].bitcast(F32), ALU.add, ALU.subtract).then_inc(lo_ok, 1)
                    for t in range(TPB):
                        dve.wait_ge(y_ok, OPB * blk + QK_TILES + t + 1)
                        dve.tensor_tensor(v_f[:, t, :], ps_y[:, t, 0:TB], b_v[:], ALU.add).then_inc(vf_ok, 1)
                    for t in range(TPB):
                        dve.wait_ge(hi_ok, OPB * blk + QK_TILES + t + 1)
                        tile = bass.ds(TPB * blk + t, 1)
                        dve.tensor_tensor(v_sb[:, :, tile, HD:2 * HD],
                                          v_f[:, t, :].rearrange("p (h a d) -> p h a d", a=1, d=HD),
                                          v_sb[:, :, tile, 0:HD].bitcast(F32), ALU.subtract).then_inc(lo_ok, 1)

        @block.tensor
        def _(pe):
            pe.wait_ge(ident_ok, 2)
            pe.wait_ge(w_lo_ok, 1)
            with pe.Fori(0, BLOCKS // 2) as i:
                for par in range(2):
                    blk = 2 * i + par
                    pe.wait_ge(xn_ok, blk + 1)
                    for k in range(KC):
                        for t in range(TPB):
                            last = pe.transpose(ps_t[:, k, t * P:(t + 1) * P],
                                                xn[par][:, t, k * P:(k + 1) * P], ident[:])
                    last.then_inc(turned, 1)
                    pe.wait_ge(xt_lo_ok, blk + 1)
                    hi, lo = xt_hi[par], xt_lo[par]
                    for m in range(QK_TILES):
                        if m < 3:
                            pe.wait_ge(vf_ok, TPB * blk + m + 1)
                        else:
                            pe.wait_ge(lo_ok, OPB * blk + m - 2)
                        cut = slice(m * P, (m + 1) * P)
                        for n, (w, v) in enumerate([(w_hi, hi), (w_hi, lo), (w_lo, hi)]):
                            for k in range(KC):
                                last = pe.matmul(ps_y[:, m % 3, 0:TB], w[:, k, cut], v[:, k, :],
                                                 start=(n + k == 0), stop=(n == 2 and k == KC - 1))
                        last.then_inc(y_ok, 1)
                    for t in range(TPB):
                        pe.wait_ge(lo_ok, OPB * blk + t + 4)
                        cut = slice(t * P, (t + 1) * P)
                        for n, (v, w) in enumerate([(hi, w_hi), (hi, w_lo), (lo, w_hi)]):
                            for k in range(KC):
                                last = pe.matmul(ps_y[:, t, 0:TB], v[:, k, cut], w[:, k, 2 * C:3 * C],
                                                 start=(n + k == 0), stop=(n == 2 and k == KC - 1))
                        last.then_inc(y_ok, 1)


QB = 2 * TB
QBLOCKS = S // QB
VARIANTS = TILES // 3
VROWS = SIDE // VARIANTS
OALL_HEADS = HEADS - 2
TOP = 2 * HD + SIDE + VROWS + 1
UNITS = QBLOCKS * TILES
LEAD = 3
LOW_LEAD = 2
POOL_EVERY = 3
SHIFT = 4
RING = 4


def one_hots(pool, key_hi, key_rest, hot, done):
    made = 0
    half = SIDE // 2
    column, row, each = [[0, half], [-1, SIDE]], [[-1, half], [0, SIDE]], [[0, half], [0, SIDE]]
    row_mod = [[0, VARIANTS // 2], [-1, VROWS], [0, SIDE]]
    for keys, rows, fills in ((key_hi, P, lambda y: [(-HD, column), (-(HD + SIDE) - y, row)]),
                              (key_rest, TOP, lambda y: [(-2 * HD, column), (-(2 * HD + SIDE), row_mod), (-(TOP - 1), each)])):
        for y in (0, half):
            pool.memset(hot, 0.0).then_inc(done, 1)
            made += 1
            steps = fills(y)
            for n, (base, pattern) in enumerate(steps):
                src = hot[0:rows, :]
                dst = keys[:, y * SIDE:(y + half) * SIDE] if n == len(steps) - 1 else src

                def shaped(v):
                    return (v.rearrange("p (y x) -> p y x", x=SIDE) if len(pattern) == 2 else
                            v.rearrange("p (v y x) -> p v y x", y=VROWS, x=SIDE))
                pool.wait_ge(done, made)
                pool.affine_select(out=shaped(dst), in_=shaped(src), compare_op=ALU.not_equal, fill=1.0, base=base,
                                   pattern=pattern, channel_multiplier=1).then_inc(done, 1)
                made += 1
            pool.wait_ge(done, made)


HOT_STEPS = 14


def phase_rel(nc, rel_t, qk_hi_d, qk_lo_d, rel_hi_d, rel_lo_d, room, key_hi, key_rest):
    with ExitStack() as ctx:
        def sb(name, shape, dt=F32):
            return ctx.enter_context(nc.sbuf_tensor(name, shape, dt))

        def sem(name):
            return ctx.enter_context(nc.semaphore(name))

        K3 = 3 * HD
        NQ = HPT * SIDE
        CPB = 2
        BANKS = 8
        FILLS = 2 * SIDE // CPB
        GROUPS = HEADS // HPT
        tab_raw = sb("tab_raw", [K3, 2, REL])
        tab_hi = sb("tab_hi", [K3, 2, REL], F32R)
        tab = sb("tab", [K3, 2, REL], F32R)
        hot = sb("hot0", [P, S // 2])
        neg_lo = sb("neg_lo", [P, 1])
        q_sb = sb("q_sb", [K3, HPT, S], F32R)
        out_hi = [room[0:SIDE, :, :].bitcast(F32R), sb("out_hi", [SIDE, HPT, S], F32R)[:]]
        out_lo = [sb(f"out_lo{a}", [SIDE, HPT, S], F32R)[:] for a in range(2)]
        ps = ctx.enter_context(nc.psum_tensor("ps", [P, BANKS, 512], F32))

        tab_in = sem("tab_in")
        mask_ok = sem("mask_ok")
        hot_ok = sem("hot_ok2")
        tab_hi_ok = sem("tab_hi_ok")
        tab_ok = sem("tab_ok")
        q_in = sem("q_in")
        ps_ok = sem("ps_ok")
        r_hi = sem("r_hi")
        r_lo = sem("r_lo")
        r_out = [sem(f"r_out{a}") for a in range(2)]
        block = ctx.enter_context(nc.Block())

        @block.sync
        def _(sp):
            for r in range(3):
                sp.dma_start(tab_raw[r * HD:(r + 1) * HD, :, :], rel_t.rearrange("a d n -> d a n")).then_inc(tab_in, 16)

            def load_q(g):
                for r, src in enumerate((qk_hi_d, qk_hi_d, qk_lo_d)):
                    sp.dma_start(q_sb[r * HD:(r + 1) * HD, :, :].bitcast(F32),
                                 src[bass.ds(g * P, P), :].rearrange("(h d) n -> d h n", d=HD)).then_inc(q_in, 16)

            def group(g, last=False):
                for a in range(2):
                    half = FILLS // 2
                    if a == 1 and not last:
                        sp.wait_ge(ps_ok, FILLS * (g + 1) + 1)
                        load_q(g + 1)
                    sp.wait_ge(r_hi, FILLS * g + half * (a + 1))
                    sp.wait_ge(r_lo, BANKS + FILLS * g + half * (a + 1))
                    for o, d in ((out_hi, rel_hi_d), (out_lo, rel_lo_d)):
                        sp.dma_start(d[bass.ds(g * HPT, HPT), a * SIDE:(a + 1) * SIDE, :].rearrange("h r n -> r h n"),
                                     o[a].bitcast(F32)).then_inc(r_out[a], 16)

            load_q(0)
            with sp.Fori(0, GROUPS - 1) as g:
                group(g)
            group(GROUPS - 1, last=True)
            for a in range(2):
                sp.wait_ge(r_out[a], 32 + 32 * GROUPS)

        @block.gpsimd
        def _(pool):
            for a in range(2):
                pool.sem_inc(r_out[a], 32)
            pool.sem_inc(ps_ok, 1)
            pool.memset(neg_lo[:], 0.0).then_inc(mask_ok, 1)
            pool.wait_ge(mask_ok, 1)
            pool.memset(neg_lo[HD:2 * HD, :], -1.0).then_inc(mask_ok, 1)
            pool.wait_ge(mask_ok, 2)
            one_hots(pool, key_hi, key_rest, hot[:], hot_ok)

        @block.tensor
        def _(pe):
            pe.wait_ge(tab_ok, 1)
            with pe.Fori(0, GROUPS) as g:
                pe.wait_ge(q_in, 48 * g + 48)
                for f in range(FILLS):
                    a, bank = f // (FILLS // 2), f % BANKS
                    pe.wait_ge(r_lo, FILLS * g + f + 1)
                    for n in range(CPB):
                        c = (f * CPB + n) % SIDE
                        own = slice(c, S, SIDE) if a == 0 else slice(c * SIDE, (c + 1) * SIDE)
                        last = pe.matmul(ps[0:SIDE, bank, n * NQ:(n + 1) * NQ],
                                         tab[:, a, SIDE - 1 - c:REL - c], q_sb[:, :, own], start=True, stop=True)
                    last.then_inc(ps_ok, 1)

        def places(o, f):
            c = f * CPB % SIDE
            v = o.rearrange("r h (y x) -> r h y x", x=SIDE)
            if f < FILLS // 2:
                return v[:, :, :, c:c + CPB].rearrange("r h y c -> r c h y")
            return v[:, :, c:c + CPB, :].rearrange("r h c x -> r c h x")

        def results(bank):
            return ps[0:SIDE, bank, 0:CPB * NQ].rearrange("r (c h y) -> r c h y", c=CPB, h=HPT)

        @block.scalar
        def _(act):
            act.wait_ge(tab_in, 48)
            act.copy(tab_hi[:], tab_raw[:]).then_inc(tab_hi_ok, 1)
            with act.Fori(0, GROUPS) as g:
                for f in range(FILLS):
                    a = f // (FILLS // 2)
                    if f % (FILLS // 2) == 0:
                        act.wait_ge(r_out[a], 32 * g + 32)
                    act.wait_ge(ps_ok, FILLS * g + f + 2)
                    act.copy(places(out_hi[a], f), results(f % BANKS)).then_inc(r_hi, 1)

        @block.vector
        def _(dve):
            dve.sem_inc(r_lo, BANKS)
            dve.wait_ge(mask_ok, 2)
            dve.wait_ge(tab_hi_ok, 1)
            dve.scalar_tensor_tensor(tab[:], tab_hi[:].bitcast(F32), neg_lo[0:K3, :], tab_raw[:], ALU.mult, ALU.add).then_inc(tab_ok, 1)
            with dve.Fori(0, GROUPS) as g:
                for f in range(FILLS):
                    a = f // (FILLS // 2)
                    dve.wait_ge(r_hi, FILLS * g + f + 1)
                    dve.tensor_tensor(places(out_lo[a], f), results(f % BANKS), places(out_hi[a], f).bitcast(F32),
                                      ALU.subtract).then_inc(r_lo, 1)


def phase_attention(nc, qk_hi_d, qk_lo_d, rel_hi_d, rel_lo_d, v_d, m_d, o_d, sums_d, key_hi0, key_rest0, room):
    with ExitStack() as ctx:
        def sb(name, shape, dt=F32):
            return ctx.enter_context(nc.sbuf_tensor(name, shape, dt))

        def sem(name):
            return ctx.enter_context(nc.semaphore(name))

        query_hi = [sb(f"query_hi{i}", [P, S], F32R) for i in range(2)]
        key_hi = [key_hi0, sb("key_hi1", [P, S], F32R)]
        key_rest = [key_rest0, sb("key_rest1", [TOP, S], F32R)]
        query_rest = [sb(f"query_rest{i}", [TOP, VARIANTS, QB], F32R) for i in range(QBLOCKS)]
        val = [sb(f"val{i}", [P, TILES, VW], F32R) for i in range(2)]
        p_hi = [sb(f"p_hi{i}", [P, 2, TB], F32R) for i in range(RING)]
        p_lo = [sb(f"p_lo{i}", [P, 2, TB], F32R) for i in range(RING)]
        p_f = [sb(f"p_f{i}", [P, 2, TB]) for i in range(2)]
        ident = sb("ident2", [P, P])
        o_all = room[:, 0:KC, :]
        hot = room[:, KC, 0:S // 2]
        mx = [sb(f"mx{i}", [P, 6, 6]) for i in range(QBLOCKS)]
        neg_m = [sb(f"neg_m{i}", [P, 6]) for i in range(QBLOCKS)]
        neg_mt = [sb(f"neg_mt{i}", [6, P], F32R) for i in range(QBLOCKS)]
        o_t = [sb(f"o_t{i}", [VW, 2, TB]) for i in range(2)]
        o_low = [sb(f"o_low{i}", [HD, 2, TB]) for i in range(2)]
        o_s = [sb(f"o_s{i}", [HD, 2, TB]) for i in range(2)]
        ps_s = ctx.enter_context(nc.psum_tensor("ps_s", [P, 4, 512], F32))
        ps_m = ctx.enter_context(nc.psum_tensor("ps_m", [P, 2, 512], F32))
        ps_o = ctx.enter_context(nc.psum_tensor("ps_o", [P, 2, 512], F32))

        ident_ok = sem("ident_ok")
        hi_in = [sem(f"hi_in{i}") for i in range(2)]
        kv_in = [sem(f"kv_in{i}") for i in range(2)]
        rest_in = [sem(f"rest_in{i}") for i in range(QBLOCKS)]
        m_out = sem("m_out")
        hot_ok = sem("hot_ok")
        s_ok = sem("s_ok")
        hi_ok = sem("p_hi_ok")
        f_ok = sem("f_ok")
        lo_dve = sem("p_lo_dve")
        lo_pool = sem("p_lo_pool")
        pv_ok = sem("pv_ok")
        mm_ok = sem("mm_ok")
        mx_ok = sem("mx_ok")
        neg_ok = sem("neg_ok")
        turned = sem("turned2")
        negt_ok = sem("negt_ok")
        acc_a = sem("acc_a")
        acc_d = sem("acc_d")
        o_go = sem("o_go")
        low_moved = sem("low_moved")
        o_sum = sem("o_sum")
        ot_out = [sem(f"ot_out{i}") for i in range(2)]
        all_in = sem("all_in")
        block = ctx.enter_context(nc.Block())

        loop_heads = OALL_HEADS

        def chunk_at(h, par, k):
            return (par, UNITS - SHIFT + k) if k < SHIFT else (1 - par, k - SHIFT)

        def unit_at(par, k, lead=LEAD):
            return (par, k + lead) if k + lead < UNITS else (1 - par, k + lead - UNITS)

        def lo_done(h, idx):
            if idx % POOL_EVERY == POOL_EVERY - 1:
                return lo_pool, UNITS // POOL_EVERY * h + idx // POOL_EVERY + 1
            return lo_dve, (UNITS - UNITS // POOL_EVERY) * h + idx - idx // POOL_EVERY + 1

        def low(engine, n, par, idx):
            r = (2 * par + idx) % RING
            engine.wait_ge(f_ok, n + 3)
            engine.tensor_tensor(p_lo[r][:], p_f[idx % 2][:], p_hi[r][:].bitcast(F32),
                                 ALU.subtract).then_inc(lo_done(0, idx)[0], 1)

        turn_at = {TILES + SHIFT + 2: 0, 2 * TILES + SHIFT + 2: 1, SHIFT + 2: 2}

        def turned_at(k, last):
            b = turn_at.get(k)
            return None if b is None or (last and b < 2) else b

        @block.sync
        def _(sp):
            def load_hi(h, par):
                rows = bass.ds(h * HD, HD)
                krows = bass.ds(C + h * HD, HD)
                sp.dma_start(key_hi[par][0:HD, :].bitcast(F32), qk_hi_d[krows, :]).then_inc(hi_in[par], 16)
                sp.dma_start(query_hi[par][0:HD, :].bitcast(F32), qk_hi_d[rows, :]).then_inc(hi_in[par], 16)
                sp.dma_start(query_hi[par][HD:P, :].bitcast(F32), rel_hi_d[bass.ds(h, 1), :, :].rearrange("a r n -> (a r) n")).then_inc(hi_in[par], 16)

            def load_kv(h, par):
                krows = bass.ds(C + h * HD, HD)
                sp.dma_start(key_rest[par][0:HD, :].bitcast(F32), qk_hi_d[krows, :]).then_inc(kv_in[par], 16)
                sp.dma_start(key_rest[par][HD:2 * HD, :].bitcast(F32), qk_lo_d[krows, :]).then_inc(kv_in[par], 16)
                sp.dma_start(val[par][:].bitcast(F32).rearrange("p t w -> p (t w)"), v_d[bass.ds(h, 1), :, :].rearrange("a p n -> (a p) n")).then_inc(kv_in[par], 16)

            def load_rest(h, b):
                rows = bass.ds(h * HD, HD)
                dst = query_rest[b]
                cols = slice(b * QB, (b + 1) * QB)

                def shared(src):
                    return src.rearrange("r (a n) -> r a n", a=1).broadcast_to([src.shape[0], VARIANTS, QB])
                rel = rel_lo_d[bass.ds(h, 1), :, cols].rearrange("a r n -> (a r) n")
                sp.dma_start(dst[0:HD, :, :].bitcast(F32), shared(qk_lo_d[rows, cols])).then_inc(rest_in[b], 16)
                sp.dma_start(dst[HD:2 * HD, :, :].bitcast(F32), shared(qk_hi_d[rows, cols])).then_inc(rest_in[b], 16)
                sp.dma_start(dst[2 * HD:2 * HD + SIDE, :, :].bitcast(F32), shared(rel[0:SIDE, :])).then_inc(rest_in[b], 16)
                sp.dma_start(dst[2 * HD + SIDE:TOP - 1, :, :].bitcast(F32),
                             rel[SIDE:2 * SIDE, :].rearrange("(v r) n -> r v n", r=VROWS)).then_inc(rest_in[b], 16)

            def load_max(h, b):
                row = m_d[bass.ds(h, 1), b * QB:(b + 1) * QB]
                sp.wait_ge(negt_ok, QBLOCKS * h + b + 1)
                sp.dma_start(row.rearrange("a (t p) -> (a t) p", p=P), neg_mt[b][:].bitcast(F32)).then_inc(m_out, 16)
                sp.wait_ge(m_out, 16 * (QBLOCKS * h + b + 1))
                sp.dma_start(query_rest[b][TOP - 1:TOP, :, :].bitcast(F32),
                             row.rearrange("r (a n) -> r a n", a=1).broadcast_to([1, VARIANTS, QB])).then_inc(rest_in[b], 16)

            def store(h, par, b):
                g = (QBLOCKS * par + b) % 2
                sp.wait_ge(o_sum, QBLOCKS * h + b + 1)
                sp.dma_start(o_d[bass.ds(h * HD, HD), b * QB:(b + 1) * QB], o_s[g][:].rearrange("r c n -> r (c n)")).then_inc(ot_out[g], 16)
                sp.dma_start(sums_d[bass.ds(h, 1), b * QB:(b + 1) * QB],
                             o_t[g][VW - 1:VW, :, :].rearrange("r c n -> r (c n)")).then_inc(ot_out[g], 16)

            def start(h, par, last=False):
                if not last:
                    sp.wait_ge(s_ok, UNITS * h + LEAD)
                    load_hi(h + 1, 1 - par)
                load_max(h, 2)

            def rest(h, par):
                sp.wait_ge(pv_ok, UNITS * h + RING)
                load_kv(h + 1, 1 - par)
                for b in range(QBLOCKS):
                    sp.wait_ge(s_ok, UNITS * h + TILES * (b + 1))
                    load_rest(h + 1, b)
                    if b < 2:
                        load_max(h + 1, b)
                        store(h, par, b)
                start(h + 1, 1 - par, isinstance(h, int) and h == HEADS - 2)
                store(h, par, 2)

            load_hi(0, 0)
            load_kv(0, 0)
            for b in range(QBLOCKS):
                load_rest(0, b)
            for b in range(2):
                load_max(0, b)
            sp.wait_ge(hot_ok, HOT_STEPS)
            start(0, 0)
            with sp.Fori(0, loop_heads // 2) as i:
                for par in range(2):
                    rest(2 * i + par, par)
            rest(HEADS - 2, 0)
            for g in range(2):
                sp.wait_ge(ot_out[g], 32 + 32 * QBLOCKS * OALL_HEADS // 2)
            for c in range(KC):
                rows = min(P, OALL_HEADS * HD - c * P)
                sp.dma_start(o_all[0:rows, c, :], o_d[c * P:c * P + rows, :]).then_inc(all_in, 16)
            for b in range(QBLOCKS):
                store(HEADS - 1, 1, b)
            for g in range(2):
                sp.wait_ge(ot_out[g], 32 + 32 * QBLOCKS * HEADS // 2)
            sp.wait_ge(all_in, 16 * KC)

        @block.gpsimd
        def _(pool):
            for g in range(2):
                pool.sem_inc(ot_out[g], 32)
            pool.memset(ident[:], 0.0).then_inc(ident_ok, 1)
            pool.wait_ge(ident_ok, 1)
            pool.affine_select(out=ident[:], in_=ident[:], compare_op=ALU.not_equal, fill=1.0, base=0,
                               pattern=[[-1, P]], channel_multiplier=1).then_inc(ident_ok, 1)
            one_hots(pool, key_hi[1], key_rest[1], hot, hot_ok)

            def joined(h, par, b, last_one):
                g = (QBLOCKS * par + b) % 2
                pool.wait_ge(acc_a, QBLOCKS * h + b + 2)
                pool.wait_ge(acc_d, QBLOCKS * h + b + 2)
                pool.wait_ge(*lo_done(h + (b == QBLOCKS - 1), (TILES * (b + 1) + 2 * POOL_EVERY - 1) % UNITS) if not last_one else lo_done(h, UNITS - 1))
                pool.sem_inc(o_go, 1)
                pool.tensor_copy(o_low[g][:], o_t[g][HD:2 * HD, :, :]).then_inc(low_moved, 1)
                pool.wait_ge(low_moved, QBLOCKS * h + b + 1)
                pool.tensor_tensor(o_s[g][:], o_t[g][0:HD, :, :], o_low[g][:], ALU.add).then_inc(o_sum, 1)

            FIRST = 3 * POOL_EVERY

            def head(h, par, last=False):
                for idx in range(FIRST - 1, UNITS + FIRST - 1, POOL_EVERY):
                    if idx < UNITS:
                        low(pool, UNITS * h + idx, par, idx)
                    elif not last:
                        low(pool, UNITS * h + idx, 1 - par, idx - UNITS)
                    for b in range(QBLOCKS):
                        if idx == TILES * (b + 1) + 2 * POOL_EVERY - 1:
                            joined(h, par, b, last and b == QBLOCKS - 1)

            for idx in range(POOL_EVERY - 1, FIRST - 1, POOL_EVERY):
                low(pool, idx, 0, idx)
            with pool.Fori(0, loop_heads // 2) as h0:
                for par in range(2):
                    head(2 * h0 + par, par)
            head(HEADS - 2, 0)
            head(HEADS - 1, 1, last=True)

        @block.tensor
        def _(pe):
            def half(tp, s, c, ps):
                tile = slice(s // 3 * P, (s // 3 + 1) * P)
                keys = slice(s % 3 * QB + c * TB, s % 3 * QB + (c + 1) * TB)
                pe.matmul(ps[:, c, 0:TB], query_hi[tp][:, tile], key_hi[tp][:, keys], start=True, stop=True).then_inc(mm_ok, 1)

            def scores(n, par, idx, turn=None):
                b, j = idx // TILES, idx % TILES
                bank = 2 * (idx % 2)
                pe.wait_ge(f_ok, n + 1)
                if turn is not None:
                    pe.transpose(ps_s[0:6, bank, TB:TB + P], neg_m[turn][:], ident[:])
                for c in range(2):
                    pe.matmul(ps_s[:, bank + c, 0:TB], key_hi[par][:, j * P:(j + 1) * P],
                              query_hi[par][:, b * QB + c * TB:b * QB + (c + 1) * TB], start=True, stop=False)
                for c in range(2):
                    last = pe.matmul(ps_s[:, bank + c, 0:TB], key_rest[par][:, j * P:(j + 1) * P],
                                     query_rest[b][:, j // 3, c * TB:(c + 1) * TB], start=False, stop=True)
                last.then_inc(s_ok, 1)

            def pv(h, par, idx):
                j, r = idx % TILES, (2 * par + idx) % RING
                pe.wait_ge(*lo_done(h, idx))
                for part in (p_hi, p_lo):
                    for c in range(2):
                        last = pe.matmul(ps_o[0:VW, c, 0:TB], val[par][:, j, :], part[r][:, c, :],
                                         start=(j == 0 and part is p_hi), stop=(j == TILES - 1 and part is p_lo))
                last.then_inc(pv_ok, 1)

            def head(h, par, last=False):
                for k in range(UNITS):
                    up, idx = unit_at(par, k)
                    if not (last and up != par):
                        turn = turned_at(k, last)
                        if idx == 0:
                            pe.wait_ge(kv_in[up], 48 * ((h + 1) // 2 + 1) if isinstance(h, int) else 48 * (h0 + 1 + par))
                        if idx % TILES == 0:
                            pe.wait_ge(rest_in[idx // TILES], 80 * (h + 1 + (up != par)))
                        if turn is not None:
                            pe.wait_ge(neg_ok, QBLOCKS * (h + (turn < 2)) + turn + 1)
                        scores(UNITS * h + k + LEAD, up, idx, turn)
                    tp, s = chunk_at(h, par, k)
                    maxima = not (last and tp != par)
                    number = 2 * (UNITS * (h + 1) + k - SHIFT)
                    if maxima:
                        if s == 0:
                            pe.wait_ge(hi_in[tp], 48 * ((h + 1) // 2 + 1) if isinstance(h, int) else 48 * (h0 + 1 + par))
                        pe.wait_ge(mx_ok, number - 1)
                        half(tp, s, 0, ps_m)
                    if k % TILES == 0:
                        pe.wait_ge(acc_a, QBLOCKS * h + k // TILES + 1)
                        pe.wait_ge(acc_d, QBLOCKS * h + k // TILES + 1)
                    pv(h, par, k)
                    if maxima:
                        pe.wait_ge(mx_ok, number)
                        half(tp, s, 1, ps_m)

            pe.wait_ge(hi_in[0], 48)
            spare = [ps_m, ps_s[:, 0:2, :], ps_s[:, 2:4, :]]
            for s in range(UNITS - SHIFT):
                if s >= 3:
                    pe.wait_ge(mx_ok, 2 * (s - 2))
                for c in range(2):
                    half(0, s, c, spare[s % 3])
                for b in range(2):
                    if s == TILES * (b + 1) + 3:
                        if b == 0:
                            pe.wait_ge(ident_ok, 2)
                        pe.wait_ge(neg_ok, b + 1)
                        pe.transpose(ps_o[0:6, b, 0:P], neg_m[b][:], ident[:]).then_inc(turned, 1)
            pe.wait_ge(mx_ok, 2 * (UNITS - SHIFT))
            pe.wait_ge(kv_in[0], 48)
            pe.wait_ge(rest_in[0], 80)
            for idx in range(LEAD):
                scores(idx, 0, idx)
            pe.wait_ge(negt_ok, 2)
            with pe.Fori(0, loop_heads // 2) as h0:
                for par in range(2):
                    head(2 * h0 + par, par)
            head(HEADS - 2, 0)
            head(HEADS - 1, 1, last=True)

        @block.scalar
        def _(act):
            def exps(h, par, idx, turn=None):
                n = UNITS * h + idx
                bank, r = 2 * (idx % 2), (2 * par + idx) % RING
                act.wait_ge(s_ok, n + 1)
                act.wait_ge(pv_ok, n + 1)
                act.activation(p_hi[r][:], ps_s[:, bank:bank + 2, 0:TB], ACT.Exp).then_inc(hi_ok, 1)
                if turn is not None:
                    act.copy(neg_mt[turn][:], ps_s[0:6, bank, TB:TB + P]).then_inc(negt_ok, 1)
                if not (isinstance(h, int) and UNITS * h + idx < 2):
                    act.wait_ge(*(lo_done(h, idx - 2) if idx >= 2 else lo_done(h - 1, idx - 2 + UNITS)))
                act.activation(p_f[idx % 2][:], ps_s[:, bank:bank + 2, 0:TB], ACT.Exp).then_inc(f_ok, 1)

            def head(h, par, last=False):
                for k in range(UNITS):
                    up, idx = unit_at(par, k)
                    if not (last and up != par):
                        exps(h + (up != par), up, idx, turned_at(k, last))
                    if k % TILES == TILES - 1:
                        b = k // TILES
                        g = (QBLOCKS * par + b) % 2
                        act.wait_ge(pv_ok, UNITS * h + k + 1 + RING)
                        act.wait_ge(ot_out[g], out_count(h, par, b))
                        act.copy(o_t[g][:, 0, :], ps_o[0:VW, 0, 0:TB]).then_inc(acc_a, 1)

            def out_count(h, par, b):
                return 32 * ((QBLOCKS * par + b) // 2) + 32 * QBLOCKS * half(h, par) + 32

            def half(h, par):
                return (h - par) // 2 if isinstance(h, int) else h0

            act.sem_inc(acc_a, 1)
            act.sem_inc(f_ok, 2)
            for b in range(2):
                act.wait_ge(turned, b + 1)
                act.copy(neg_mt[b][:], ps_o[0:6, b, 0:P]).then_inc(negt_ok, 1)
            for idx in range(LEAD):
                exps(0, 0, idx)
            with act.Fori(0, loop_heads // 2) as h0:
                for par in range(2):
                    head(2 * h0 + par, par)
            head(HEADS - 2, 0)
            head(HEADS - 1, 1, last=True)

        @block.vector
        def _(dve):
            def negated(count, s):
                if s % TILES == TILES - 1:
                    dve.wait_ge(mx_ok, 2 * count + 2)
                    dve.tensor_reduce(neg_m[s // TILES][:], mx[s // TILES][:], AX.X, ALU.max, negate=True).then_inc(neg_ok, 1)

            def reduce_half(count, s, c):
                dve.wait_ge(mm_ok, 2 * count + c + 1)
                col = s % 3 * 2 + c
                dve.tensor_reduce(mx[s // TILES][:, s // 3 % 6, col:col + 1], ps_m[:, c, 0:TB], AX.X, ALU.max).then_inc(mx_ok, 1)

            def reduce_both(s, ps):
                dve.wait_ge(mm_ok, 2 * s + 2)
                col = s % 3 * 2
                dve.tensor_reduce(mx[s // TILES][:, s // 3 % 6, col:col + 2], ps[:, :, 0:TB], AX.X, ALU.max).then_inc(mx_ok, 2)
                negated(s, s)

            def head(h, par, last=False):
                for k in range(UNITS):
                    tp, s = chunk_at(h, par, k)
                    maxima = not (last and tp != par)
                    number = UNITS * (h + 1) + k - SHIFT
                    if maxima:
                        reduce_half(number, s, 0)
                    up, idx = unit_at(par, k, LOW_LEAD)
                    if not (last and up != par) and idx % POOL_EVERY < POOL_EVERY - 1:
                        low(dve, UNITS * h + k + LOW_LEAD, up, idx)
                    if maxima:
                        reduce_half(number, s, 1)
                        negated(number, s)
                    if k % TILES == TILES - 1:
                        b = k // TILES
                        g = (QBLOCKS * par + b) % 2
                        dve.wait_ge(pv_ok, UNITS * h + k + 1 + RING)
                        dve.wait_ge(ot_out[g], out_count(h, par, b))
                        dve.tensor_copy(o_t[g][:, 1, :], ps_o[0:VW, 1, 0:TB]).then_inc(acc_d, 1)

            def out_count(h, par, b):
                return 32 * ((QBLOCKS * par + b) // 2) + 32 * QBLOCKS * half(h, par) + 32

            def half(h, par):
                return (h - par) // 2 if isinstance(h, int) else h0

            dve.sem_inc(acc_d, 1)
            dve.sem_inc(pv_ok, RING)
            for s in range(UNITS - SHIFT):
                reduce_both(s, [ps_m, ps_s[:, 0:2, :], ps_s[:, 2:4, :]][s % 3])
            for idx in range(LOW_LEAD):
                if idx % POOL_EVERY < POOL_EVERY - 1:
                    low(dve, idx, 0, idx)
            with dve.Fori(0, loop_heads // 2) as h0:
                for par in range(2):
                    head(2 * h0 + par, par)
            head(HEADS - 2, 0)
            head(HEADS - 1, 1, last=True)


EXPERTS = 8
TOP_K = 2
FF = 4 * C
QUARTERS = 4
FQ = FF // QUARTERS
FC = FQ // P


def phase_proj(nc, x, o_d, sums_d, rec_d, proj_w, proj_b, o_all, x1):
    with ExitStack() as ctx:
        def sb(name, shape, dt=F32):
            return ctx.enter_context(nc.sbuf_tensor(name, shape, dt))

        def sem(name):
            return ctx.enter_context(nc.semaphore(name))

        FLAT = HEADS * S // P
        rflat = sb("rflat", [P, FLAT])
        rsum = sb("rsum", [HEADS, S])
        spread = sb("spread", [HEADS, KC, P])
        o_f = [sb(f"o_f{i}", [P, KC, TB]) for i in range(2)]
        o_hi = [sb(f"o_hi{i}", [P, KC, TB], F32R) for i in range(2)]
        o_lo = [sb(f"o_lo{i}", [P, KC, TB], F32R) for i in range(2)]
        w_raw = sb("pw_raw", [P, KC, C])
        w_hi = sb("pw_hi", [P, KC, C], F32R)
        w_lo = sb("pw_lo", [P, KC, C], F32R)
        p_b = sb("p_b", [P, C])
        ps_r = ctx.enter_context(nc.psum_tensor("ps_r", [P, KC, 512], F32))
        ps_y = ctx.enter_context(nc.psum_tensor("ps_y2", [P, TPB, 512], F32))

        s_in = sem("sums_in")
        rec_out = sem("rec_out")
        rec_in = sem("rec_in")
        o_in = sem("o_in")
        x_in = sem("x_in2")
        w_in = sem("w_in2")
        spread_made = sem("spread_made")
        w_hi_ok = sem("w_hi_ok2")
        w_lo_ok = sem("w_lo_ok2")
        x_ok = sem("x_ok")
        r_ok = sem("r_ok")
        spread_ok = sem("spread_ok")
        of_ok = sem("of_ok")
        ohi_ok = sem("ohi_ok")
        olo_ok = sem("olo_ok")
        y_ok = sem("y_ok2")
        x1_ok = sem("x1_ok")
        block = ctx.enter_context(nc.Block())

        @block.sync
        def _(sp):
            sp.dma_start(rflat[:], sums_d.rearrange("h n -> (h n)").rearrange("(p n) -> p n", p=P)).then_inc(s_in, 16)
            rows = OALL_HEADS * HD - (KC - 1) * P
            sp.dma_start(o_all[rows:P, KC - 1, :], o_d[OALL_HEADS * HD:C, :]).then_inc(o_in, 16)
            sp.wait_ge(r_ok, 1)
            sp.dma_start(rec_d.rearrange("h n -> (h n)").rearrange("(p n) -> p n", p=P), rflat[:]).then_inc(rec_out, 16)
            sp.wait_ge(rec_out, 16)
            sp.dma_start(rsum[:], rec_d).then_inc(rec_in, 16)
            sp.wait_ge(rec_in, 16)

        @block.gpsimd
        def _(pool):
            pool.memset(spread[:], 1.0).then_inc(spread_made, 1)
            flat = spread[:].rearrange("h c r -> h (c r)")
            pool.wait_ge(spread_made, 1)
            pool.affine_select(out=flat, in_=flat, compare_op=ALU.is_ge, fill=0.0, base=0,
                               pattern=[[1, KC * P]], channel_multiplier=-HD).then_inc(spread_made, 1)
            pool.wait_ge(spread_made, 2)
            pool.affine_select(out=flat, in_=flat, compare_op=ALU.is_ge, fill=0.0, base=HD - 1,
                               pattern=[[-1, KC * P]], channel_multiplier=HD).then_inc(spread_made, 1)
            pool.wait_ge(w_in, 32)
            pool.wait_ge(x_in, 16)
            bias = p_b[:].rearrange("p (a n) -> p a n", a=1).broadcast_to([P, TPB, C])
            with pool.Fori(0, BLOCKS) as b:
                rows = x1[:, bass.ds(b * TPB, TPB), :]
                pool.tensor_tensor(rows, rows, bias, ALU.add).then_inc(x_ok, 1)

        @block.tensor
        def _(pe):
            def spread_block(blk):
                pe.wait_ge(of_ok, blk + 1)
                for c in range(KC):
                    last = pe.matmul(ps_r[:, c, 0:TB], spread[:, c, :], rsum[:, bass.ds(blk * TB, TB)],
                                     start=True, stop=True)
                last.then_inc(spread_ok, 1)

            def product(blk, par):
                pe.wait_ge(olo_ok, blk + 1)
                for t in range(TPB):
                    pe.wait_ge(x1_ok, TPB * blk + t + 1)
                    cut = slice(t * P, (t + 1) * P)
                    for n, (v, w) in enumerate([(o_hi, w_hi), (o_hi, w_lo), (o_lo, w_hi)]):
                        for k in range(KC):
                            last = pe.matmul(ps_y[:, t, 0:C], v[par][:, k, cut], w[:, k, :],
                                             start=(n + k == 0), stop=(n == 2 and k == KC - 1))
                    last.then_inc(y_ok, 1)

            pe.wait_ge(spread_made, 3)
            pe.wait_ge(rec_in, 16)
            pe.wait_ge(w_lo_ok, 1)
            spread_block(0)
            with pe.Fori(0, BLOCKS // 2 - 1) as i:
                for par in range(2):
                    spread_block(2 * i + par + 1)
                    product(2 * i + par, par)
            spread_block(BLOCKS - 1)
            product(BLOCKS - 2, 0)
            product(BLOCKS - 1, 1)

        @block.scalar
        def _(act):
            act.dma_start(w_raw[:], proj_w.rearrange("(k p) n -> p k n", p=P)).then_inc(w_in, 16)
            act.dma_start(p_b[:], proj_b.rearrange("(a n) -> a n", a=1).broadcast_to([P, C])).then_inc(w_in, 16)
            act.dma_start(x1[:], x.rearrange("(t p) c -> p t c", p=P)).then_inc(x_in, 16)
            act.wait_ge(w_in, 32)
            act.copy(w_hi[:], w_raw[:]).then_inc(w_hi_ok, 1)
            with act.Fori(0, BLOCKS // 2) as i:
                for par in range(2):
                    blk = 2 * i + par
                    act.wait_ge(of_ok, blk + 2)
                    act.copy(o_hi[par][:], o_f[par][:]).then_inc(ohi_ok, 1)

        @block.vector
        def _(dve):
            def normalised(blk, par):
                dve.wait_ge(spread_ok, blk + 1)
                dve.tensor_tensor(o_f[par][:], ps_r[:, :, 0:TB], o_all[:, :, bass.ds(blk * TB, TB)], ALU.mult).then_inc(of_ok, 1)
                dve.wait_ge(ohi_ok, blk + 1)
                dve.tensor_tensor(o_lo[par][:], o_f[par][:], o_hi[par][:].bitcast(F32), ALU.subtract).then_inc(olo_ok, 1)

            def added(blk):
                dve.wait_ge(x_ok, blk + 1)
                for t in range(TPB):
                    dve.wait_ge(y_ok, TPB * blk + t + 1)
                    row = x1[:, bass.ds(TPB * blk + t, 1), :].rearrange("p a c -> p (a c)")
                    dve.tensor_tensor(row, ps_y[:, t, 0:C], row, ALU.add).then_inc(x1_ok, 1)

            dve.sem_inc(x1_ok, TPB)
            dve.sem_inc(of_ok, 1)
            dve.wait_ge(s_in, 16)
            dve.reciprocal(rflat[:], rflat[:]).then_inc(r_ok, 1)
            dve.wait_ge(w_hi_ok, 1)
            dve.tensor_tensor(w_lo[:], w_raw[:], w_hi[:].bitcast(F32), ALU.subtract).then_inc(w_lo_ok, 1)
            dve.wait_ge(o_in, 16)
            normalised(0, 0)
            with dve.Fori(0, BLOCKS // 2 - 1) as i:
                for par in range(2):
                    normalised(2 * i + par + 1, 1 - par)
                    added(2 * i + par)
            normalised(BLOCKS - 1, 1)
            added(BLOCKS - 2)
            added(BLOCKS - 1)


def phase_gates(nc, gate_w, gate_b, x1, xt_hi, xt_lo, comb, experts):
    with ExitStack() as ctx:
        def sb(name, shape, dt=F32):
            return ctx.enter_context(nc.sbuf_tensor(name, shape, dt))

        def sem(name):
            return ctx.enter_context(nc.semaphore(name))

        g_raw = sb("g_raw", [P, KC, EXPERTS])
        g_hi = sb("g_hi", [P, KC, EXPERTS], F32R)
        g_lo = sb("g_lo", [P, KC, EXPERTS], F32R)
        g_b = sb("g_b", [EXPERTS, 1])
        ident = sb("ident3", [P, P])
        stats = sb("stats2", [P, TILES, 6])
        mv = sb("mv2", [P, TILES, 2])
        veps = sb("veps2", [P, TILES])
        root = sb("root2", [P, TILES])
        rstd = sb("rstd2", [P, TILES])
        nt = sb("nt2", [P, TILES])
        xn = [sb(f"xnn{i}", [P, TPB, C]) for i in range(2)]
        logit_t = sb("logit_t", [EXPERTS, S])
        gate = sb("gate", [P, TILES, EXPERTS])
        gate_e = sb("gate_e", [P, TILES, EXPERTS])
        beats = sb("beats", [P, EXPERTS, TILES, EXPERTS])
        rank = sb("rank", [P, TILES, EXPERTS])
        top = sb("top", [P, TILES])
        ps_t = [ctx.enter_context(nc.psum_tensor(f"ps_t{i}", [P, KC, 512], F32)) for i in range(2)]
        ps_g = ctx.enter_context(nc.psum_tensor("ps_g", [P, 2, 512], F32))

        w_in = sem("g_in")
        const_ok = sem("const_ok")
        w_hi_ok = sem("gw_hi_ok")
        w_lo_ok = sem("gw_lo_ok")
        own = sem("own2")
        root_in = sem("root_in")
        root_ok = sem("root_ok2")
        xn_ok = sem("xn_ok2")
        t_ok = sem("t_ok")
        thi_ok = sem("thi_ok")
        tlo_ok = sem("tlo_ok")
        l_ok = sem("l_ok")
        lt_ok = sem("lt_ok")
        g_ok = sem("g_ok")
        e_in = sem("e_in")
        e_ok = sem("e_ok")
        block = ctx.enter_context(nc.Block())

        @block.sync
        def _(sp):
            experts.load_biases(sp)
            for u in range(2):
                experts.load_unit(sp, u, u)
            sp.wait_ge(experts.b_in, 32)

        @block.gpsimd
        def _(pool):
            pool.memset(ident[:], 0.0).then_inc(const_ok, 1)
            pool.wait_ge(const_ok, 1)
            pool.affine_select(out=ident[:], in_=ident[:], compare_op=ALU.not_equal, fill=1.0, base=0,
                               pattern=[[-1, P]], channel_multiplier=1).then_inc(const_ok, 1)
            for u in range(2):
                pool.wait_ge(experts.raw_in[u], 32)
                pool.sem_inc(experts.split_go, 1)
                experts.split_unit(pool, u, u)

        @block.tensor
        def _(pe):
            def transposed(par):
                for k in range(KC):
                    for t in range(TPB):
                        last = pe.transpose(ps_t[par][:, k, t * P:(t + 1) * P], xn[par][:, t, k * P:(k + 1) * P], ident[:])
                last.then_inc(t_ok, 1)

            pe.wait_ge(const_ok, 2)
            pe.wait_ge(w_lo_ok, 1)
            with pe.Fori(0, BLOCKS // 2) as i:
                for par in range(2):
                    pe.wait_ge(xn_ok, 2 * i + par + 1)
                    transposed(par)
                for par in range(2):
                    blk = 2 * i + par
                    pe.wait_ge(tlo_ok, blk + 1)
                    pe.wait_ge(lt_ok, blk + 1)
                    cols = bass.ds(blk * TB, TB)
                    for n, (w, v) in enumerate([(g_hi, xt_hi), (g_lo, xt_hi), (g_hi, xt_lo)]):
                        for k in range(KC):
                            last = pe.matmul(ps_g[0:EXPERTS, par, 0:TB], w[:, k, :], v[:, k, cols],
                                             start=(n + k == 0), stop=(n == 2 and k == KC - 1))
                    last.then_inc(l_ok, 1)
            pe.wait_ge(lt_ok, BLOCKS + 2)
            for t in range(TILES):
                last = pe.transpose(ps_g[:, 0, t * EXPERTS:(t + 1) * EXPERTS], logit_t[:, t * P:(t + 1) * P],
                                    ident[0:EXPERTS, 0:EXPERTS])
            last.then_inc(g_ok, 1)

        @block.scalar
        def _(act):
            act.dma_start(g_raw[:], gate_w.rearrange("(k p) n -> p k n", p=P)).then_inc(w_in, 16)
            act.dma_start(g_b[:], gate_b.rearrange("(n a) -> n a", a=1)).then_inc(w_in, 16)
            act.wait_ge(w_in, 32)
            act.copy(g_hi[:], g_raw[:]).then_inc(w_hi_ok, 1)
            act.wait_ge(root_in, 1)
            act.activation(root[:], veps[:], ACT.Sqrt).then_inc(root_ok, 1)
            with act.Fori(0, BLOCKS // 2) as i:
                for par in range(2):
                    act.wait_ge(t_ok, 2 * i + par + 1)
                    act.copy(xt_hi[:, :, bass.ds((2 * i + par) * TB, TB)], ps_t[par][:, :, 0:TB]).then_inc(thi_ok, 1)
                for par in range(2):
                    act.wait_ge(l_ok, 2 * i + par + 1)
                    act.activation(logit_t[:, bass.ds((2 * i + par) * TB, TB)], ps_g[0:EXPERTS, par, 0:TB], ACT.Identity,
                                   bias=g_b[:]).then_inc(lt_ok, 1)
            act.wait_ge(e_in, 1)
            act.activation(gate_e[:], gate[:], ACT.Exp).then_inc(e_ok, 1)

        @block.vector
        def _(dve):
            n_own = [0]

            def step(ins):
                n_own[0] += 1
                ins.then_inc(own, 1)
                dve.wait_ge(own, n_own[0])

            dve.sem_inc(lt_ok, 2)
            with dve.Fori(0, TILES) as t:
                dve.bn_stats(stats[:, bass.ds(t, 1), :].rearrange("p a c -> p (a c)"),
                             x1[:, bass.ds(t, 1), :].rearrange("p a c -> p (a c)")).then_inc(own, 1)
            n_own[0] += TILES
            dve.wait_ge(own, n_own[0])
            for t in range(TILES):
                last = dve.bn_aggr(mv[:, t, :], stats[:, t, :])
            step(last)
            dve.tensor_scalar(veps[:], mv[:, :, 1], LN2_EPS, None, ALU.add).then_inc(root_in, 1)
            dve.wait_ge(w_hi_ok, 1)
            dve.tensor_tensor(g_lo[:], g_raw[:], g_hi[:].bitcast(F32), ALU.subtract).then_inc(w_lo_ok, 1)
            dve.wait_ge(root_ok, 1)
            step(dve.reciprocal(rstd[:], root[:]))
            step(dve.tensor_tensor(nt[:], rstd[:], rstd[:], ALU.mult))
            step(dve.tensor_tensor(nt[:], nt[:], veps[:], ALU.mult))
            step(dve.tensor_scalar(nt[:], nt[:], -0.5, 1.5, ALU.mult, ALU.add))
            step(dve.tensor_tensor(rstd[:], rstd[:], nt[:], ALU.mult))
            with dve.Fori(0, BLOCKS // 2) as i:
                for par in range(2):
                    blk = 2 * i + par
                    for t in range(TPB):
                        tile = bass.ds(TPB * blk + t, 1)
                        last = dve.tensor_scalar(xn[par][:, t, :], x1[:, tile, :].rearrange("p a c -> p (a c)"),
                                                 mv[:, tile, 0:1].rearrange("p a c -> p (a c)"), rstd[:, tile],
                                                 ALU.subtract, ALU.mult)
                    last.then_inc(xn_ok, 1)
                for par in range(2):
                    blk = 2 * i + par
                    cols = bass.ds(blk * TB, TB)
                    dve.wait_ge(thi_ok, blk + 1)
                    dve.tensor_tensor(xt_lo[:, :, cols], ps_t[par][:, :, 0:TB], xt_hi[:, :, cols].bitcast(F32),
                                      ALU.subtract).then_inc(tlo_ok, 1)
            each = [P, TILES, EXPERTS]

            def over(v):
                return v.rearrange("p (t a) -> p t a", a=1).broadcast_to(each)
            dve.wait_ge(g_ok, 1)
            logits = ps_g[:, 0, 0:TILES * EXPERTS].rearrange("p (t e) -> p t e", e=EXPERTS)
            step(dve.tensor_reduce(top[:], logits, AX.X, ALU.max))
            dve.tensor_tensor(gate[:], logits, over(top[:]), ALU.subtract).then_inc(e_in, 1)
            dve.wait_ge(e_ok, 1)
            step(dve.tensor_reduce(top[:], gate_e[:], AX.X, ALU.add))
            step(dve.reciprocal(top[:], top[:]))
            step(dve.tensor_tensor(gate[:], gate_e[:], over(top[:]), ALU.mult))
            for s in range(EXPERTS):
                for lo_e, hi_e, op in ((0, s + 1, ALU.is_gt), (s + 1, EXPERTS, ALU.is_ge)):
                    if lo_e < hi_e:
                        last = dve.tensor_tensor(beats[:, s, :, lo_e:hi_e],
                                                 gate[:, :, s:s + 1].broadcast_to([P, TILES, hi_e - lo_e]),
                                                 gate[:, :, lo_e:hi_e], op)
            step(last)
            step(dve.tensor_reduce(rank[:].rearrange("p t e -> p (t e)"), beats[:].rearrange("p s t e -> p (t e) s"), AX.X, ALU.add))
            step(dve.scalar_tensor_tensor(comb[:].rearrange("p e t -> p t e"), rank[:], TOP_K - 0.5, gate[:], ALU.is_lt, ALU.mult))


class ExpertWeights:

    def __init__(self, nc, ctx, w1_u, b1_t, w2_u, b2):
        def sb(name, shape, dt=F32):
            return ctx.enter_context(nc.sbuf_tensor(name, shape, dt))

        def sem(name):
            return ctx.enter_context(nc.semaphore(name))

        self.w1_u, self.b1_t, self.w2_u, self.b2 = w1_u, b1_t, w2_u, b2
        self.w1_raw = [sb(f"w1_raw{i}", [P, KC, FQ]) for i in range(2)]
        self.w2_raw = [sb(f"w2_raw{i}", [P, FC, C]) for i in range(2)]
        self.w1_hi = [sb(f"w1_hi{i}", [P, KC, FQ], F32R) for i in range(2)]
        self.w1_lo = [sb(f"w1_lo{i}", [P, KC, FQ], F32R) for i in range(2)]
        self.w2_hi = [sb(f"w2_hi{i}", [P, FC, C], F32R) for i in range(2)]
        self.w2_lo = [sb(f"w2_lo{i}", [P, FC, C], F32R) for i in range(2)]
        self.b1_sb = sb("b1_sb", [P, EXPERTS * FF // P])
        self.b2_sb = sb("b2_sb", [P, EXPERTS * C])
        self.b_in = sem("b_in3")
        self.raw_in = [sem(f"raw_in{i}") for i in range(2)]
        self.split_go = sem("split_go")
        self.hi_ok = sem("w_hi_ok3")
        self.w_ok = sem("w_ok")

    def load_biases(self, sp):
        sp.dma_start(self.b1_sb[:], self.b1_t).then_inc(self.b_in, 16)
        sp.dma_start(self.b2_sb[:], self.b2.rearrange("(a e) n -> a (e n)", a=1).broadcast_to([P, EXPERTS * C])).then_inc(self.b_in, 16)

    def load_unit(self, sp, u, par):
        for raw, src in ((self.w1_raw, self.w1_u), (self.w2_raw, self.w2_u)):
            sp.dma_start(raw[par][:].rearrange("p k n -> p (k n)"),
                         src[bass.ds(u, 1), :, :].rearrange("a p n -> (a p) n")).then_inc(self.raw_in[par], 16)

    def split_unit(self, pool, u, par):
        pool.tensor_copy(self.w1_hi[par][:], self.w1_raw[par][:]).then_inc(self.hi_ok, 1)
        pool.tensor_copy(self.w2_hi[par][:], self.w2_raw[par][:]).then_inc(self.hi_ok, 1)
        pool.wait_ge(self.hi_ok, 2 * u + 2)
        pool.tensor_tensor(self.w1_lo[par][:], self.w1_raw[par][:], self.w1_hi[par][:].bitcast(F32), ALU.subtract)
        pool.tensor_tensor(self.w2_lo[par][:], self.w2_raw[par][:], self.w2_hi[par][:].bitcast(F32), ALU.subtract).then_inc(self.w_ok, 1)


def phase_experts(nc, experts, out, x1, xt_hi, xt_lo, comb):
    with ExitStack() as ctx:
        def sb(name, shape, dt=F32):
            return ctx.enter_context(nc.sbuf_tensor(name, shape, dt))

        def sem(name):
            return ctx.enter_context(nc.semaphore(name))

        w1_hi, w1_lo, w2_hi, w2_lo = experts.w1_hi, experts.w1_lo, experts.w2_hi, experts.w2_lo
        b1_sb, b2_sb, raw_in, w_ok = experts.b1_sb, experts.b2_sb, experts.raw_in, experts.w_ok
        h_f = sb("h_f", [P, FC, TB])
        h_hi = [sb(f"h_hi{i}", [P, FC, TB], F32R) for i in range(2)]
        h_lo = [sb(f"h_lo{i}", [P, FC, TB], F32R) for i in range(2)]
        ps_h = ctx.enter_context(nc.psum_tensor("ps_h", [P, FC, 512], F32))
        ps_o = ctx.enter_context(nc.psum_tensor("ps_o3", [P, TPB, 512], F32))

        h_ok = sem("h_ok")
        g_hi = sem("g_hi_ok")
        g_f = sem("g_f_ok")
        g_lo = sem("g_lo_ok")
        y_ok = sem("y_ok3")
        y_free = sem("y_free")
        b2_ok = sem("b2_ok")
        done = sem("done")
        block = ctx.enter_context(nc.Block())

        UNITS_E = EXPERTS * QUARTERS
        CB2 = C // QUARTERS
        OUT_CREDIT = TILES + 1

        @block.sync
        def _(sp):
            with sp.Fori(1, UNITS_E // 2) as i:
                for par in range(2):
                    u = 2 * i + par
                    sp.wait_ge(w_ok, u - 1)
                    experts.load_unit(sp, u, par)
            sp.wait_ge(y_free, TPB + UNITS_E * TILES)
            sp.wait_ge(b2_ok, UNITS_E * TILES)
            sp.dma_start(out.rearrange("(t p) c -> p t c", p=P), x1[:]).then_inc(done, 16)
            sp.wait_ge(done, 16)

        @block.gpsimd
        def _(pool):
            with pool.Fori(1, UNITS_E // 2) as i:
                for par in range(2):
                    u = 2 * i + par
                    pool.wait_ge(raw_in[par], 32 * i + 32)
                    pool.wait_ge(y_ok, TILES * u - TILES + OUT_CREDIT)
                    pool.sem_inc(experts.split_go, 1)
                    experts.split_unit(pool, u, par)

        @block.tensor
        def _(pe):
            with pe.Fori(0, UNITS_E // 2) as i:
                for w in range(2):
                    with pe.Fori(0, BLOCKS // 2) as j:
                        pe.wait_ge(w_ok, 2 * i + w + 1)
                        for par in range(2):
                            blk = 2 * j + par
                            n = (2 * i + w) * BLOCKS + blk
                            cols = bass.ds(blk * TB, TB)
                            for f in range(FC):
                                pe.wait_ge(g_f, FC * n + f + 1)
                                cut = slice(f * P, (f + 1) * P)
                                for m, (wt, v) in enumerate([(w1_hi, xt_hi), (w1_lo, xt_hi), (w1_hi, xt_lo)]):
                                    for k in range(KC):
                                        last = pe.matmul(ps_h[:, f, 0:TB], wt[w][:, k, cut], v[:, k, cols],
                                                         start=(m + k == 0), stop=(m == 2 and k == KC - 1))
                                last.then_inc(h_ok, 1)
                            for f in range(FC):
                                pe.wait_ge(g_lo, FC * n + f + 1 + FC)
                                for t in range(TPB):
                                    if f == 0:
                                        pe.wait_ge(y_free, TPB * n + t + 1)
                                    cut = slice(t * P, (t + 1) * P)
                                    for m, (v, wt) in enumerate([(h_hi, w2_hi), (h_hi, w2_lo), (h_lo, w2_hi)]):
                                        last = pe.matmul(ps_o[:, t, 0:C], v[par][:, f, cut], wt[w][:, f, :],
                                                         start=(m + f == 0), stop=(m == 2 and f == FC - 1))
                                    if f == FC - 1:
                                        last.then_inc(y_ok, 1)

        @block.scalar
        def _(act):
            act.activation(h_f[:, 0, 0:1], b1_sb[:, 0:1], ACT.Gelu).then_inc(g_f, FC)
            with act.Fori(0, UNITS_E) as u:
                with act.Fori(0, BLOCKS // 2) as j:
                    for par in range(2):
                        n = u * BLOCKS + 2 * j + par
                        act.wait_ge(y_ok, TPB * n - TPB + OUT_CREDIT)
                        for f in range(FC):
                            bias = b1_sb[:, bass.ds(FC * u + f, 1)]
                            act.wait_ge(h_ok, FC * n + f + 1)
                            act.activation(h_hi[par][:, f, :], ps_h[:, f, 0:TB], ACT.Gelu, bias=bias).then_inc(g_hi, 1)
                            act.wait_ge(g_lo, FC * n + f + 1)
                            act.activation(h_f[:, f, :], ps_h[:, f, 0:TB], ACT.Gelu, bias=bias).then_inc(g_f, 1)

        @block.vector
        def _(dve):
            dve.sem_inc(g_lo, FC)
            dve.sem_inc(y_ok, OUT_CREDIT)
            dve.sem_inc(y_free, TPB)
            with dve.Fori(0, EXPERTS) as e:
                with dve.Fori(0, QUARTERS) as q:
                    with dve.Fori(0, BLOCKS // 2) as j:
                        for par in range(2):
                            blk = 2 * j + par
                            n = e * (QUARTERS * BLOCKS) + q * BLOCKS + blk
                            for f in range(FC):
                                dve.wait_ge(g_f, FC * n + f + 1 + FC)
                                dve.tensor_tensor(h_lo[par][:, f, :], h_f[:, f, :], h_hi[par][:, f, :].bitcast(F32),
                                                  ALU.subtract).then_inc(g_lo, 1)
                            for t in range(TPB):
                                part = x1[:, bass.ds(TPB * blk + t, 1), bass.ds(q * CB2, CB2)].rearrange("p a c -> p (a c)")
                                weight = comb[:].rearrange("p e t -> p (e t)")[:, bass.ds(e * TILES + TPB * blk + t, 1)]
                                dve.scalar_tensor_tensor(part, b2_sb[:, bass.ds(e * C + q * CB2, CB2)], weight, part,
                                                         ALU.mult, ALU.add).then_inc(b2_ok, 1)
                            dve.wait_ge(b2_ok, TPB * n + TPB)
                            for t in range(TPB):
                                row = x1[:, bass.ds(TPB * blk + t, 1), :].rearrange("p a c -> p (a c)")
                                weight = comb[:].rearrange("p e t -> p (e t)")[:, bass.ds(e * TILES + TPB * blk + t, 1)]
                                dve.wait_ge(y_ok, TPB * n + t + 1 + OUT_CREDIT)
                                dve.scalar_tensor_tensor(row, ps_o[:, t, 0:C], weight, row, ALU.mult, ALU.add).then_inc(y_free, 1)


def program(nc, x, qkv_w, qkv_b, qkv_b_t, proj_w, proj_b, rel_t, gate_w, gate_b, w1_u, b1_t, w2_u, b2, out):
    def dram(name, shape):
        return nc.dram_tensor(name, shape, F32).ap()

    nc.disable_value_cache = True
    qk_hi_d = dram("qk_hi_d", [2 * C, S])
    qk_lo_d = dram("qk_lo_d", [2 * C, S])
    v_d = dram("v_d", [HEADS, P, TILES * VW])
    rel_hi_d = dram("rel_hi_d", [HEADS, 2 * SIDE, S])
    rel_lo_d = dram("rel_lo_d", [HEADS, 2 * SIDE, S])
    m_d = dram("m_d", [HEADS, S])
    o_d = dram("o_d", [C, S])
    sums_d = dram("sums_d", [HEADS, S])
    rec_d = dram("rec_d", [HEADS, S])
    phase_qkv(nc, x, qkv_w, qkv_b, qkv_b_t, qk_hi_d, qk_lo_d, v_d)
    with ExitStack() as ctx:
        room = ctx.enter_context(nc.sbuf_tensor("room", [P, HPT, S], F32))
        with ExitStack() as keys:
            key_hi = keys.enter_context(nc.sbuf_tensor("key_hi0", [P, S], F32R))
            key_rest = keys.enter_context(nc.sbuf_tensor("key_rest0", [TOP, S], F32R))
            phase_rel(nc, rel_t, qk_hi_d, qk_lo_d, rel_hi_d, rel_lo_d, room, key_hi, key_rest)
            phase_attention(nc, qk_hi_d, qk_lo_d, rel_hi_d, rel_lo_d, v_d, m_d, o_d, sums_d, key_hi, key_rest, room)
        x1 = ctx.enter_context(nc.sbuf_tensor("x1", [P, TILES, C], F32))
        phase_proj(nc, x, o_d, sums_d, rec_d, proj_w, proj_b, room[:, 0:KC, :], x1)
        xt_hi = room[:, 0:KC, :].bitcast(F32R)
        xt_lo = ctx.enter_context(nc.sbuf_tensor("xt_lo", [P, KC, S], F32R))
        comb = ctx.enter_context(nc.sbuf_tensor("comb", [P, EXPERTS, TILES], F32))
        experts = ExpertWeights(nc, ctx, w1_u, b1_t, w2_u, b2)
        phase_gates(nc, gate_w, gate_b, x1, xt_hi, xt_lo, comb, experts)
        phase_experts(nc, experts, out, x1, xt_hi, xt_lo, comb)


def kernel(**inputs):
    import numpy as np
    import concourse.bacc as bacc
    from concourse.bass_utils import run_bass_kernel_spmd

    a = {k: np.asarray(v) for k, v in inputs.items()}
    laid = {
        "x": a["x"].reshape(S, C),
        "qkv_w": a["L0_conv_qkv_w"],
        "qkv_b": a["L0_conv_qkv_b"],
        "qkv_b_t": a["L0_conv_qkv_b"].reshape(-1, P).T,
        "proj_w": a["L0_conv_proj_w"],
        "proj_b": a["L0_conv_proj_b"],
        "rel_t": np.stack([a["L0_conv_rel_pos_w"][::-1].T, a["L0_conv_rel_pos_h"][::-1].T]),
        "gate_w": a["L0_ffn_Wg"],
        "gate_b": a["L0_ffn_bg"],
        "w1_u": a["L0_ffn_W1"].reshape(EXPERTS, KC, P, QUARTERS, FQ).transpose(0, 3, 2, 1, 4).reshape(-1, P, KC * FQ),
        "b1_t": a["L0_ffn_b1"].reshape(-1, P).T,
        "w2_u": a["L0_ffn_W2"].reshape(EXPERTS * QUARTERS, FC, P, C).transpose(0, 2, 1, 3).reshape(-1, P, FC * C),
        "b2": a["L0_ffn_b2"],
    }
    laid = {k: np.ascontiguousarray(v) for k, v in laid.items()}
    nc = bacc.Bacc("TRN2", target_bir_lowering=False, num_devices=1)
    aps = {k: nc.dram_tensor(k, v.shape, mybir.dt.from_np(v.dtype), kind="ExternalInput").ap() for k, v in laid.items()}
    out = nc.dram_tensor("out", (S, C), F32, kind="ExternalOutput").ap()
    program(nc, **aps, out=out)
    r = run_bass_kernel_spmd(nc, [laid], core_ids=[0])
    return r.results[0]["out"].reshape(a["x"].shape)
```

```python
from contextlib import ExitStack

import concourse.bass as bass
from concourse import mybir

F32 = mybir.dt.float32
F32R = mybir.dt.float32r
ACT = mybir.ActivationFunctionType
ALU = mybir.AluOpType
AX = mybir.AxisListType

P = 128
SIDE = 48
S = SIDE * SIDE
C = 384
KC = C // P
HEADS = 12
HD = C // HEADS
TILES = S // P
TB = 384
BLOCKS = S // TB
TPB = TB // P
QK_TILES = 2 * KC
HPT = P // HD
REL = 2 * SIDE - 1
VW = 2 * HD + 1
SCALE = float(HD) ** -0.5
LN1_EPS = 1e-6
LN2_EPS = 1e-5


def phase_qkv(nc, x, qkv_w, qkv_b, qkv_b_t, qk_hi_d, qk_lo_d, v_d):
    GT = 6
    LN_STEPS = 7
    with ExitStack() as ctx:
        def sb(name, shape, dt=F32):
            return ctx.enter_context(nc.sbuf_tensor(name, shape, dt))

        def sem(name):
            return ctx.enter_context(nc.semaphore(name))

        x_sb = sb("x_sb", [P, TILES, C])
        xn = [sb(f"xn{i}", [P, TPB, C]) for i in range(2)]
        stats = [sb(f"stats{i}", [P, TPB, 6]) for i in range(2)]
        mv = [sb(f"mv{i}", [P, TPB, 2]) for i in range(2)]
        veps = [sb(f"veps{i}", [P, TPB]) for i in range(2)]
        root = [sb(f"root{i}", [P, TPB]) for i in range(2)]
        rstd = [sb(f"rstd{i}", [P, TPB]) for i in range(2)]
        nt = [sb(f"nt{i}", [P, TPB]) for i in range(2)]
        w_raw = sb("w_raw", [P, KC, 3 * C])
        w_hi = sb("w_hi", [P, KC, 3 * C], F32R)
        w_lo = sb("w_lo", [P, KC, 3 * C], F32R)
        b_qk = sb("b_qk", [P, QK_TILES])
        b_v = sb("b_v", [P, C])
        ident = sb("ident", [P, P])
        xt_hi = [sb(f"xt_hi{i}", [P, KC, TB], F32R) for i in range(2)]
        xt_lo = [sb(f"xt_lo{i}", [P, KC, TB], F32R) for i in range(2)]
        qk_hi = [sb(f"qk_hi{i}", [P, QK_TILES, TB], F32R) for i in range(2)]
        qk_lo = [sb(f"qk_lo{i}", [P, QK_TILES, TB], F32R) for i in range(2)]
        v_f = sb("v_f", [P, 3, C])
        v_sb = sb("v_sb", [P, HEADS, TILES, VW], F32R)
        ps_t = ctx.enter_context(nc.psum_tensor("ps_t", [P, KC, 512], F32))
        ps_y = ctx.enter_context(nc.psum_tensor("ps_y", [P, 3, 512], F32))

        x_in = [sem(f"x_in{g}") for g in range(TILES // GT)]
        w_in = sem("w_in")
        b_in = sem("b_in")
        bv_in = sem("bv_in")
        ident_ok = sem("ident_ok")
        b_scaled = sem("b_scaled")
        w_hi_ok = sem("w_hi_ok")
        w_lo_ok = sem("w_lo_ok")
        wv_lo_ok = sem("wv_lo_ok")
        aggr_go = sem("aggr_go")
        ln_step = sem("ln_step")
        root_ok = sem("root_ok")
        ln_own = sem("ln_own")
        xn_ok = sem("xn_ok")
        turned = sem("turned")
        xt_hi_ok = sem("xt_hi_ok")
        xt_lo_ok = sem("xt_lo_ok")
        y_ok = sem("y_ok")
        hi_ok = sem("hi_ok")
        lo_ok = sem("lo_ok")
        vf_ok = sem("vf_ok")
        st_out = [sem(f"st_out{i}") for i in range(2)]
        block = ctx.enter_context(nc.Block())

        x_v = x.rearrange("(t p) c -> p t c", p=P)
        qk_hi_v = qk_hi_d.rearrange("(m p) n -> p m n", p=P)
        qk_lo_v = qk_lo_d.rearrange("(m p) n -> p m n", p=P)
        v_dv = v_d.rearrange("h p n -> p h n")
        OPB = QK_TILES + TPB

        @block.sync
        def _(sp):
            for g in range(TILES // GT):
                sp.dma_start(x_sb[:, g * GT:(g + 1) * GT, :], x_v[:, g * GT:(g + 1) * GT, :]).then_inc(x_in[g], 16)
                if g == 0:
                    sp.dma_start(b_qk[:], qkv_b_t[:, 0:QK_TILES]).then_inc(b_in, 16)
                    sp.dma_start(w_raw[:], qkv_w.rearrange("(k p) n -> p k n", p=P)).then_inc(w_in, 16)
            sp.dma_start(b_v[:], qkv_b[2 * C:3 * C].rearrange("(a n) -> a n", a=1).broadcast_to([P, C])).then_inc(bv_in, 16)
            sp.wait_ge(ident_ok, 3)
            with sp.Fori(0, BLOCKS // 2) as i:
                for par in range(2):
                    blk = 2 * i + par
                    sp.wait_ge(hi_ok, OPB * blk + QK_TILES)
                    sp.wait_ge(lo_ok, OPB * blk + QK_TILES)
                    cols = bass.ds(blk * TB, TB)
                    sp.dma_start(qk_hi_v[:, :, cols], qk_hi[par][:].bitcast(F32)).then_inc(st_out[par], 16)
                    sp.dma_start(qk_lo_v[:, :, cols], qk_lo[par][:].bitcast(F32)).then_inc(st_out[par], 16)
                    sp.wait_ge(hi_ok, OPB * blk + OPB)
                    sp.wait_ge(lo_ok, OPB * blk + OPB)
                    sp.dma_start(v_dv[:, :, bass.ds(blk * TPB * VW, TPB * VW)],
                                 v_sb[:].bitcast(F32).rearrange("p h t w -> p h (t w)")[:, :, bass.ds(blk * TPB * VW, TPB * VW)]).then_inc(st_out[par], 16)
            for par in range(2):
                sp.wait_ge(st_out[par], 48 + 24 * BLOCKS)

        @block.gpsimd
        def _(pool):
            for par in range(2):
                pool.sem_inc(st_out[par], 48)
            pool.memset(ident[:], 0.0).then_inc(ident_ok, 1)
            pool.wait_ge(ident_ok, 1)
            pool.affine_select(out=ident[:], in_=ident[:], compare_op=ALU.not_equal, fill=1.0, base=0,
                               pattern=[[-1, P]], channel_multiplier=1).then_inc(ident_ok, 1)
            pool.memset(v_sb[:, :, :, 2 * HD:VW].bitcast(F32), 1.0).then_inc(ident_ok, 1)
            pool.wait_ge(w_hi_ok, 3)
            pool.tensor_tensor(w_lo[:, :, 2 * C:3 * C], w_raw[:, :, 2 * C:3 * C], w_hi[:, :, 2 * C:3 * C].bitcast(F32),
                               ALU.subtract).then_inc(wv_lo_ok, 1)

        @block.scalar
        def _(act):
            def rooted(blk, par):
                act.wait_ge(ln_step, blk + 1)
                act.activation(root[par][:], veps[par][:], ACT.Sqrt).then_inc(root_ok, 1)

            def turned_hi(blk, par):
                act.wait_ge(turned, blk + 1)
                act.copy(xt_hi[par][:], ps_t[:, :, 0:TB]).then_inc(xt_hi_ok, 1)

            def projected(i, par, last=False):
                blk = 2 * i + par
                act.wait_ge(st_out[par], 48 * i + 48)
                for m in range(QK_TILES):
                    act.wait_ge(y_ok, OPB * blk + m + 1)
                    act.activation(qk_hi[par][:, m, :], ps_y[:, m % 3, 0:TB], ACT.Identity,
                                   bias=b_qk[:, m:m + 1]).then_inc(hi_ok, 1)
                    if m == 3 and not last:
                        rooted(blk + 1, 1 - par)
                if not last:
                    turned_hi(blk + 1, 1 - par)
                for t in range(TPB):
                    act.wait_ge(vf_ok, TPB * blk + TPB + t + 1)
                    act.copy(v_sb[:, :, bass.ds(TPB * blk + t, 1), 0:HD],
                             v_f[:, t, :].rearrange("p (h a d) -> p h a d", a=1, d=HD)).then_inc(hi_ok, 1)

            rooted(0, 0)
            act.wait_ge(w_in, 16)
            for n in range(3):
                cols = slice(n * C, (n + 1) * C)
                if n == 1:
                    act.activation(w_hi[:, :, cols], w_raw[:, :, cols], ACT.Copy, scale=SCALE).then_inc(w_hi_ok, 1)
                else:
                    act.copy(w_hi[:, :, cols], w_raw[:, :, cols]).then_inc(w_hi_ok, 1)
                if n == 1:
                    turned_hi(0, 0)
            act.wait_ge(b_scaled, 1)
            with act.Fori(0, BLOCKS // 2 - 1) as i:
                for par in range(2):
                    projected(i, par)
            projected(BLOCKS // 2 - 1, 0)
            projected(BLOCKS // 2 - 1, 1, last=True)

        @block.vector
        def _(dve):
            def row(blk, t):
                return x_sb[:, bass.ds(TPB * blk + t, 1), :].rearrange("p a c -> p (a c)")

            def step(ins, blk, n):
                ins.then_inc(ln_own, 1)
                dve.wait_ge(ln_own, LN_STEPS * blk + n)

            def measured(blk, par):
                for t in range(TPB):
                    last = dve.bn_stats(stats[par][:, t, :], row(blk, t))
                step(last, blk, 1)
                dve.sem_inc(aggr_go, 1)
                for t in range(TPB):
                    last = dve.bn_aggr(mv[par][:, t, :], stats[par][:, t, :])
                step(last, blk, 2)
                dve.tensor_scalar(veps[par][:], mv[par][:, :, 1], LN1_EPS, None, ALU.add).then_inc(ln_step, 1)

            def normalised(blk, par):
                inv, newton = rstd[par][:], nt[par][:]
                dve.wait_ge(root_ok, blk + 1)
                step(dve.reciprocal(inv, root[par][:]), blk, 3)
                step(dve.tensor_tensor(newton, inv, inv, ALU.mult), blk, 4)
                step(dve.tensor_tensor(newton, newton, veps[par][:], ALU.mult), blk, 5)
                step(dve.tensor_scalar(newton, newton, -0.5, 1.5, ALU.mult, ALU.add), blk, 6)
                step(dve.tensor_tensor(inv, inv, newton, ALU.mult), blk, 7)
                for t in range(TPB):
                    last = dve.tensor_scalar(xn[par][:, t, :], row(blk, t), mv[par][:, t, 0:1], inv[:, t:t + 1],
                                             ALU.subtract, ALU.mult)
                last.then_inc(xn_ok, 1)

            def turned_lo(blk, par):
                dve.wait_ge(xt_hi_ok, blk + 1)
                dve.tensor_tensor(xt_lo[par][:], ps_t[:, :, 0:TB], xt_hi[par][:].bitcast(F32),
                                  ALU.subtract).then_inc(xt_lo_ok, 1)

            def projected(i, par, last=False):
                blk = 2 * i + par
                for m in range(QK_TILES):
                    if m == 2 and not last:
                        measured(blk + 1, 1 - par)
                    if m == 4 and not last:
                        normalised(blk + 1, 1 - par)
                    dve.wait_ge(hi_ok, OPB * blk + m + 1)
                    dve.scalar_tensor_tensor(qk_lo[par][:, m, :], ps_y[:, m % 3, 0:TB], b_qk[:, m:m + 1],
                                             qk_hi[par][:, m, :].bitcast(F32), ALU.add, ALU.subtract).then_inc(lo_ok, 1)
                if not last:
                    turned_lo(blk + 1, 1 - par)
                for t in range(TPB):
                    dve.wait_ge(y_ok, OPB * blk + QK_TILES + t + 1)
                    dve.tensor_tensor(v_f[:, t, :], ps_y[:, t, 0:TB], b_v[:], ALU.add).then_inc(vf_ok, 1)
                for t in range(TPB):
                    dve.wait_ge(hi_ok, OPB * blk + QK_TILES + t + 1)
                    tile = bass.ds(TPB * blk + t, 1)
                    dve.tensor_tensor(v_sb[:, :, tile, HD:2 * HD],
                                      v_f[:, t, :].rearrange("p (h a d) -> p h a d", a=1, d=HD),
                                      v_sb[:, :, tile, 0:HD].bitcast(F32), ALU.subtract).then_inc(lo_ok, 1)

            dve.sem_inc(vf_ok, TPB)
            dve.wait_ge(x_in[0], 16)
            measured(0, 0)
            normalised(0, 0)
            dve.wait_ge(b_in, 16)
            dve.tensor_scalar(b_qk[:, KC:QK_TILES], b_qk[:, KC:QK_TILES], SCALE, None, ALU.mult).then_inc(b_scaled, 1)
            dve.wait_ge(w_hi_ok, 1)
            dve.tensor_tensor(w_lo[:, :, 0:C], w_raw[:, :, 0:C], w_hi[:, :, 0:C].bitcast(F32), ALU.subtract)
            dve.wait_ge(w_hi_ok, 2)
            dve.scalar_tensor_tensor(w_lo[:, :, C:2 * C], w_raw[:, :, C:2 * C], SCALE, w_hi[:, :, C:2 * C].bitcast(F32),
                                     ALU.mult, ALU.subtract).then_inc(w_lo_ok, 1)
            turned_lo(0, 0)
            for g in range(1, TILES // GT):
                dve.wait_ge(x_in[g], 16)
            dve.wait_ge(bv_in, 16)
            with dve.Fori(0, BLOCKS // 2 - 1) as i:
                for par in range(2):
                    projected(i, par)
            projected(BLOCKS // 2 - 1, 0)
            projected(BLOCKS // 2 - 1, 1, last=True)

        @block.tensor
        def _(pe):
            def transposed(blk, par):
                pe.wait_ge(xn_ok, blk + 1)
                for k in range(KC):
                    for t in range(TPB):
                        last = pe.transpose(ps_t[:, k, t * P:(t + 1) * P],
                                            xn[par][:, t, k * P:(k + 1) * P], ident[:])
                last.then_inc(turned, 1)

            def projected(blk, par, last_block=False):
                pe.wait_ge(xt_lo_ok, blk + 1)
                hi, lo = xt_hi[par], xt_lo[par]
                for m in range(QK_TILES):
                    if m < 3:
                        pe.wait_ge(vf_ok, TPB * blk + m + 1)
                    else:
                        pe.wait_ge(lo_ok, OPB * blk + m - 2)
                    cut = slice(m * P, (m + 1) * P)
                    for n, (w, v) in enumerate([(w_hi, hi), (w_hi, lo), (w_lo, hi)]):
                        for k in range(KC):
                            last = pe.matmul(ps_y[:, m % 3, 0:TB], w[:, k, cut], v[:, k, :],
                                             start=(n + k == 0), stop=(n == 2 and k == KC - 1))
                    last.then_inc(y_ok, 1)
                if not last_block:
                    transposed(blk + 1, 1 - par)
                for t in range(TPB):
                    pe.wait_ge(lo_ok, OPB * blk + t + 4)
                    cut = slice(t * P, (t + 1) * P)
                    for n, (v, w) in enumerate([(hi, w_hi), (hi, w_lo), (lo, w_hi)]):
                        for k in range(KC):
                            last = pe.matmul(ps_y[:, t, 0:TB], v[:, k, cut], w[:, k, 2 * C:3 * C],
                                             start=(n + k == 0), stop=(n == 2 and k == KC - 1))
                    last.then_inc(y_ok, 1)

            pe.wait_ge(ident_ok, 2)
            transposed(0, 0)
            pe.wait_ge(w_lo_ok, 1)
            pe.wait_ge(wv_lo_ok, 1)
            with pe.Fori(0, BLOCKS // 2 - 1) as i:
                for par in range(2):
                    projected(2 * i + par, par)
            projected(BLOCKS - 2, 0)
            projected(BLOCKS - 1, 1, last_block=True)


QB = 2 * TB
QBLOCKS = S // QB
VARIANTS = TILES // 3
VROWS = SIDE // VARIANTS
OALL_HEADS = HEADS - 2
TOP = 2 * HD + SIDE + VROWS + 1
UNITS = QBLOCKS * TILES
LEAD = 3
LOW_LEAD = 2
POOL_EVERY = 3
SHIFT = 4
RING = 4


def one_hots(pool, key_hi, key_rest, hot, done):
    made = 0
    half = SIDE // 2
    column, row, each = [[0, half], [-1, SIDE]], [[-1, half], [0, SIDE]], [[0, half], [0, SIDE]]
    row_mod = [[0, VARIANTS // 2], [-1, VROWS], [0, SIDE]]
    for keys, rows, fills in ((key_hi, P, lambda y: [(-HD, column), (-(HD + SIDE) - y, row)]),
                              (key_rest, TOP, lambda y: [(-2 * HD, column), (-(2 * HD + SIDE), row_mod), (-(TOP - 1), each)])):
        for y in (0, half):
            pool.memset(hot, 0.0).then_inc(done, 1)
            made += 1
            steps = fills(y)
            for n, (base, pattern) in enumerate(steps):
                src = hot[0:rows, :]
                dst = keys[:, y * SIDE:(y + half) * SIDE] if n == len(steps) - 1 else src

                def shaped(v):
                    return (v.rearrange("p (y x) -> p y x", x=SIDE) if len(pattern) == 2 else
                            v.rearrange("p (v y x) -> p v y x", y=VROWS, x=SIDE))
                pool.wait_ge(done, made)
                pool.affine_select(out=shaped(dst), in_=shaped(src), compare_op=ALU.not_equal, fill=1.0, base=base,
                                   pattern=pattern, channel_multiplier=1).then_inc(done, 1)
                made += 1
            pool.wait_ge(done, made)


HOT_STEPS = 14


def phase_rel(nc, rel_t, qk_hi_d, qk_lo_d, rel_hi_d, rel_lo_d, room, key_hi, key_rest):
    with ExitStack() as ctx:
        def sb(name, shape, dt=F32):
            return ctx.enter_context(nc.sbuf_tensor(name, shape, dt))

        def sem(name):
            return ctx.enter_context(nc.semaphore(name))

        K3 = 3 * HD
        NQ = HPT * SIDE
        CPB = 2
        BANKS = 8
        FILLS = 2 * SIDE // CPB
        GROUPS = HEADS // HPT
        Q_PARTS = 4
        ORDER = (1, 0)
        tab_raw = sb("tab_raw", [K3, 2, REL])
        tab_hi = sb("tab_hi", [K3, 2, REL], F32R)
        tab = sb("tab", [K3, 2, REL], F32R)
        hot = sb("hot0", [P, S // 2])
        neg_lo = sb("neg_lo", [P, 1])
        q_sb = sb("q_sb", [K3, HPT, S], F32R)
        out_hi = [room[0:SIDE, :, :].bitcast(F32R), sb("out_hi", [SIDE, HPT, S], F32R)[:]]
        out_lo = [sb(f"out_lo{a}", [SIDE, HPT, S], F32R)[:] for a in range(2)]
        ps = ctx.enter_context(nc.psum_tensor("ps", [P, BANKS, 512], F32))

        tab_in = sem("tab_in")
        mask_ok = sem("mask_ok")
        hot_ok = sem("hot_ok2")
        tab_hi_ok = sem("tab_hi_ok")
        tab_ok = sem("tab_ok")
        q_in = [sem(f"q_in{i}") for i in range(Q_PARTS)]
        ps_ok = sem("ps_ok")
        r_hi = sem("r_hi")
        r_lo = sem("r_lo")
        r_out = [sem(f"r_out{a}") for a in range(2)]
        block = ctx.enter_context(nc.Block())

        @block.sync
        def _(sp):
            for r in range(3):
                sp.dma_start(tab_raw[r * HD:(r + 1) * HD, :, :], rel_t.rearrange("a d n -> d a n")).then_inc(tab_in, 16)

            def load_q(g):
                for part in range(Q_PARTS):
                    cols = slice(part * S // Q_PARTS, (part + 1) * S // Q_PARTS)
                    for r, src in enumerate((qk_hi_d, qk_hi_d, qk_lo_d)):
                        sp.dma_start(q_sb[r * HD:(r + 1) * HD, :, cols].bitcast(F32),
                                     src[bass.ds(g * P, P), cols].rearrange("(h d) n -> d h n", d=HD)).then_inc(q_in[part], 16)

            def group(g, last=False):
                for n, a in enumerate(ORDER):
                    half = FILLS // 2
                    if n == 1 and not last:
                        sp.wait_ge(ps_ok, FILLS * (g + 1) + 1)
                        load_q(g + 1)
                    sp.wait_ge(r_hi, FILLS * g + half * (n + 1))
                    sp.wait_ge(r_lo, BANKS + FILLS * g + half * (n + 1))
                    for o, d in ((out_hi, rel_hi_d), (out_lo, rel_lo_d)):
                        sp.dma_start(d[bass.ds(g * HPT, HPT), a * SIDE:(a + 1) * SIDE, :].rearrange("h r n -> r h n"),
                                     o[a].bitcast(F32)).then_inc(r_out[a], 16)

            load_q(0)
            with sp.Fori(0, GROUPS - 1) as g:
                group(g)
            group(GROUPS - 1, last=True)
            for a in range(2):
                sp.wait_ge(r_out[a], 32 + 32 * GROUPS)

        @block.gpsimd
        def _(pool):
            for a in range(2):
                pool.sem_inc(r_out[a], 32)
            pool.sem_inc(ps_ok, 1)
            pool.memset(neg_lo[:], 0.0).then_inc(mask_ok, 1)
            pool.wait_ge(mask_ok, 1)
            pool.memset(neg_lo[HD:2 * HD, :], -1.0).then_inc(mask_ok, 1)
            pool.wait_ge(mask_ok, 2)
            one_hots(pool, key_hi, key_rest, hot[:], hot_ok)

        @block.tensor
        def _(pe):
            pe.wait_ge(tab_ok, 1)
            with pe.Fori(0, GROUPS) as g:
                for f in range(FILLS):
                    a, bank = ORDER[f // (FILLS // 2)], f % BANKS
                    if a == 1 and f * CPB % (SIDE // Q_PARTS) == 0:
                        pe.wait_ge(q_in[f * CPB // (SIDE // Q_PARTS)], 48 * g + 48)
                    pe.wait_ge(r_lo, FILLS * g + f + 1)
                    for n in range(CPB):
                        c = (f * CPB + n) % SIDE
                        own = slice(c, S, SIDE) if a == 0 else slice(c * SIDE, (c + 1) * SIDE)
                        last = pe.matmul(ps[0:SIDE, bank, n * NQ:(n + 1) * NQ],
                                         tab[:, a, SIDE - 1 - c:REL - c], q_sb[:, :, own], start=True, stop=True)
                    last.then_inc(ps_ok, 1)

        def places(o, f):
            c = f * CPB % SIDE
            v = o.rearrange("r h (y x) -> r h y x", x=SIDE)
            if ORDER[f // (FILLS // 2)] == 0:
                return v[:, :, :, c:c + CPB].rearrange("r h y c -> r c h y")
            return v[:, :, c:c + CPB, :].rearrange("r h c x -> r c h x")

        def results(bank):
            return ps[0:SIDE, bank, 0:CPB * NQ].rearrange("r (c h y) -> r c h y", c=CPB, h=HPT)

        @block.scalar
        def _(act):
            act.wait_ge(tab_in, 48)
            act.copy(tab_hi[:], tab_raw[:]).then_inc(tab_hi_ok, 1)
            with act.Fori(0, GROUPS) as g:
                for f in range(FILLS):
                    a = ORDER[f // (FILLS // 2)]
                    if f % (FILLS // 2) == 0:
                        act.wait_ge(r_out[a], 32 * g + 32)
                    act.wait_ge(ps_ok, FILLS * g + f + 2)
                    act.copy(places(out_hi[a], f), results(f % BANKS)).then_inc(r_hi, 1)

        @block.vector
        def _(dve):
            dve.sem_inc(r_lo, BANKS)
            dve.wait_ge(mask_ok, 2)
            dve.wait_ge(tab_hi_ok, 1)
            dve.scalar_tensor_tensor(tab[:], tab_hi[:].bitcast(F32), neg_lo[0:K3, :], tab_raw[:], ALU.mult, ALU.add).then_inc(tab_ok, 1)
            with dve.Fori(0, GROUPS) as g:
                for f in range(FILLS):
                    a = ORDER[f // (FILLS // 2)]
                    dve.wait_ge(r_hi, FILLS * g + f + 1)
                    dve.tensor_tensor(places(out_lo[a], f), results(f % BANKS), places(out_hi[a], f).bitcast(F32),
                                      ALU.subtract).then_inc(r_lo, 1)


def phase_attention(nc, qk_hi_d, qk_lo_d, rel_hi_d, rel_lo_d, v_d, m_d, o_d, sums_d, key_hi0, key_rest0, room):
    with ExitStack() as ctx:
        def sb(name, shape, dt=F32):
            return ctx.enter_context(nc.sbuf_tensor(name, shape, dt))

        def sem(name):
            return ctx.enter_context(nc.semaphore(name))

        query_hi = [sb(f"query_hi{i}", [P, S], F32R) for i in range(2)]
        key_hi = [key_hi0, sb("key_hi1", [P, S], F32R)]
        key_rest = [key_rest0, sb("key_rest1", [TOP, S], F32R)]
        query_rest = [sb(f"query_rest{i}", [TOP, VARIANTS, QB], F32R) for i in range(QBLOCKS)]
        val = [sb(f"val{i}", [P, TILES, VW], F32R) for i in range(2)]
        p_hi = [sb(f"p_hi{i}", [P, 2, TB], F32R) for i in range(RING)]
        p_lo = [sb(f"p_lo{i}", [P, 2, TB], F32R) for i in range(RING)]
        p_both = sb("p_f", [P, 2, 2, TB])
        p_f = [p_both[:, i, :, :] for i in range(2)]
        hot = p_both[:].rearrange("p i c n -> p (i c n)")[:, 0:S // 2]
        ident = sb("ident2", [P, P])
        o_all = room[:, 0:KC, :]
        mx = [sb(f"mx{i}", [P, 6, 6]) for i in range(QBLOCKS)]
        neg_m = [sb(f"neg_m{i}", [P, 6]) for i in range(QBLOCKS)]
        neg_mt = [sb(f"neg_mt{i}", [6, P], F32R) for i in range(QBLOCKS)]
        o_t = [sb(f"o_t{i}", [VW, 2, TB]) for i in range(2)]
        o_low = [sb(f"o_low{i}", [HD, 2, TB]) for i in range(2)]
        o_s = [sb(f"o_s{i}", [HD, 2, TB]) for i in range(2)]
        ps_s = ctx.enter_context(nc.psum_tensor("ps_s", [P, 4, 512], F32))
        ps_m = ctx.enter_context(nc.psum_tensor("ps_m", [P, 2, 512], F32))
        ps_o = ctx.enter_context(nc.psum_tensor("ps_o", [P, 2, 512], F32))

        ident_ok = sem("ident_ok")
        hi_in = [sem(f"hi_in{i}") for i in range(2)]
        kv_in = [sem(f"kv_in{i}") for i in range(2)]
        rest_in = [sem(f"rest_in{i}") for i in range(QBLOCKS)]
        m_out = sem("m_out")
        hot_ok = sem("hot_ok")
        s_ok = sem("s_ok")
        f_ok = sem("f_ok")
        lo_dve = sem("p_lo_dve")
        lo_pool = sem("p_lo_pool")
        pv_ok = sem("pv_ok")
        mm_ok = sem("mm_ok")
        mx_ok = sem("mx_ok")
        neg_ok = sem("neg_ok")
        turned = sem("turned2")
        negt_ok = sem("negt_ok")
        acc_a = sem("acc_a")
        acc_d = sem("acc_d")
        o_go = sem("o_go")
        low_moved = sem("low_moved")
        o_sum = sem("o_sum")
        ot_out = [sem(f"ot_out{i}") for i in range(2)]
        all_in = sem("all_in")
        block = ctx.enter_context(nc.Block())

        def chunk_at(h, par, k):
            return (par, UNITS - SHIFT + k) if k < SHIFT else (1 - par, k - SHIFT)

        def unit_at(par, k, lead=LEAD):
            return (par, k + lead) if k + lead < UNITS else (1 - par, k + lead - UNITS)

        def lo_done(h, idx):
            if idx % POOL_EVERY == POOL_EVERY - 1:
                return lo_pool, UNITS // POOL_EVERY * h + idx // POOL_EVERY + 1
            return lo_dve, (UNITS - UNITS // POOL_EVERY) * h + idx - idx // POOL_EVERY + 1

        def low(engine, n, par, idx):
            r = (2 * par + idx) % RING
            engine.wait_ge(f_ok, n + 3)
            engine.tensor_tensor(p_lo[r][:], p_f[idx % 2], p_hi[r][:].bitcast(F32),
                                 ALU.subtract).then_inc(lo_done(0, idx)[0], 1)

        turn_at = {TILES + SHIFT + 2: 0, 2 * TILES + SHIFT + 2: 1, SHIFT + 2: 2}

        def turned_at(k, last):
            b = turn_at.get(k)
            return None if b is None or (last and b < 2) else b

        @block.sync
        def _(sp):
            def load_hi(h, par):
                rows = bass.ds(h * HD, HD)
                krows = bass.ds(C + h * HD, HD)
                sp.dma_start(key_hi[par][0:HD, :].bitcast(F32), qk_hi_d[krows, :]).then_inc(hi_in[par], 16)
                sp.dma_start(query_hi[par][0:HD, :].bitcast(F32), qk_hi_d[rows, :]).then_inc(hi_in[par], 16)
                sp.dma_start(query_hi[par][HD:P, :].bitcast(F32), rel_hi_d[bass.ds(h, 1), :, :].rearrange("a r n -> (a r) n")).then_inc(hi_in[par], 16)

            def load_kv(h, par):
                krows = bass.ds(C + h * HD, HD)
                sp.dma_start(key_rest[par][0:HD, :].bitcast(F32), qk_hi_d[krows, :]).then_inc(kv_in[par], 16)
                sp.dma_start(key_rest[par][HD:2 * HD, :].bitcast(F32), qk_lo_d[krows, :]).then_inc(kv_in[par], 16)
                sp.dma_start(val[par][:].bitcast(F32).rearrange("p t w -> p (t w)"), v_d[bass.ds(h, 1), :, :].rearrange("a p n -> (a p) n")).then_inc(kv_in[par], 16)

            def load_rest(h, b):
                rows = bass.ds(h * HD, HD)
                dst = query_rest[b]
                cols = slice(b * QB, (b + 1) * QB)

                def shared(src):
                    return src.rearrange("r (a n) -> r a n", a=1).broadcast_to([src.shape[0], VARIANTS, QB])
                rel = rel_lo_d[bass.ds(h, 1), :, cols].rearrange("a r n -> (a r) n")
                sp.dma_start(dst[0:HD, :, :].bitcast(F32), shared(qk_lo_d[rows, cols])).then_inc(rest_in[b], 16)
                sp.dma_start(dst[HD:2 * HD, :, :].bitcast(F32), shared(qk_hi_d[rows, cols])).then_inc(rest_in[b], 16)
                sp.dma_start(dst[2 * HD:2 * HD + SIDE, :, :].bitcast(F32), shared(rel[0:SIDE, :])).then_inc(rest_in[b], 16)
                sp.dma_start(dst[2 * HD + SIDE:TOP - 1, :, :].bitcast(F32),
                             rel[SIDE:2 * SIDE, :].rearrange("(v r) n -> r v n", r=VROWS)).then_inc(rest_in[b], 16)

            def load_max(h, b):
                row = m_d[bass.ds(h, 1), b * QB:(b + 1) * QB]
                sp.wait_ge(negt_ok, QBLOCKS * h + b + 1)
                sp.dma_start(row.rearrange("a (t p) -> (a t) p", p=P), neg_mt[b][:].bitcast(F32)).then_inc(m_out, 16)
                sp.wait_ge(m_out, 16 * (QBLOCKS * h + b + 1))
                sp.dma_start(query_rest[b][TOP - 1:TOP, :, :].bitcast(F32),
                             row.rearrange("r (a n) -> r a n", a=1).broadcast_to([1, VARIANTS, QB])).then_inc(rest_in[b], 16)

            def store(h, par, b):
                g = (QBLOCKS * par + b) % 2
                sp.wait_ge(o_sum, QBLOCKS * h + b + 1)
                sp.dma_start(o_d[bass.ds(h * HD, HD), b * QB:(b + 1) * QB], o_s[g][:].rearrange("r c n -> r (c n)")).then_inc(ot_out[g], 16)
                sp.dma_start(sums_d[bass.ds(h, 1), b * QB:(b + 1) * QB],
                             o_t[g][VW - 1:VW, :, :].rearrange("r c n -> r (c n)")).then_inc(ot_out[g], 16)

            def start(h, par, last=False):
                if not last:
                    sp.wait_ge(s_ok, UNITS * h + LEAD)
                    load_hi(h + 1, 1 - par)
                load_max(h, 2)

            def rest(h, par):
                sp.wait_ge(pv_ok, UNITS * h + RING)
                load_kv(h + 1, 1 - par)
                for b in range(QBLOCKS):
                    sp.wait_ge(s_ok, UNITS * h + TILES * (b + 1))
                    load_rest(h + 1, b)
                    if b < 2:
                        load_max(h + 1, b)
                        store(h, par, b)
                start(h + 1, 1 - par, isinstance(h, int) and h == HEADS - 2)
                store(h, par, 2)

            load_hi(0, 0)
            load_kv(0, 0)
            for b in range(QBLOCKS):
                load_rest(0, b)
            for b in range(2):
                load_max(0, b)
            sp.wait_ge(hot_ok, HOT_STEPS)
            start(0, 0)
            with sp.Fori(0, OALL_HEADS // 2) as i:
                for par in range(2):
                    rest(2 * i + par, par)
            rest(HEADS - 2, 0)
            for g in range(2):
                sp.wait_ge(ot_out[g], 32 + 32 * QBLOCKS * OALL_HEADS // 2)
            for c in range(KC):
                rows = min(P, OALL_HEADS * HD - c * P)
                sp.dma_start(o_all[0:rows, c, :], o_d[c * P:c * P + rows, :]).then_inc(all_in, 16)
            for b in range(QBLOCKS):
                store(HEADS - 1, 1, b)
            for g in range(2):
                sp.wait_ge(ot_out[g], 32 + 32 * QBLOCKS * HEADS // 2)
            sp.wait_ge(all_in, 16 * KC)

        @block.gpsimd
        def _(pool):
            for g in range(2):
                pool.sem_inc(ot_out[g], 32)
            pool.memset(ident[:], 0.0).then_inc(ident_ok, 1)
            pool.wait_ge(ident_ok, 1)
            pool.affine_select(out=ident[:], in_=ident[:], compare_op=ALU.not_equal, fill=1.0, base=0,
                               pattern=[[-1, P]], channel_multiplier=1).then_inc(ident_ok, 1)
            one_hots(pool, key_hi[1], key_rest[1], hot, hot_ok)

            def joined_at(b):
                return TILES * (b + 1) + 2 * POOL_EVERY - 1

            def joined(h, par, b, last_one):
                g = (QBLOCKS * par + b) % 2
                pool.wait_ge(acc_a, QBLOCKS * h + b + 2)
                pool.wait_ge(acc_d, QBLOCKS * h + b + 2)
                pool.wait_ge(*(lo_done(h, UNITS - 1) if last_one else lo_done(h + (b == QBLOCKS - 1), joined_at(b) % UNITS)))
                pool.sem_inc(o_go, 1)
                pool.tensor_copy(o_low[g][:], o_t[g][HD:2 * HD, :, :]).then_inc(low_moved, 1)
                pool.wait_ge(low_moved, QBLOCKS * h + b + 1)
                pool.tensor_tensor(o_s[g][:], o_t[g][0:HD, :, :], o_low[g][:], ALU.add).then_inc(o_sum, 1)

            FIRST = 3 * POOL_EVERY

            def head(h, par, last=False):
                for idx in range(FIRST - 1, UNITS + FIRST - 1, POOL_EVERY):
                    if idx < UNITS:
                        low(pool, UNITS * h + idx, par, idx)
                    elif not last:
                        low(pool, UNITS * h + idx, 1 - par, idx - UNITS)
                    for b in range(QBLOCKS):
                        if idx == joined_at(b):
                            joined(h, par, b, last and b == QBLOCKS - 1)

            for idx in range(POOL_EVERY - 1, FIRST - 1, POOL_EVERY):
                low(pool, idx, 0, idx)
            with pool.Fori(0, OALL_HEADS // 2) as h0:
                for par in range(2):
                    head(2 * h0 + par, par)
            head(HEADS - 2, 0)
            head(HEADS - 1, 1, last=True)

        @block.tensor
        def _(pe):
            def half(tp, s, c, ps):
                tile = slice(s // 3 * P, (s // 3 + 1) * P)
                keys = slice(s % 3 * QB + c * TB, s % 3 * QB + (c + 1) * TB)
                pe.matmul(ps[:, c, 0:TB], query_hi[tp][:, tile], key_hi[tp][:, keys], start=True, stop=True).then_inc(mm_ok, 1)

            def scores(n, par, idx, turn=None):
                b, j = idx // TILES, idx % TILES
                bank = 2 * (idx % 2)
                pe.wait_ge(f_ok, n + 1)
                if turn is not None:
                    pe.transpose(ps_s[0:6, bank, TB:TB + P], neg_m[turn][:], ident[:])
                for c in range(2):
                    pe.matmul(ps_s[:, bank + c, 0:TB], key_hi[par][:, j * P:(j + 1) * P],
                              query_hi[par][:, b * QB + c * TB:b * QB + (c + 1) * TB], start=True, stop=False)
                for c in range(2):
                    last = pe.matmul(ps_s[:, bank + c, 0:TB], key_rest[par][:, j * P:(j + 1) * P],
                                     query_rest[b][:, j // 3, c * TB:(c + 1) * TB], start=False, stop=True)
                last.then_inc(s_ok, 1)

            def pv(h, par, idx):
                j, r = idx % TILES, (2 * par + idx) % RING
                pe.wait_ge(*lo_done(h, idx))
                for part in (p_hi, p_lo):
                    for c in range(2):
                        last = pe.matmul(ps_o[0:VW, c, 0:TB], val[par][:, j, :], part[r][:, c, :],
                                         start=(j == 0 and part is p_hi), stop=(j == TILES - 1 and part is p_lo))
                last.then_inc(pv_ok, 1)

            def head(h, par, last=False):
                for k in range(UNITS):
                    if k % TILES == TILES - 1:
                        pv(h, par, k)
                    up, idx = unit_at(par, k)
                    if not (last and up != par):
                        turn = turned_at(k, last)
                        if idx == 0:
                            pe.wait_ge(kv_in[up], 48 * ((h + 1) // 2 + 1) if isinstance(h, int) else 48 * (h0 + 1 + par))
                        if idx % TILES == 0:
                            pe.wait_ge(rest_in[idx // TILES], 80 * (h + 1 + (up != par)))
                        if turn is not None:
                            pe.wait_ge(neg_ok, QBLOCKS * (h + (turn < 2)) + turn + 1)
                        scores(UNITS * h + k + LEAD, up, idx, turn)
                    tp, s = chunk_at(h, par, k)
                    maxima = not (last and tp != par)
                    number = 2 * (UNITS * (h + 1) + k - SHIFT)
                    if maxima:
                        if s == 0:
                            pe.wait_ge(hi_in[tp], 48 * ((h + 1) // 2 + 1) if isinstance(h, int) else 48 * (h0 + 1 + par))
                        pe.wait_ge(mx_ok, number - 1)
                        half(tp, s, 0, ps_m)
                    if k % TILES == 0:
                        pe.wait_ge(acc_a, QBLOCKS * h + k // TILES + 1)
                        pe.wait_ge(acc_d, QBLOCKS * h + k // TILES + 1)
                    if k % TILES < TILES - 1:
                        pv(h, par, k)
                    if maxima:
                        pe.wait_ge(mx_ok, number)
                        half(tp, s, 1, ps_m)

            pe.wait_ge(hi_in[0], 48)
            spare = [ps_m, ps_s[:, 0:2, :], ps_s[:, 2:4, :]]
            for s in range(UNITS - SHIFT):
                if s >= 3:
                    pe.wait_ge(mx_ok, 2 * (s - 2))
                for c in range(2):
                    half(0, s, c, spare[s % 3])
                for b in range(2):
                    if s == TILES * (b + 1) + 3:
                        if b == 0:
                            pe.wait_ge(ident_ok, 2)
                        pe.wait_ge(neg_ok, b + 1)
                        pe.transpose(ps_o[0:6, b, 0:P], neg_m[b][:], ident[:]).then_inc(turned, 1)
            pe.wait_ge(mx_ok, 2 * (UNITS - SHIFT))
            pe.wait_ge(kv_in[0], 48)
            pe.wait_ge(rest_in[0], 80)
            for idx in range(LEAD):
                scores(idx, 0, idx)
            pe.wait_ge(negt_ok, 2)
            with pe.Fori(0, OALL_HEADS // 2) as h0:
                for par in range(2):
                    head(2 * h0 + par, par)
            head(HEADS - 2, 0)
            head(HEADS - 1, 1, last=True)

        @block.scalar
        def _(act):
            def exps(h, par, idx, turn=None):
                n = UNITS * h + idx
                bank, r = 2 * (idx % 2), (2 * par + idx) % RING
                act.wait_ge(s_ok, n + 1)
                act.wait_ge(pv_ok, n + 1)
                act.activation(p_hi[r][:], ps_s[:, bank:bank + 2, 0:TB], ACT.Exp)
                if turn is not None:
                    act.copy(neg_mt[turn][:], ps_s[0:6, bank, TB:TB + P]).then_inc(negt_ok, 1)
                if not (isinstance(h, int) and UNITS * h + idx < 2):
                    act.wait_ge(*(lo_done(h, idx - 2) if idx >= 2 else lo_done(h - 1, idx - 2 + UNITS)))
                act.activation(p_f[idx % 2], ps_s[:, bank:bank + 2, 0:TB], ACT.Exp).then_inc(f_ok, 1)

            def head(h, par, last=False):
                for k in range(UNITS):
                    if k % TILES == TILES - 1:
                        b = k // TILES
                        g = (QBLOCKS * par + b) % 2
                        act.wait_ge(pv_ok, UNITS * h + k + 1 + RING)
                        act.wait_ge(ot_out[g], out_count(h, par, b))
                        act.copy(o_t[g][:, 0, :], ps_o[0:VW, 0, 0:TB]).then_inc(acc_a, 1)
                    up, idx = unit_at(par, k)
                    if not (last and up != par):
                        exps(h + (up != par), up, idx, turned_at(k, last))

            def out_count(h, par, b):
                return 32 * ((QBLOCKS * par + b) // 2) + 32 * QBLOCKS * half(h, par) + 32

            def half(h, par):
                return (h - par) // 2 if isinstance(h, int) else h0

            act.sem_inc(acc_a, 1)
            act.sem_inc(f_ok, 2)
            for b in range(2):
                act.wait_ge(turned, b + 1)
                act.copy(neg_mt[b][:], ps_o[0:6, b, 0:P]).then_inc(negt_ok, 1)
            act.wait_ge(hot_ok, HOT_STEPS)
            for idx in range(LEAD):
                exps(0, 0, idx)
            with act.Fori(0, OALL_HEADS // 2) as h0:
                for par in range(2):
                    head(2 * h0 + par, par)
            head(HEADS - 2, 0)
            head(HEADS - 1, 1, last=True)

        @block.vector
        def _(dve):
            def negated(count, s):
                if s % TILES == TILES - 1:
                    dve.wait_ge(mx_ok, 2 * count + 2)
                    dve.tensor_reduce(neg_m[s // TILES][:], mx[s // TILES][:], AX.X, ALU.max, negate=True).then_inc(neg_ok, 1)

            def reduce_half(count, s, c):
                dve.wait_ge(mm_ok, 2 * count + c + 1)
                col = s % 3 * 2 + c
                dve.tensor_reduce(mx[s // TILES][:, s // 3 % 6, col:col + 1], ps_m[:, c, 0:TB], AX.X, ALU.max).then_inc(mx_ok, 1)

            def reduce_both(s, ps):
                dve.wait_ge(mm_ok, 2 * s + 2)
                col = s % 3 * 2
                dve.tensor_reduce(mx[s // TILES][:, s // 3 % 6, col:col + 2], ps[:, :, 0:TB], AX.X, ALU.max).then_inc(mx_ok, 2)
                negated(s, s)

            def head(h, par, last=False):
                for k in range(UNITS):
                    if k % TILES == TILES - 1:
                        b = k // TILES
                        g = (QBLOCKS * par + b) % 2
                        dve.wait_ge(pv_ok, UNITS * h + k + 1 + RING)
                        dve.wait_ge(ot_out[g], out_count(h, par, b))
                        dve.tensor_copy(o_t[g][:, 1, :], ps_o[0:VW, 1, 0:TB]).then_inc(acc_d, 1)
                    tp, s = chunk_at(h, par, k)
                    maxima = not (last and tp != par)
                    number = UNITS * (h + 1) + k - SHIFT
                    if maxima:
                        reduce_half(number, s, 0)
                    up, idx = unit_at(par, k, LOW_LEAD)
                    if not (last and up != par) and idx % POOL_EVERY < POOL_EVERY - 1:
                        low(dve, UNITS * h + k + LOW_LEAD, up, idx)
                    if maxima:
                        reduce_half(number, s, 1)
                        negated(number, s)

            def out_count(h, par, b):
                return 32 * ((QBLOCKS * par + b) // 2) + 32 * QBLOCKS * half(h, par) + 32

            def half(h, par):
                return (h - par) // 2 if isinstance(h, int) else h0

            dve.sem_inc(acc_d, 1)
            dve.sem_inc(pv_ok, RING)
            for s in range(UNITS - SHIFT):
                reduce_both(s, [ps_m, ps_s[:, 0:2, :], ps_s[:, 2:4, :]][s % 3])
            for idx in range(LOW_LEAD):
                if idx % POOL_EVERY < POOL_EVERY - 1:
                    low(dve, idx, 0, idx)
            with dve.Fori(0, OALL_HEADS // 2) as h0:
                for par in range(2):
                    head(2 * h0 + par, par)
            head(HEADS - 2, 0)
            head(HEADS - 1, 1, last=True)


EXPERTS = 8
TOP_K = 2
FF = 4 * C
QUARTERS = 4
FQ = FF // QUARTERS
FC = FQ // P


def phase_proj(nc, x, o_d, sums_d, rec_d, proj_w, proj_b, o_all, x1, stats, experts):
    with ExitStack() as ctx:
        def sb(name, shape, dt=F32):
            return ctx.enter_context(nc.sbuf_tensor(name, shape, dt))

        def sem(name):
            return ctx.enter_context(nc.semaphore(name))

        FLAT = HEADS * S // P
        rflat = sb("rflat", [P, FLAT])
        rsum = sb("rsum", [HEADS, S])
        spread = sb("spread", [HEADS, KC, P])
        o_f = [sb(f"o_f{i}", [P, KC, TB]) for i in range(2)]
        o_hi = [sb(f"o_hi{i}", [P, KC, TB], F32R) for i in range(2)]
        o_lo = [sb(f"o_lo{i}", [P, KC, TB], F32R) for i in range(2)]
        w_raw = sb("pw_raw", [P, KC, C])
        w_hi = sb("pw_hi", [P, KC, C], F32R)
        w_lo = sb("pw_lo", [P, KC, C], F32R)
        p_b = sb("p_b", [P, C])
        ps_r = ctx.enter_context(nc.psum_tensor("ps_r", [P, KC, 512], F32))
        ps_y = ctx.enter_context(nc.psum_tensor("ps_y2", [P, TPB, 512], F32))

        s_in = sem("sums_in")
        rec_out = sem("rec_out")
        rec_in = sem("rec_in")
        o_in = sem("o_in")
        X_LOADS = BLOCKS // 2
        x_in = [sem(f"x_in2_{g}") for g in range(X_LOADS)]
        w_in = sem("w_in2")
        spread_made = sem("spread_made")
        w_hi_ok = sem("w_hi_ok2")
        w_lo_ok = sem("w_lo_ok2")
        x_ok = sem("x_ok")
        r_ok = sem("r_ok")
        spread_ok = sem("spread_ok")
        of_ok = sem("of_ok")
        ohi_ok = sem("ohi_ok")
        olo_ok = sem("olo_ok")
        y_ok = sem("y_ok2")
        x1_ok = sem("x1_ok")
        block = ctx.enter_context(nc.Block())

        @block.sync
        def _(sp):
            sp.dma_start(rflat[:], sums_d.rearrange("h n -> (h n)").rearrange("(p n) -> p n", p=P)).then_inc(s_in, 16)
            rows = OALL_HEADS * HD - (KC - 1) * P
            sp.dma_start(o_all[rows:P, KC - 1, :], o_d[OALL_HEADS * HD:C, :]).then_inc(o_in, 16)
            sp.wait_ge(r_ok, 1)
            sp.dma_start(rec_d.rearrange("h n -> (h n)").rearrange("(p n) -> p n", p=P), rflat[:]).then_inc(rec_out, 16)
            sp.wait_ge(rec_out, 16)
            sp.dma_start(rsum[:], rec_d).then_inc(rec_in, 16)
            for g in range(X_LOADS):
                rows = slice(g * TILES // X_LOADS, (g + 1) * TILES // X_LOADS)
                sp.dma_start(x1[:, rows, :], x.rearrange("(t p) c -> p t c", p=P)[:, rows, :]).then_inc(x_in[g], 16)
            for u in range(2):
                experts.load_unit(sp, u, u)
            experts.load_biases(sp)
            sp.wait_ge(experts.b_in, 32)

        @block.gpsimd
        def _(pool):
            pool.memset(spread[:], 1.0).then_inc(spread_made, 1)
            flat = spread[:].rearrange("h c r -> h (c r)")
            pool.wait_ge(spread_made, 1)
            pool.affine_select(out=flat, in_=flat, compare_op=ALU.is_ge, fill=0.0, base=0,
                               pattern=[[1, KC * P]], channel_multiplier=-HD).then_inc(spread_made, 1)
            pool.wait_ge(spread_made, 2)
            pool.affine_select(out=flat, in_=flat, compare_op=ALU.is_ge, fill=0.0, base=HD - 1,
                               pattern=[[-1, KC * P]], channel_multiplier=HD).then_inc(spread_made, 1)
            pool.wait_ge(w_in, 32)
            bias = p_b[:].rearrange("p (a n) -> p a n", a=1).broadcast_to([P, TPB, C])
            for b in range(BLOCKS):
                rows = x1[:, b * TPB:(b + 1) * TPB, :]
                pool.wait_ge(x_in[b * X_LOADS // BLOCKS], 16)
                pool.tensor_tensor(rows, rows, bias, ALU.add).then_inc(x_ok, 1)
            for u in range(2):
                pool.wait_ge(experts.raw_in[u], 32)
                pool.sem_inc(experts.split_go, 1)
                experts.split_unit(pool, u, u)

        @block.tensor
        def _(pe):
            def spread_block(blk):
                pe.wait_ge(of_ok, blk + 1)
                for c in range(KC):
                    last = pe.matmul(ps_r[:, c, 0:TB], spread[:, c, :], rsum[:, bass.ds(blk * TB, TB)],
                                     start=True, stop=True)
                last.then_inc(spread_ok, 1)

            def product(blk, par):
                pe.wait_ge(olo_ok, blk + 1)
                for t in range(TPB):
                    pe.wait_ge(x1_ok, TPB * blk + t + 1)
                    cut = slice(t * P, (t + 1) * P)
                    for n, (v, w) in enumerate([(o_hi, w_hi), (o_hi, w_lo), (o_lo, w_hi)]):
                        for k in range(KC):
                            last = pe.matmul(ps_y[:, t, 0:C], v[par][:, k, cut], w[:, k, :],
                                             start=(n + k == 0), stop=(n == 2 and k == KC - 1))
                    last.then_inc(y_ok, 1)

            pe.wait_ge(spread_made, 3)
            pe.wait_ge(rec_in, 16)
            pe.wait_ge(w_lo_ok, 1)
            spread_block(0)
            with pe.Fori(0, BLOCKS // 2 - 1) as i:
                for par in range(2):
                    spread_block(2 * i + par + 1)
                    product(2 * i + par, par)
            spread_block(BLOCKS - 1)
            product(BLOCKS - 2, 0)
            product(BLOCKS - 1, 1)

        @block.scalar
        def _(act):
            act.dma_start(w_raw[:], proj_w.rearrange("(k p) n -> p k n", p=P)).then_inc(w_in, 16)
            act.dma_start(p_b[:], proj_b.rearrange("(a n) -> a n", a=1).broadcast_to([P, C])).then_inc(w_in, 16)
            act.wait_ge(w_in, 32)
            act.copy(w_hi[:], w_raw[:]).then_inc(w_hi_ok, 1)
            with act.Fori(0, BLOCKS // 2) as i:
                for par in range(2):
                    blk = 2 * i + par
                    act.wait_ge(of_ok, blk + 2)
                    act.copy(o_hi[par][:], o_f[par][:]).then_inc(ohi_ok, 1)

        @block.vector
        def _(dve):
            def normalised(blk, par):
                dve.wait_ge(spread_ok, blk + 1)
                dve.tensor_tensor(o_f[par][:], ps_r[:, :, 0:TB], o_all[:, :, bass.ds(blk * TB, TB)], ALU.mult).then_inc(of_ok, 1)
                dve.wait_ge(ohi_ok, blk + 1)
                dve.tensor_tensor(o_lo[par][:], o_f[par][:], o_hi[par][:].bitcast(F32), ALU.subtract).then_inc(olo_ok, 1)

            def added(blk):
                dve.wait_ge(x_ok, blk + 1)
                for t in range(TPB):
                    dve.wait_ge(y_ok, TPB * blk + t + 1)
                    row = x1[:, bass.ds(TPB * blk + t, 1), :].rearrange("p a c -> p (a c)")
                    dve.tensor_tensor(row, ps_y[:, t, 0:C], row, ALU.add).then_inc(x1_ok, 1)

            def measured(blk):
                dve.wait_ge(x1_ok, TPB * blk + 2 * TPB)
                for t in range(TPB):
                    tile = bass.ds(TPB * blk + t, 1)
                    dve.bn_stats(stats[:, tile, :].rearrange("p a c -> p (a c)"), x1[:, tile, :].rearrange("p a c -> p (a c)"))

            dve.sem_inc(x1_ok, TPB)
            dve.sem_inc(of_ok, 1)
            dve.wait_ge(s_in, 16)
            dve.reciprocal(rflat[:], rflat[:]).then_inc(r_ok, 1)
            dve.wait_ge(w_hi_ok, 1)
            dve.tensor_tensor(w_lo[:], w_raw[:], w_hi[:].bitcast(F32), ALU.subtract).then_inc(w_lo_ok, 1)
            dve.wait_ge(o_in, 16)
            normalised(0, 0)
            with dve.Fori(0, BLOCKS // 2 - 1) as i:
                for par in range(2):
                    normalised(2 * i + par + 1, 1 - par)
                    added(2 * i + par)
                    measured(2 * i + par)
            normalised(BLOCKS - 1, 1)
            for blk in (BLOCKS - 2, BLOCKS - 1):
                added(blk)
                measured(blk)


def phase_gates(nc, gate_w, gate_b, x1, stats, xt_hi, xt_lo, comb):
    with ExitStack() as ctx:
        def sb(name, shape, dt=F32):
            return ctx.enter_context(nc.sbuf_tensor(name, shape, dt))

        def sem(name):
            return ctx.enter_context(nc.semaphore(name))

        g_raw = sb("g_raw", [P, KC, EXPERTS])
        g_hi = sb("g_hi", [P, KC, EXPERTS], F32R)
        g_lo = sb("g_lo", [P, KC, EXPERTS], F32R)
        g_b = sb("g_b", [EXPERTS, 1])
        ident = sb("ident3", [P, P])
        mv = sb("mv2", [P, TILES, 2])
        veps = sb("veps2", [P, TILES])
        root = sb("root2", [P, TILES])
        rstd = sb("rstd2", [P, TILES])
        nt = sb("nt2", [P, TILES])
        xn = [sb(f"xnn{i}", [P, TPB, C]) for i in range(2)]
        logit_t = sb("logit_t", [EXPERTS, S])
        gate = sb("gate", [P, TILES, EXPERTS])
        gate_e = sb("gate_e", [P, TILES, EXPERTS])
        beats = sb("beats", [P, EXPERTS, TILES, EXPERTS])
        rank = sb("rank", [P, TILES, EXPERTS])
        top = sb("top", [P, TILES])
        ps_t = [ctx.enter_context(nc.psum_tensor(f"ps_t{i}", [P, KC, 512], F32)) for i in range(2)]
        ps_g = ctx.enter_context(nc.psum_tensor("ps_g", [P, 2, 512], F32))

        w_in = sem("g_in")
        const_ok = sem("const_ok")
        w_hi_ok = sem("gw_hi_ok")
        w_lo_ok = sem("gw_lo_ok")
        own = sem("own2")
        root_in = sem("root_in")
        root_ok = sem("root_ok2")
        xn_ok = sem("xn_ok2")
        t_ok = sem("t_ok")
        thi_ok = sem("thi_ok")
        tlo_ok = sem("tlo_ok")
        l_ok = sem("l_ok")
        lt_ok = sem("lt_ok")
        g_ok = sem("g_ok")
        e_in = sem("e_in")
        e_ok = sem("e_ok")
        block = ctx.enter_context(nc.Block())

        @block.gpsimd
        def _(pool):
            pool.memset(ident[:], 0.0).then_inc(const_ok, 1)
            pool.wait_ge(const_ok, 1)
            pool.affine_select(out=ident[:], in_=ident[:], compare_op=ALU.not_equal, fill=1.0, base=0,
                               pattern=[[-1, P]], channel_multiplier=1).then_inc(const_ok, 1)
        @block.tensor
        def _(pe):
            def transposed(blk, par):
                pe.wait_ge(xn_ok, blk + 1)
                for k in range(KC):
                    for t in range(TPB):
                        last = pe.transpose(ps_t[par][:, k, t * P:(t + 1) * P], xn[par][:, t, k * P:(k + 1) * P], ident[:])
                last.then_inc(t_ok, 1)

            pe.wait_ge(const_ok, 2)

            def step(i, par, last=False):
                blk = 2 * i + par
                pe.wait_ge(tlo_ok, blk + 1)
                if not last:
                    transposed(blk + 2, par)
                pe.wait_ge(lt_ok, blk + 1)
                cols = bass.ds(blk * TB, TB)
                for n, (w, v) in enumerate([(g_hi, xt_hi), (g_lo, xt_hi), (g_hi, xt_lo)]):
                    for k in range(KC):
                        logits = pe.matmul(ps_g[0:EXPERTS, par, 0:TB], w[:, k, :], v[:, k, cols],
                                           start=(n + k == 0), stop=(n == 2 and k == KC - 1))
                logits.then_inc(l_ok, 1)

            for par in range(2):
                transposed(par, par)
            pe.wait_ge(w_lo_ok, 1)
            with pe.Fori(0, BLOCKS // 2 - 1) as i:
                for par in range(2):
                    step(i, par)
            for par in range(2):
                step(BLOCKS // 2 - 1, par, last=True)
            pe.wait_ge(lt_ok, BLOCKS + 2)
            for t in range(TILES):
                last = pe.transpose(ps_g[:, 0, t * EXPERTS:(t + 1) * EXPERTS], logit_t[:, t * P:(t + 1) * P],
                                    ident[0:EXPERTS, 0:EXPERTS])
            last.then_inc(g_ok, 1)

        @block.scalar
        def _(act):
            act.dma_start(g_raw[:], gate_w.rearrange("(k p) n -> p k n", p=P)).then_inc(w_in, 16)
            act.dma_start(g_b[:], gate_b.rearrange("(n a) -> n a", a=1)).then_inc(w_in, 16)
            act.wait_ge(root_in, 1)
            act.activation(root[:], veps[:], ACT.Sqrt).then_inc(root_ok, 1)
            act.wait_ge(w_in, 32)
            act.copy(g_hi[:], g_raw[:]).then_inc(w_hi_ok, 1)

            def turned_hi(blk, par):
                act.wait_ge(t_ok, blk + 1)
                act.copy(xt_hi[:, :, bass.ds(blk * TB, TB)], ps_t[par][:, :, 0:TB]).then_inc(thi_ok, 1)

            def logits_out(blk, par):
                act.wait_ge(l_ok, blk + 1)
                act.activation(logit_t[:, bass.ds(blk * TB, TB)], ps_g[0:EXPERTS, par, 0:TB], ACT.Identity,
                               bias=g_b[:]).then_inc(lt_ok, 1)

            for par in range(2):
                turned_hi(par, par)
            with act.Fori(0, BLOCKS // 2 - 1) as i:
                for par in range(2):
                    turned_hi(2 * i + par + 2, par)
                    logits_out(2 * i + par, par)
            for par in range(2):
                logits_out(BLOCKS - 2 + par, par)
            act.wait_ge(e_in, 1)
            act.activation(gate_e[:], gate[:], ACT.Exp).then_inc(e_ok, 1)

        @block.vector
        def _(dve):
            n_own = [0]

            def step(ins):
                n_own[0] += 1
                ins.then_inc(own, 1)
                dve.wait_ge(own, n_own[0])

            dve.sem_inc(lt_ok, 2)
            for t in range(TILES):
                last = dve.bn_aggr(mv[:, t, :], stats[:, t, :])
            step(last)
            dve.tensor_scalar(veps[:], mv[:, :, 1], LN2_EPS, None, ALU.add).then_inc(root_in, 1)
            dve.wait_ge(root_ok, 1)
            step(dve.reciprocal(rstd[:], root[:]))
            step(dve.tensor_tensor(nt[:], rstd[:], rstd[:], ALU.mult))
            step(dve.tensor_tensor(nt[:], nt[:], veps[:], ALU.mult))
            step(dve.tensor_scalar(nt[:], nt[:], -0.5, 1.5, ALU.mult, ALU.add))
            step(dve.tensor_tensor(rstd[:], rstd[:], nt[:], ALU.mult))

            def normalised(blk, par):
                for t in range(TPB):
                    tile = bass.ds(TPB * blk + t, 1)
                    last = dve.tensor_scalar(xn[par][:, t, :], x1[:, tile, :].rearrange("p a c -> p (a c)"),
                                             mv[:, tile, 0:1].rearrange("p a c -> p (a c)"), rstd[:, tile],
                                             ALU.subtract, ALU.mult)
                last.then_inc(xn_ok, 1)

            def turned_lo(blk, par):
                cols = bass.ds(blk * TB, TB)
                dve.wait_ge(thi_ok, blk + 1)
                dve.tensor_tensor(xt_lo[:, :, cols], ps_t[par][:, :, 0:TB], xt_hi[:, :, cols].bitcast(F32),
                                  ALU.subtract).then_inc(tlo_ok, 1)

            for par in range(2):
                normalised(par, par)
            dve.wait_ge(w_hi_ok, 1)
            dve.tensor_tensor(g_lo[:], g_raw[:], g_hi[:].bitcast(F32), ALU.subtract).then_inc(w_lo_ok, 1)
            with dve.Fori(0, BLOCKS // 2 - 1) as i:
                for par in range(2):
                    turned_lo(2 * i + par, par)
                    normalised(2 * i + par + 2, par)
            for par in range(2):
                turned_lo(BLOCKS - 2 + par, par)
            each = [P, TILES, EXPERTS]

            def over(v):
                return v.rearrange("p (t a) -> p t a", a=1).broadcast_to(each)
            dve.wait_ge(g_ok, 1)
            logits = ps_g[:, 0, 0:TILES * EXPERTS].rearrange("p (t e) -> p t e", e=EXPERTS)
            step(dve.tensor_reduce(top[:], logits, AX.X, ALU.max))
            dve.tensor_tensor(gate[:], logits, over(top[:]), ALU.subtract).then_inc(e_in, 1)
            dve.wait_ge(e_ok, 1)
            step(dve.tensor_reduce(top[:], gate_e[:], AX.X, ALU.add))
            step(dve.reciprocal(top[:], top[:]))
            step(dve.tensor_tensor(gate[:], gate_e[:], over(top[:]), ALU.mult))
            for s in range(EXPERTS):
                for lo_e, hi_e, op in ((0, s + 1, ALU.is_gt), (s + 1, EXPERTS, ALU.is_ge)):
                    if lo_e < hi_e:
                        last = dve.tensor_tensor(beats[:, s, :, lo_e:hi_e],
                                                 gate[:, :, s:s + 1].broadcast_to([P, TILES, hi_e - lo_e]),
                                                 gate[:, :, lo_e:hi_e], op)
            step(last)
            step(dve.tensor_reduce(rank[:].rearrange("p t e -> p (t e)"), beats[:].rearrange("p s t e -> p (t e) s"), AX.X, ALU.add))
            step(dve.scalar_tensor_tensor(comb[:].rearrange("p e t -> p t e"), rank[:], TOP_K - 0.5, gate[:], ALU.is_lt, ALU.mult))


class ExpertWeights:

    def __init__(self, nc, ctx, w1_u, b1_t, w2_u, b2):
        def sb(name, shape, dt=F32):
            return ctx.enter_context(nc.sbuf_tensor(name, shape, dt))

        def sem(name):
            return ctx.enter_context(nc.semaphore(name))

        self.w1_u, self.b1_t, self.w2_u, self.b2 = w1_u, b1_t, w2_u, b2
        self.w1_raw = [sb(f"w1_raw{i}", [P, KC, FQ]) for i in range(2)]
        self.w2_raw = [sb(f"w2_raw{i}", [P, FC, C]) for i in range(2)]
        self.w1_hi = [sb(f"w1_hi{i}", [P, KC, FQ], F32R) for i in range(2)]
        self.w1_lo = [sb(f"w1_lo{i}", [P, KC, FQ], F32R) for i in range(2)]
        self.w2_hi = [sb(f"w2_hi{i}", [P, FC, C], F32R) for i in range(2)]
        self.w2_lo = [sb(f"w2_lo{i}", [P, FC, C], F32R) for i in range(2)]
        self.b1_sb = sb("b1_sb", [P, EXPERTS * FF // P])
        self.b2_sb = sb("b2_sb", [P, EXPERTS * C])
        self.b_in = sem("b_in3")
        self.raw_in = [sem(f"raw_in{i}") for i in range(2)]
        self.split_go = sem("split_go")
        self.hi_ok = sem("w_hi_ok3")
        self.w_ok = sem("w_ok")

    def load_biases(self, sp):
        sp.dma_start(self.b1_sb[:], self.b1_t).then_inc(self.b_in, 16)
        sp.dma_start(self.b2_sb[:], self.b2.rearrange("(a e) n -> a (e n)", a=1).broadcast_to([P, EXPERTS * C])).then_inc(self.b_in, 16)

    def load_unit(self, sp, u, par):
        for raw, src in ((self.w1_raw, self.w1_u), (self.w2_raw, self.w2_u)):
            sp.dma_start(raw[par][:].rearrange("p k n -> p (k n)"),
                         src[bass.ds(u, 1), :, :].rearrange("a p n -> (a p) n")).then_inc(self.raw_in[par], 16)

    def split_unit(self, pool, u, par):
        pool.tensor_copy(self.w1_hi[par][:], self.w1_raw[par][:]).then_inc(self.hi_ok, 1)
        pool.tensor_copy(self.w2_hi[par][:], self.w2_raw[par][:]).then_inc(self.hi_ok, 1)
        pool.wait_ge(self.hi_ok, 2 * u + 2)
        pool.tensor_tensor(self.w1_lo[par][:], self.w1_raw[par][:], self.w1_hi[par][:].bitcast(F32), ALU.subtract)
        pool.tensor_tensor(self.w2_lo[par][:], self.w2_raw[par][:], self.w2_hi[par][:].bitcast(F32), ALU.subtract).then_inc(self.w_ok, 1)


def phase_experts(nc, experts, out, x1, xt_hi, xt_lo, comb):
    with ExitStack() as ctx:
        def sb(name, shape, dt=F32):
            return ctx.enter_context(nc.sbuf_tensor(name, shape, dt))

        def sem(name):
            return ctx.enter_context(nc.semaphore(name))

        w1_hi, w1_lo, w2_hi, w2_lo = experts.w1_hi, experts.w1_lo, experts.w2_hi, experts.w2_lo
        b1_sb, b2_sb, raw_in, w_ok = experts.b1_sb, experts.b2_sb, experts.raw_in, experts.w_ok
        h_f = sb("h_f", [P, FC, TB])
        h_hi = [sb(f"h_hi{i}", [P, FC, TB], F32R) for i in range(2)]
        h_lo = [sb(f"h_lo{i}", [P, FC, TB], F32R) for i in range(2)]
        ps_h = ctx.enter_context(nc.psum_tensor("ps_h", [P, FC, 512], F32))
        ps_o = ctx.enter_context(nc.psum_tensor("ps_o3", [P, TPB, 512], F32))

        h_ok = sem("h_ok")
        g_f = sem("g_f_ok")
        g_lo = sem("g_lo_ok")
        y_ok = sem("y_ok3")
        y_free = sem("y_free")
        b2_ok = sem("b2_ok")
        done = sem("done")
        block = ctx.enter_context(nc.Block())

        UNITS_E = EXPERTS * QUARTERS
        CB2 = C // QUARTERS
        OUT_CREDIT = TILES + 1

        @block.sync
        def _(sp):
            with sp.Fori(1, UNITS_E // 2) as i:
                for par in range(2):
                    u = 2 * i + par
                    sp.wait_ge(w_ok, u - 1)
                    experts.load_unit(sp, u, par)
            for blk in range(BLOCKS):
                tiles = slice(blk * TPB, (blk + 1) * TPB)
                behind = TILES - (blk + 1) * TPB
                sp.wait_ge(y_free, TPB + UNITS_E * TILES - behind)
                sp.wait_ge(b2_ok, UNITS_E * TILES - behind)
                sp.dma_start(out.rearrange("(t p) c -> p t c", p=P)[:, tiles, :], x1[:, tiles, :]).then_inc(done, 16)
            sp.wait_ge(done, 16 * BLOCKS)

        @block.gpsimd
        def _(pool):
            with pool.Fori(1, UNITS_E // 2) as i:
                for par in range(2):
                    u = 2 * i + par
                    pool.wait_ge(raw_in[par], 32 * i + 32)
                    pool.wait_ge(y_ok, TILES * u - TILES + OUT_CREDIT)
                    pool.sem_inc(experts.split_go, 1)
                    experts.split_unit(pool, u, par)

        @block.tensor
        def _(pe):
            with pe.Fori(0, UNITS_E // 2) as i:
                for w in range(2):
                    with pe.Fori(0, BLOCKS // 2) as j:
                        pe.wait_ge(w_ok, 2 * i + w + 1)
                        for par in range(2):
                            blk = 2 * j + par
                            n = (2 * i + w) * BLOCKS + blk
                            cols = bass.ds(blk * TB, TB)
                            for f in range(FC):
                                pe.wait_ge(g_f, FC * n + f + 1)
                                cut = slice(f * P, (f + 1) * P)
                                for m, (wt, v) in enumerate([(w1_hi, xt_hi), (w1_lo, xt_hi), (w1_hi, xt_lo)]):
                                    for k in range(KC):
                                        last = pe.matmul(ps_h[:, f, 0:TB], wt[w][:, k, cut], v[:, k, cols],
                                                         start=(m + k == 0), stop=(m == 2 and k == KC - 1))
                                last.then_inc(h_ok, 1)
                            for f in range(FC):
                                pe.wait_ge(g_lo, FC * n + f + 1 + FC)
                                for t in range(TPB):
                                    if f == 0:
                                        pe.wait_ge(y_free, TPB * n + t + 1)
                                    cut = slice(t * P, (t + 1) * P)
                                    for m, (v, wt) in enumerate([(h_hi, w2_hi), (h_hi, w2_lo), (h_lo, w2_hi)]):
                                        last = pe.matmul(ps_o[:, t, 0:C], v[par][:, f, cut], wt[w][:, f, :],
                                                         start=(m + f == 0), stop=(m == 2 and f == FC - 1))
                                    if f == FC - 1:
                                        last.then_inc(y_ok, 1)

        @block.scalar
        def _(act):
            act.activation(h_f[:, 0, 0:1], b1_sb[:, 0:1], ACT.Gelu).then_inc(g_f, FC)
            with act.Fori(0, UNITS_E) as u:
                with act.Fori(0, BLOCKS // 2) as j:
                    for par in range(2):
                        n = u * BLOCKS + 2 * j + par
                        act.wait_ge(y_ok, TPB * n - TPB + OUT_CREDIT)
                        for f in range(FC):
                            bias = b1_sb[:, bass.ds(FC * u + f, 1)]
                            act.wait_ge(h_ok, FC * n + f + 1)
                            act.activation(h_hi[par][:, f, :], ps_h[:, f, 0:TB], ACT.Gelu, bias=bias)
                            act.wait_ge(g_lo, FC * n + f + 1)
                            act.activation(h_f[:, f, :], ps_h[:, f, 0:TB], ACT.Gelu, bias=bias).then_inc(g_f, 1)

        @block.vector
        def _(dve):
            dve.sem_inc(g_lo, FC)
            dve.sem_inc(y_ok, OUT_CREDIT)
            dve.sem_inc(y_free, TPB)
            with dve.Fori(0, EXPERTS) as e:
                with dve.Fori(0, QUARTERS) as q:
                    with dve.Fori(0, BLOCKS // 2) as j:
                        for par in range(2):
                            blk = 2 * j + par
                            n = e * (QUARTERS * BLOCKS) + q * BLOCKS + blk
                            for f in range(FC):
                                dve.wait_ge(g_f, FC * n + f + 1 + FC)
                                dve.tensor_tensor(h_lo[par][:, f, :], h_f[:, f, :], h_hi[par][:, f, :].bitcast(F32),
                                                  ALU.subtract).then_inc(g_lo, 1)
                            for t in range(TPB):
                                part = x1[:, bass.ds(TPB * blk + t, 1), bass.ds(q * CB2, CB2)].rearrange("p a c -> p (a c)")
                                weight = comb[:].rearrange("p e t -> p (e t)")[:, bass.ds(e * TILES + TPB * blk + t, 1)]
                                dve.scalar_tensor_tensor(part, b2_sb[:, bass.ds(e * C + q * CB2, CB2)], weight, part,
                                                         ALU.mult, ALU.add).then_inc(b2_ok, 1)
                            dve.wait_ge(b2_ok, TPB * n + TPB)
                            for t in range(TPB):
                                row = x1[:, bass.ds(TPB * blk + t, 1), :].rearrange("p a c -> p (a c)")
                                weight = comb[:].rearrange("p e t -> p (e t)")[:, bass.ds(e * TILES + TPB * blk + t, 1)]
                                dve.wait_ge(y_ok, TPB * n + t + 1 + OUT_CREDIT)
                                dve.scalar_tensor_tensor(row, ps_o[:, t, 0:C], weight, row, ALU.mult, ALU.add).then_inc(y_free, 1)


def program(nc, x, qkv_w, qkv_b, qkv_b_t, proj_w, proj_b, rel_t, gate_w, gate_b, w1_u, b1_t, w2_u, b2, out):
    def dram(name, shape):
        return nc.dram_tensor(name, shape, F32).ap()

    nc.disable_value_cache = True
    qk_hi_d = dram("qk_hi_d", [2 * C, S])
    qk_lo_d = dram("qk_lo_d", [2 * C, S])
    v_d = dram("v_d", [HEADS, P, TILES * VW])
    rel_hi_d = dram("rel_hi_d", [HEADS, 2 * SIDE, S])
    rel_lo_d = dram("rel_lo_d", [HEADS, 2 * SIDE, S])
    m_d = dram("m_d", [HEADS, S])
    o_d = dram("o_d", [C, S])
    sums_d = dram("sums_d", [HEADS, S])
    rec_d = dram("rec_d", [HEADS, S])
    phase_qkv(nc, x, qkv_w, qkv_b, qkv_b_t, qk_hi_d, qk_lo_d, v_d)
    with ExitStack() as ctx:
        room = ctx.enter_context(nc.sbuf_tensor("room", [P, HPT, S], F32))
        with ExitStack() as keys:
            key_hi = keys.enter_context(nc.sbuf_tensor("key_hi0", [P, S], F32R))
            key_rest = keys.enter_context(nc.sbuf_tensor("key_rest0", [TOP, S], F32R))
            phase_rel(nc, rel_t, qk_hi_d, qk_lo_d, rel_hi_d, rel_lo_d, room, key_hi, key_rest)
            phase_attention(nc, qk_hi_d, qk_lo_d, rel_hi_d, rel_lo_d, v_d, m_d, o_d, sums_d, key_hi, key_rest, room)
        x1 = ctx.enter_context(nc.sbuf_tensor("x1", [P, TILES, C], F32))
        stats = ctx.enter_context(nc.sbuf_tensor("x1_stats", [P, TILES, 6], F32))
        experts = ExpertWeights(nc, ctx, w1_u, b1_t, w2_u, b2)
        phase_proj(nc, x, o_d, sums_d, rec_d, proj_w, proj_b, room[:, 0:KC, :], x1, stats, experts)
        xt_hi = room[:, 0:KC, :].bitcast(F32R)
        xt_lo = ctx.enter_context(nc.sbuf_tensor("xt_lo", [P, KC, S], F32R))
        comb = ctx.enter_context(nc.sbuf_tensor("comb", [P, EXPERTS, TILES], F32))
        phase_gates(nc, gate_w, gate_b, x1, stats, xt_hi, xt_lo, comb)
        phase_experts(nc, experts, out, x1, xt_hi, xt_lo, comb)


def kernel(**inputs):
    import numpy as np
    import concourse.bacc as bacc
    from concourse.bass_utils import run_bass_kernel_spmd

    a = {k: np.asarray(v) for k, v in inputs.items()}
    laid = {
        "x": a["x"].reshape(S, C),
        "qkv_w": a["L0_conv_qkv_w"],
        "qkv_b": a["L0_conv_qkv_b"],
        "qkv_b_t": a["L0_conv_qkv_b"].reshape(-1, P).T,
        "proj_w": a["L0_conv_proj_w"],
        "proj_b": a["L0_conv_proj_b"],
        "rel_t": np.stack([a["L0_conv_rel_pos_w"][::-1].T, a["L0_conv_rel_pos_h"][::-1].T]),
        "gate_w": a["L0_ffn_Wg"],
        "gate_b": a["L0_ffn_bg"],
        "w1_u": a["L0_ffn_W1"].reshape(EXPERTS, KC, P, QUARTERS, FQ).transpose(0, 3, 2, 1, 4).reshape(-1, P, KC * FQ),
        "b1_t": a["L0_ffn_b1"].reshape(-1, P).T,
        "w2_u": a["L0_ffn_W2"].reshape(EXPERTS * QUARTERS, FC, P, C).transpose(0, 2, 1, 3).reshape(-1, P, FC * C),
        "b2": a["L0_ffn_b2"],
    }
    laid = {k: np.ascontiguousarray(v) for k, v in laid.items()}
    nc = bacc.Bacc("TRN2", target_bir_lowering=False, num_devices=1)
    aps = {k: nc.dram_tensor(k, v.shape, mybir.dt.from_np(v.dtype), kind="ExternalInput").ap() for k, v in laid.items()}
    out = nc.dram_tensor("out", (S, C), F32, kind="ExternalOutput").ap()
    program(nc, **aps, out=out)
    r = run_bass_kernel_spmd(nc, [laid], core_ids=[0])
    return r.results[0]["out"].reshape(a["x"].shape)
```
